# Optimizing a Trainium2 kernel written in Bass

```python
import numpy as np
import jax
import jax.numpy as jnp

def _softmax(x, axis=-1):
    return jax.nn.softmax(x, axis=axis)

def _gelu(x):
    return jax.nn.gelu(x, approximate=True)

def _silu(x):
    return jax.nn.silu(x)

def _sigmoid(x):
    return jax.nn.sigmoid(x)

def _layernorm(x, axis=-1, eps=1e-05):
    m = jnp.mean(x, axis=axis, keepdims=True)
    v = jnp.var(x, axis=axis, keepdims=True)
    return (x - m) / jnp.sqrt(v + eps)

def _scatter_add(tgt, idx, src, axis=0):
    return tgt.at[idx].add(src)

def _segment_sum(src, seg, n):
    return jax.ops.segment_sum(src, seg, n)
kernel_name = 'mk_perceiver_d2_seqx_r8_84b3c4'

def setup_inputs(seed: int=0):
    np.random.seed(seed)
    _w = jnp.asarray

    def _rec_inputs():
        import jax
        import jax.numpy as jnp
        _rk = jax.random.key(seed)
        x = 7.22e-05 + 1 * jax.random.normal(jax.random.fold_in(_rk, 1), (1, 64, 128), jnp.float32)
        _lenS = 64 - jax.random.randint(jax.random.fold_in(_rk, 7), (1,), 0, max(1, 64 // 4) + 1, jnp.int32)
        _lenS2 = 6272 - jax.random.randint(jax.random.fold_in(_rk, 8), (1,), 0, max(1, 6272 // 4) + 1, jnp.int32)
        _ctx_768P = jax.random.normal(jax.random.fold_in(_rk, 11), (1, 16, 96), jnp.float32)
        _ctx_768c = jax.random.dirichlet(jax.random.fold_in(_rk, 511), 0.3 * jnp.ones((16,), jnp.float32), (1, 6272))
        _ctx_768t = jnp.einsum('bsk,bkd->bsd', _ctx_768c, _ctx_768P)
        _ctx_768t = _ctx_768t * jax.lax.rsqrt(jnp.mean(jnp.square(_ctx_768t)) + 1e-12) * 0.953939
        ctx_768 = 3.88148e-05 + 0.999967 * (_ctx_768t + 0.3 * jax.random.normal(jax.random.fold_in(_rk, 611), (1, 6272, 96), jnp.float32))
        _validS = jnp.arange(64)[None, :] < _lenS[:, None]
        _validS2 = jnp.arange(6272)[None, :] < _lenS2[:, None]
        _causal = jnp.tril(jnp.ones((64, 64), dtype=bool))
        mask_BxS_bf1 = jnp.ones((1, 64), dtype=bool)
        mask_BxS2_bf1 = jnp.ones((1, 6272), dtype=bool)
        return (x, ctx_768, mask_BxS_bf1, mask_BxS2_bf1)
    x, ctx_768, mask_BxS_bf1, mask_BxS2_bf1 = _rec_inputs()

    def _L0_xattn_setup():
        import jax, jax.numpy as jnp
        import numpy as np
        B, T, DT, G, DV = (16, 64, 128, 72, 96)
        H, DH = (4, 32)
        INNER = H * DH
        HID = 4 * DT
        N_STATE = 64
        K_TOP = 32

        def layernorm(x, g, b, eps=1e-05):
            m = x.mean(-1, keepdims=True)
            v = x.var(-1, keepdims=True)
            return (x - m) * jax.lax.rsqrt(v + eps) * g + b

        def s4d(x, log_dt, A_re, A_im, C_re, C_im, D_skip):
            Bb, L, D = x.shape
            dt = jnp.exp(log_dt)
            A = A_re + 1j * A_im
            C = C_re + 1j * C_im
            dtA = dt[:, None] * A
            dC = C * (jnp.exp(dtA) - 1.0) / A
            powers = jnp.exp(dtA[:, :, None] * jnp.arange(L))
            K = 2.0 * jnp.einsum('dn,dnl->dl', dC, powers).real
            n = 2 * L
            Kf = jnp.fft.rfft(K, n=n, axis=-1)
            xf = jnp.fft.rfft(x, n=n, axis=1)
            y = jnp.fft.irfft(xf * Kf.T[None], n=n, axis=1)[:, :L]
            return y + x * D_skip
        key = jax.random.key(seed)
        ks = jax.random.split(key, 16)
        s = 0.02
        inp = {'x_text': jax.random.normal(ks[0], (B, T, DT), jnp.float32), 'x_vision': jax.random.normal(ks[1], (B, G, DV), jnp.float32), 'text_mask': jnp.ones((B, T), bool), 'vision_mask': jnp.ones((B, G), bool), 'Wq': jax.random.normal(ks[2], (DT, INNER), jnp.float32) * s, 'Wk': jax.random.normal(ks[3], (DV, INNER), jnp.float32) * s, 'Wv': jax.random.normal(ks[4], (DV, DT), jnp.float32) * s, 'W_film_in': jax.random.normal(ks[5], (DT, 2 * DT), jnp.float32) * s, 'b_film_in': jnp.zeros((2 * DT,), jnp.float32), 'W_film_out': jax.random.normal(ks[6], (DT, 2 * DT), jnp.float32) * s, 'b_film_out': jnp.zeros((2 * DT,), jnp.float32), 'g_norm_in': jnp.ones((DT,), jnp.float32), 'b_norm_in': jnp.zeros((DT,), jnp.float32), 'g_norm_out': jnp.ones((DT,), jnp.float32), 'b_norm_out': jnp.zeros((DT,), jnp.float32), 'g_ffn': jnp.ones((DT,), jnp.float32), 'b_ffn': jnp.zeros((DT,), jnp.float32), 'W1': jax.random.normal(ks[7], (DT, HID), jnp.float32) * s, 'b1': jnp.zeros((HID,), jnp.float32), 'W2': jax.random.normal(ks[8], (HID, DT), jnp.float32) * s, 'b2': jnp.zeros((DT,), jnp.float32), 'log_dt': jnp.log(0.001) + jax.random.uniform(ks[9], (DT,), jnp.float32) * (jnp.log(0.1) - jnp.log(0.001)), 'A_re': -0.5 * jnp.ones((DT, N_STATE), jnp.float32), 'A_im': jnp.tile(jnp.pi * jnp.arange(N_STATE, dtype=jnp.float32), (DT, 1)), 'C_re': jax.random.normal(ks[10], (DT, N_STATE), jnp.float32) * 0.5 ** 0.5, 'C_im': jax.random.normal(ks[11], (DT, N_STATE), jnp.float32) * 0.5 ** 0.5, 'D_skip': jax.random.normal(ks[12], (DT,), jnp.float32), 'mod_gate': jnp.array(0.5, jnp.float32)}
        return inp
    _L0_xattn_all = _L0_xattn_setup()
    _L0_xattn_in = {k: v for k, v in _L0_xattn_all.items() if k in ('Wq', 'Wk', 'Wv', 'W_film_in', 'b_film_in', 'W_film_out', 'b_film_out', 'g_norm_in', 'b_norm_in', 'g_norm_out', 'b_norm_out', 'g_ffn', 'b_ffn', 'W1', 'b1', 'W2', 'b2', 'log_dt', 'A_re', 'A_im', 'C_re', 'C_im', 'D_skip', 'mod_gate')}
    del _L0_xattn_all

    def _L0_attn_setup():
        import jax, jax.numpy as jnp
        import numpy as np
        B, L, D, R, GH = (4, 512, 128, 32, 32)

        def _xavier(key, shape, gain=1.0):
            fan_in, fan_out = (shape[0], shape[1])
            lim = gain * np.sqrt(6.0 / (fan_in + fan_out))
            return jax.random.uniform(key, shape, jnp.float32, -lim, lim)
        key = jax.random.key(seed)
        ks = jax.random.split(key, 9)
        x = jax.random.normal(ks[0], (B, L, D), jnp.float32)
        gate_w1 = _xavier(ks[1], (D, GH), 1.0)
        gate_b1 = jnp.zeros((GH,), jnp.float32)
        gate_w2 = _xavier(ks[2], (GH, R), 1.0)
        gate_b2 = jnp.zeros((R,), jnp.float32)
        U_w = _xavier(ks[3], (D, R), 0.02)
        V_w = _xavier(ks[4], (D, R), 0.02)
        conv_w = jax.random.normal(ks[5], (D, 3), jnp.float32) * 0.02
        out_w = _xavier(ks[6], (R, D), 1.0)
        out_b = jnp.zeros((D,), jnp.float32)
        return {'x': x, 'gate_w1': gate_w1, 'gate_b1': gate_b1, 'gate_w2': gate_w2, 'gate_b2': gate_b2, 'U_w': U_w, 'V_w': V_w, 'conv_w': conv_w, 'out_w': out_w, 'out_b': out_b}
    _L0_attn_all = _L0_attn_setup()
    _L0_attn_in = {k: v for k, v in _L0_attn_all.items() if k in ('gate_w1', 'gate_b1', 'gate_w2', 'gate_b2', 'U_w', 'V_w', 'conv_w', 'out_w', 'out_b')}
    del _L0_attn_all

    def _L0_ffn_setup():
        import jax, jax.numpy as jnp
        import numpy as np
        H = 128
        E = 8
        TOP_K = 2
        FF = 4 * H
        B, S = (2, 256)

        def _moe_forward(x, gate_w, gate_b, w1, b1, w2, b2, sw1, sb1, sw2, sb2):
            b, s, h = x.shape
            xf = x.reshape(-1, h)
            scores = jax.nn.sigmoid(xf @ gate_w.T + gate_b)
            top_scores, top_idx = jax.lax.top_k(scores, TOP_K)
            top_scores = top_scores / (top_scores.sum(-1, keepdims=True) + 1e-06)
            comb = (jax.nn.one_hot(top_idx, E, dtype=xf.dtype) * top_scores[..., None]).sum(1)
            hdn = jax.nn.gelu(jnp.einsum('th,ehf->etf', xf, w1) + b1[:, None, :], approximate=False)
            y = jnp.einsum('etf,efh->eth', hdn, w2) + b2[:, None, :]
            routed = jnp.einsum('te,eth->th', comb, y)
            shared = (jax.nn.gelu(xf @ sw1 + sb1, approximate=False) @ sw2 + sb2) * 0.1
            return (routed + shared).reshape(b, s, h)
        key = jax.random.key(seed)
        ks = jax.random.split(key, 12)
        std = 0.02 / np.sqrt(H)
        return {'x': jax.random.normal(ks[0], (B, S, H), dtype=jnp.float32), 'gate_w': jax.random.normal(ks[1], (E, H), dtype=jnp.float32) * std, 'gate_b': jnp.zeros((E,), dtype=jnp.float32), 'w1': jax.random.normal(ks[2], (E, H, FF), dtype=jnp.float32) * (1.0 / np.sqrt(H)), 'b1': jnp.zeros((E, FF), dtype=jnp.float32), 'w2': jax.random.normal(ks[3], (E, FF, H), dtype=jnp.float32) * (1.0 / np.sqrt(FF)), 'b2': jnp.zeros((E, H), dtype=jnp.float32), 'sw1': jax.random.normal(ks[4], (H, FF), dtype=jnp.float32) * (1.0 / np.sqrt(H)), 'sb1': jnp.zeros((FF,), dtype=jnp.float32), 'sw2': jax.random.normal(ks[5], (FF, H), dtype=jnp.float32) * (1.0 / np.sqrt(FF)), 'sb2': jnp.zeros((H,), dtype=jnp.float32)}
    _L0_ffn_all = _L0_ffn_setup()
    _L0_ffn_in = {k: v for k, v in _L0_ffn_all.items() if k in ('gate_w', 'gate_b', 'w1', 'b1', 'w2', 'b2', 'sw1', 'sb1', 'sw2', 'sb2')}
    del _L0_ffn_all

    def _L1_xattn_setup():
        import jax, jax.numpy as jnp
        import numpy as np
        B, LQ, LKV = (4, 64, 256)
        DQ, DKV, H = (128, 96, 16)
        HD = DQ // H
        key = jax.random.key(seed)
        ks = jax.random.split(key, 12)
        s_q = 1.0 / np.sqrt(DQ)
        s_kv = 1.0 / np.sqrt(DKV)
        return {'q': jax.random.normal(ks[0], (B, LQ, DQ), jnp.float32), 'kv': jax.random.normal(ks[1], (B, LKV, DKV), jnp.float32), 'Wq': jax.random.normal(ks[2], (DQ, DQ), jnp.float32) * s_q, 'bq': jnp.zeros((DQ,), jnp.float32), 'Wk': jax.random.normal(ks[3], (DKV, DQ), jnp.float32) * s_kv, 'bk': jnp.zeros((DQ,), jnp.float32), 'Wv': jax.random.normal(ks[4], (DKV, DQ), jnp.float32) * s_kv, 'bv': jnp.zeros((DQ,), jnp.float32), 'Wo': jax.random.normal(ks[5], (DQ, DQ), jnp.float32) * s_q, 'bo': jnp.zeros((DQ,), jnp.float32), 'scale': jnp.ones((1,), jnp.float32) * DQ ** (-0.5)}
    _L1_xattn_all = _L1_xattn_setup()
    _L1_xattn_in = {k: v for k, v in _L1_xattn_all.items() if k in ('Wq', 'bq', 'Wk', 'bk', 'Wv', 'bv', 'Wo', 'bo', 'scale')}
    del _L1_xattn_all

    def _L1_attn_setup():
        import jax, jax.numpy as jnp
        import numpy as np
        key = jax.random.key(seed)
        ks = jax.random.split(key, 5)
        B, S, D = (2, 256, 128)
        scale = 0.02
        return {'x': jax.random.normal(ks[0], (B, S, D), dtype=jnp.float32), 'q_proj_weight': jax.random.normal(ks[1], (D, D), dtype=jnp.float32) * scale, 'k_proj_weight': jax.random.normal(ks[2], (D, D), dtype=jnp.float32) * scale, 'v_proj_weight': jax.random.normal(ks[3], (D, D), dtype=jnp.float32) * scale, 'o_proj_weight': jax.random.normal(ks[4], (D, D), dtype=jnp.float32) * scale}
    _L1_attn_all = _L1_attn_setup()
    _L1_attn_in = {k: v for k, v in _L1_attn_all.items() if k in ('q_proj_weight', 'k_proj_weight', 'v_proj_weight', 'o_proj_weight')}
    del _L1_attn_all

    def _L1_ffn_setup():
        import jax, jax.numpy as jnp
        import numpy as np
        TOP_K = 2
        CAPACITY = 512
        EPS = 1e-06
        W_SCALE = 0.02

        def _rms(x, w):
            return x * jax.lax.rsqrt(jnp.mean(x * x, axis=-1, keepdims=True) + EPS) * w
        key = jax.random.key(seed)
        ks = jax.random.split(key, 8)
        B, S, H, F, E = (8, 512, 128, 256, 8)
        F4 = F // 4
        return {'hidden_states': jax.random.normal(ks[0], (B, S, H), jnp.float32), 'Wr': jax.random.normal(ks[1], (H, E), jnp.float32) * W_SCALE, 'norm_w': jnp.ones((E, H), jnp.float32), 'Wg': jax.random.normal(ks[2], (E, H, F), jnp.float32) * W_SCALE, 'Wu': jax.random.normal(ks[3], (E, H, F), jnp.float32) * W_SCALE, 'Wd': jax.random.normal(ks[4], (E, F, H), jnp.float32) * W_SCALE, 'f_norm': jnp.ones((H,), jnp.float32), 'fWg': jax.random.normal(ks[5], (H, F4), jnp.float32) * W_SCALE, 'fWu': jax.random.normal(ks[6], (H, F4), jnp.float32) * W_SCALE, 'fWd': jax.random.normal(ks[7], (F4, H), jnp.float32) * W_SCALE}
    _L1_ffn_all = _L1_ffn_setup()
    _L1_ffn_in = {k: v for k, v in _L1_ffn_all.items() if k in ('Wr', 'norm_w', 'Wg', 'Wu', 'Wd', 'f_norm', 'fWg', 'fWu', 'fWd')}
    del _L1_ffn_all
    return {'x': x, 'ctx_768': ctx_768, 'mask_BxS_bf1': mask_BxS_bf1, 'mask_BxS2_bf1': mask_BxS2_bf1, 'L0_xattn_Wq': _L0_xattn_in['Wq'], 'L0_xattn_Wk': _L0_xattn_in['Wk'], 'L0_xattn_Wv': _L0_xattn_in['Wv'], 'L0_xattn_W_film_in': _L0_xattn_in['W_film_in'], 'L0_xattn_b_film_in': _L0_xattn_in['b_film_in'], 'L0_xattn_W_film_out': _L0_xattn_in['W_film_out'], 'L0_xattn_b_film_out': _L0_xattn_in['b_film_out'], 'L0_xattn_g_norm_in': _L0_xattn_in['g_norm_in'], 'L0_xattn_b_norm_in': _L0_xattn_in['b_norm_in'], 'L0_xattn_g_norm_out': _L0_xattn_in['g_norm_out'], 'L0_xattn_b_norm_out': _L0_xattn_in['b_norm_out'], 'L0_xattn_g_ffn': _L0_xattn_in['g_ffn'], 'L0_xattn_b_ffn': _L0_xattn_in['b_ffn'], 'L0_xattn_W1': _L0_xattn_in['W1'], 'L0_xattn_b1': _L0_xattn_in['b1'], 'L0_xattn_W2': _L0_xattn_in['W2'], 'L0_xattn_b2': _L0_xattn_in['b2'], 'L0_xattn_log_dt': _L0_xattn_in['log_dt'], 'L0_xattn_A_re': _L0_xattn_in['A_re'], 'L0_xattn_A_im': _L0_xattn_in['A_im'], 'L0_xattn_C_re': _L0_xattn_in['C_re'], 'L0_xattn_C_im': _L0_xattn_in['C_im'], 'L0_xattn_D_skip': _L0_xattn_in['D_skip'], 'L0_xattn_mod_gate': _L0_xattn_in['mod_gate'], 'L0_attn_gate_w1': _L0_attn_in['gate_w1'], 'L0_attn_gate_b1': _L0_attn_in['gate_b1'], 'L0_attn_gate_w2': _L0_attn_in['gate_w2'], 'L0_attn_gate_b2': _L0_attn_in['gate_b2'], 'L0_attn_U_w': _L0_attn_in['U_w'], 'L0_attn_V_w': _L0_attn_in['V_w'], 'L0_attn_conv_w': _L0_attn_in['conv_w'], 'L0_attn_out_w': _L0_attn_in['out_w'], 'L0_attn_out_b': _L0_attn_in['out_b'], 'L0_ffn_gate_w': _L0_ffn_in['gate_w'], 'L0_ffn_gate_b': _L0_ffn_in['gate_b'], 'L0_ffn_w1': _L0_ffn_in['w1'], 'L0_ffn_b1': _L0_ffn_in['b1'], 'L0_ffn_w2': _L0_ffn_in['w2'], 'L0_ffn_b2': _L0_ffn_in['b2'], 'L0_ffn_sw1': _L0_ffn_in['sw1'], 'L0_ffn_sb1': _L0_ffn_in['sb1'], 'L0_ffn_sw2': _L0_ffn_in['sw2'], 'L0_ffn_sb2': _L0_ffn_in['sb2'], 'L1_xattn_Wq': _L1_xattn_in['Wq'], 'L1_xattn_bq': _L1_xattn_in['bq'], 'L1_xattn_Wk': _L1_xattn_in['Wk'], 'L1_xattn_bk': _L1_xattn_in['bk'], 'L1_xattn_Wv': _L1_xattn_in['Wv'], 'L1_xattn_bv': _L1_xattn_in['bv'], 'L1_xattn_Wo': _L1_xattn_in['Wo'], 'L1_xattn_bo': _L1_xattn_in['bo'], 'L1_xattn_scale': _L1_xattn_in['scale'], 'L1_attn_q_proj_weight': _L1_attn_in['q_proj_weight'], 'L1_attn_k_proj_weight': _L1_attn_in['k_proj_weight'], 'L1_attn_v_proj_weight': _L1_attn_in['v_proj_weight'], 'L1_attn_o_proj_weight': _L1_attn_in['o_proj_weight'], 'L1_ffn_Wr': _L1_ffn_in['Wr'], 'L1_ffn_norm_w': _L1_ffn_in['norm_w'], 'L1_ffn_Wg': _L1_ffn_in['Wg'], 'L1_ffn_Wu': _L1_ffn_in['Wu'], 'L1_ffn_Wd': _L1_ffn_in['Wd'], 'L1_ffn_f_norm': _L1_ffn_in['f_norm'], 'L1_ffn_fWg': _L1_ffn_in['fWg'], 'L1_ffn_fWu': _L1_ffn_in['fWu'], 'L1_ffn_fWd': _L1_ffn_in['fWd']}

def reference(x, ctx_768, mask_BxS_bf1, mask_BxS2_bf1, L0_xattn_Wq, L0_xattn_Wk, L0_xattn_Wv, L0_xattn_W_film_in, L0_xattn_b_film_in, L0_xattn_W_film_out, L0_xattn_b_film_out, L0_xattn_g_norm_in, L0_xattn_b_norm_in, L0_xattn_g_norm_out, L0_xattn_b_norm_out, L0_xattn_g_ffn, L0_xattn_b_ffn, L0_xattn_W1, L0_xattn_b1, L0_xattn_W2, L0_xattn_b2, L0_xattn_log_dt, L0_xattn_A_re, L0_xattn_A_im, L0_xattn_C_re, L0_xattn_C_im, L0_xattn_D_skip, L0_xattn_mod_gate, L0_attn_gate_w1, L0_attn_gate_b1, L0_attn_gate_w2, L0_attn_gate_b2, L0_attn_U_w, L0_attn_V_w, L0_attn_conv_w, L0_attn_out_w, L0_attn_out_b, L0_ffn_gate_w, L0_ffn_gate_b, L0_ffn_w1, L0_ffn_b1, L0_ffn_w2, L0_ffn_b2, L0_ffn_sw1, L0_ffn_sb1, L0_ffn_sw2, L0_ffn_sb2, L1_xattn_Wq, L1_xattn_bq, L1_xattn_Wk, L1_xattn_bk, L1_xattn_Wv, L1_xattn_bv, L1_xattn_Wo, L1_xattn_bo, L1_xattn_scale, L1_attn_q_proj_weight, L1_attn_k_proj_weight, L1_attn_v_proj_weight, L1_attn_o_proj_weight, L1_ffn_Wr, L1_ffn_norm_w, L1_ffn_Wg, L1_ffn_Wu, L1_ffn_Wd, L1_ffn_f_norm, L1_ffn_fWg, L1_ffn_fWu, L1_ffn_fWd):
    import jax
    import jax.numpy as jnp

    def _L0_xattn_ref(x_text, x_vision, text_mask, vision_mask, Wq, Wk, Wv, W_film_in, b_film_in, W_film_out, b_film_out, g_norm_in, b_norm_in, g_norm_out, b_norm_out, g_ffn, b_ffn, W1, b1, W2, b2, log_dt, A_re, A_im, C_re, C_im, D_skip, mod_gate):
        import jax, jax.numpy as jnp
        import numpy as np
        B, T, DT, G, DV = (16, 64, 128, 72, 96)
        H, DH = (4, 32)
        INNER = H * DH
        HID = 4 * DT
        N_STATE = 64
        K_TOP = 32

        def layernorm(x, g, b, eps=1e-05):
            m = x.mean(-1, keepdims=True)
            v = x.var(-1, keepdims=True)
            return (x - m) * jax.lax.rsqrt(v + eps) * g + b

        def s4d(x, log_dt, A_re, A_im, C_re, C_im, D_skip):
            Bb, L, D = x.shape
            dt = jnp.exp(log_dt)
            A = A_re + 1j * A_im
            C = C_re + 1j * C_im
            dtA = dt[:, None] * A
            dC = C * (jnp.exp(dtA) - 1.0) / A
            powers = jnp.exp(dtA[:, :, None] * jnp.arange(L))
            K = 2.0 * jnp.einsum('dn,dnl->dl', dC, powers).real
            n = 2 * L
            Kf = jnp.fft.rfft(K, n=n, axis=-1)
            xf = jnp.fft.rfft(x, n=n, axis=1)
            y = jnp.fft.irfft(xf * Kf.T[None], n=n, axis=1)[:, :L]
            return y + x * D_skip
        Bb, Tt, D = x_text.shape
        Gg = x_vision.shape[1]
        Q = (x_text @ Wq).reshape(Bb, Tt, H, DH)
        K = (x_vision @ Wk).reshape(Bb, Gg, H, DH)
        scores = jnp.einsum('bthd,bghd->bhtg', Q, K) / np.sqrt(DH).astype(np.float32)
        scores = jnp.where(vision_mask[:, None, None, :], scores, -jnp.inf)
        topv, topi = jax.lax.top_k(scores, K_TOP)
        probs = jax.nn.softmax(topv, axis=-1)
        bi = jnp.arange(Bb)[:, None, None, None]
        hi = jnp.arange(H)[None, :, None, None]
        ti = jnp.arange(Tt)[None, None, :, None]
        attn = jnp.zeros_like(scores).at[bi, hi, ti, topi].set(probs)
        attn_mean = attn.mean(axis=1)
        V = x_vision @ Wv
        c_t = jnp.einsum('btg,bgd->btd', attn_mean, V)
        c_t = c_t * text_mask[..., None]
        x = layernorm(x_text, g_norm_in, b_norm_in)
        scale_in, shift_in = jnp.split(c_t @ W_film_in + b_film_in, 2, axis=-1)
        x = x * (1.0 + mod_gate * scale_in) + mod_gate * shift_in
        y = s4d(x, log_dt, A_re, A_im, C_re, C_im, D_skip)
        scale_out, shift_out = jnp.split(c_t @ W_film_out + b_film_out, 2, axis=-1)
        y = y * (1.0 + mod_gate * scale_out) + mod_gate * shift_out
        xt = x_text + y
        h = layernorm(xt, g_ffn, b_ffn)
        h = jax.nn.gelu(h @ W1 + b1, approximate=False) @ W2 + b2
        xt = xt + h
        return layernorm(xt, g_norm_out, b_norm_out)

    def _L0_attn_ref(x, gate_w1, gate_b1, gate_w2, gate_b2, U_w, V_w, conv_w, out_w, out_b):
        import jax, jax.numpy as jnp
        import numpy as np
        B, L, D, R, GH = (4, 512, 128, 32, 32)

        def _xavier(key, shape, gain=1.0):
            fan_in, fan_out = (shape[0], shape[1])
            lim = gain * np.sqrt(6.0 / (fan_in + fan_out))
            return jax.random.uniform(key, shape, jnp.float32, -lim, lim)
        h = jax.nn.relu(jnp.einsum('bld,dg->blg', x, gate_w1) + gate_b1)
        gate = jax.nn.sigmoid(jnp.einsum('blg,gr->blr', h, gate_w2) + gate_b2)
        U = jnp.einsum('bld,dr->blr', x, U_w)
        V = jnp.einsum('bld,dr->blr', x, V_w)
        S = jnp.cumsum(V, axis=1)
        glob = gate * U * S
        y_global = jnp.einsum('blr,rd->bld', glob, out_w) + out_b
        xpad = jnp.pad(x, ((0, 0), (1, 1), (0, 0)))
        t_out = xpad[:, :-2] * conv_w[:, 0] + xpad[:, 1:-1] * conv_w[:, 1] + xpad[:, 2:] * conv_w[:, 2]
        return t_out + y_global

    def _L0_ffn_ref(x, gate_w, gate_b, w1, b1, w2, b2, sw1, sb1, sw2, sb2):
        import jax, jax.numpy as jnp
        import numpy as np
        H = 128
        E = 8
        TOP_K = 2
        FF = 4 * H
        B, S = (2, 256)

        def _moe_forward(x, gate_w, gate_b, w1, b1, w2, b2, sw1, sb1, sw2, sb2):
            b, s, h = x.shape
            xf = x.reshape(-1, h)
            scores = jax.nn.sigmoid(xf @ gate_w.T + gate_b)
            top_scores, top_idx = jax.lax.top_k(scores, TOP_K)
            top_scores = top_scores / (top_scores.sum(-1, keepdims=True) + 1e-06)
            comb = (jax.nn.one_hot(top_idx, E, dtype=xf.dtype) * top_scores[..., None]).sum(1)
            hdn = jax.nn.gelu(jnp.einsum('th,ehf->etf', xf, w1) + b1[:, None, :], approximate=False)
            y = jnp.einsum('etf,efh->eth', hdn, w2) + b2[:, None, :]
            routed = jnp.einsum('te,eth->th', comb, y)
            shared = (jax.nn.gelu(xf @ sw1 + sb1, approximate=False) @ sw2 + sb2) * 0.1
            return (routed + shared).reshape(b, s, h)
        return _moe_forward(x, gate_w, gate_b, w1, b1, w2, b2, sw1, sb1, sw2, sb2)

    def _L1_xattn_ref(q, kv, Wq, bq, Wk, bk, Wv, bv, Wo, bo, scale):
        import jax, jax.numpy as jnp
        import numpy as np
        B, LQ, LKV = (4, 64, 256)
        DQ, DKV, H = (128, 96, 16)
        HD = DQ // H
        b, lq, _ = q.shape
        lkv = kv.shape[1]
        qh = (q @ Wq + bq).reshape(b, lq, H, HD).transpose(0, 2, 1, 3)
        kh = (kv @ Wk + bk).reshape(b, lkv, H, HD).transpose(0, 2, 1, 3)
        vh = (kv @ Wv + bv).reshape(b, lkv, H, HD).transpose(0, 2, 1, 3)
        scores = jnp.einsum('bhqd,bhkd->bhqk', qh, kh) * scale[0]
        attn = jax.nn.softmax(scores, axis=-1)
        out = jnp.einsum('bhqk,bhkd->bhqd', attn, vh)
        out = out.transpose(0, 2, 1, 3).reshape(b, lq, DQ)
        return out @ Wo + bo

    def _L1_attn_ref(x, q_proj_weight, k_proj_weight, v_proj_weight, o_proj_weight):
        import jax, jax.numpy as jnp
        import numpy as np
        num_heads = 16
        B, S, d_in = x.shape
        d_k = q_proj_weight.shape[0]
        head_size = d_k // num_heads

        def split_heads(t):
            return t.reshape(B, S, num_heads, head_size).transpose(0, 2, 1, 3)
        q = split_heads(jnp.einsum('bsd,kd->bsk', x, q_proj_weight))
        k = split_heads(jnp.einsum('bsd,kd->bsk', x, k_proj_weight))
        v = split_heads(jnp.einsum('bsd,kd->bsk', x, v_proj_weight))
        scale = jnp.float32(head_size) ** (-0.5)
        scores = jnp.einsum('bhtc,bhkc->bhtk', q, k) * scale
        causal = jnp.tril(jnp.ones((S, S), dtype=bool))
        scores = jnp.where(causal, scores, -jnp.inf)
        attn = jax.nn.softmax(scores, axis=-1)
        out = jnp.einsum('bhtk,bhkc->bhtc', attn, v)
        out = out.transpose(0, 2, 1, 3).reshape(B, S, d_k)
        return jnp.einsum('bsv,dv->bsd', out, o_proj_weight)

    def _L1_ffn_ref(hidden_states, Wr, norm_w, Wg, Wu, Wd, f_norm, fWg, fWu, fWd):
        import jax, jax.numpy as jnp
        import numpy as np
        TOP_K = 2
        CAPACITY = 512
        EPS = 1e-06
        W_SCALE = 0.02

        def _rms(x, w):
            return x * jax.lax.rsqrt(jnp.mean(x * x, axis=-1, keepdims=True) + EPS) * w
        B, S, H = hidden_states.shape
        E = Wr.shape[1]
        N = B * S
        x = hidden_states.reshape(N, H)
        probs = jax.nn.softmax(x @ Wr, axis=-1)
        w_topk, e_topk = jax.lax.top_k(probs, TOP_K)
        e_flat = e_topk.reshape(-1)
        oh = jax.nn.one_hot(e_flat, E, dtype=jnp.int32)
        pos = jnp.take_along_axis(jnp.cumsum(oh, axis=0) - 1, e_flat[:, None], axis=1)[:, 0]
        keep = pos < CAPACITY
        x_rep = jnp.repeat(x, TOP_K, axis=0)
        buf = jnp.zeros((E, CAPACITY, H), x.dtype).at[e_flat, pos].set(x_rep, mode='drop')
        h = _rms(buf, norm_w[:, None, :])
        gate = jax.nn.gelu(jnp.einsum('ech,ehf->ecf', h, Wg), approximate=False)
        up = jnp.einsum('ech,ehf->ecf', h, Wu)
        buf_out = jnp.einsum('ecf,efh->ech', gate * up, Wd) + buf
        exp_out = buf_out[e_flat, jnp.minimum(pos, CAPACITY - 1)]
        contrib = w_topk.reshape(-1)[:, None] * exp_out * keep[:, None].astype(x.dtype)
        combined = x + contrib.reshape(N, TOP_K, H).sum(axis=1)
        overflow = (~keep).reshape(N, TOP_K).any(axis=1)
        fh = _rms(x, f_norm)
        fout = jax.nn.gelu(fh @ fWg, approximate=False) * (fh @ fWu) @ fWd + x
        out = jnp.where(overflow[:, None], fout, combined)
        return out.reshape(B, S, H)
    x = x + _L0_xattn_ref(_layernorm(x, axis=-1), ctx_768, mask_BxS_bf1, mask_BxS2_bf1, L0_xattn_Wq, L0_xattn_Wk, L0_xattn_Wv, L0_xattn_W_film_in, L0_xattn_b_film_in, L0_xattn_W_film_out, L0_xattn_b_film_out, L0_xattn_g_norm_in, L0_xattn_b_norm_in, L0_xattn_g_norm_out, L0_xattn_b_norm_out, L0_xattn_g_ffn, L0_xattn_b_ffn, L0_xattn_W1, L0_xattn_b1, L0_xattn_W2, L0_xattn_b2, L0_xattn_log_dt, L0_xattn_A_re, L0_xattn_A_im, L0_xattn_C_re, L0_xattn_C_im, L0_xattn_D_skip, L0_xattn_mod_gate)
    x = x + _L0_attn_ref(_layernorm(x, axis=-1), L0_attn_gate_w1, L0_attn_gate_b1, L0_attn_gate_w2, L0_attn_gate_b2, L0_attn_U_w, L0_attn_V_w, L0_attn_conv_w, L0_attn_out_w, L0_attn_out_b)
    x = x + _L0_ffn_ref(_layernorm(x, axis=-1), L0_ffn_gate_w, L0_ffn_gate_b, L0_ffn_w1, L0_ffn_b1, L0_ffn_w2, L0_ffn_b2, L0_ffn_sw1, L0_ffn_sb1, L0_ffn_sw2, L0_ffn_sb2)
    x = x + _L1_xattn_ref(_layernorm(x, axis=-1), ctx_768, L1_xattn_Wq, L1_xattn_bq, L1_xattn_Wk, L1_xattn_bk, L1_xattn_Wv, L1_xattn_bv, L1_xattn_Wo, L1_xattn_bo, L1_xattn_scale)
    x = x + _L1_attn_ref(_layernorm(x, axis=-1), L1_attn_q_proj_weight, L1_attn_k_proj_weight, L1_attn_v_proj_weight, L1_attn_o_proj_weight)
    x = x + _L1_ffn_ref(_layernorm(x, axis=-1), L1_ffn_Wr, L1_ffn_norm_w, L1_ffn_Wg, L1_ffn_Wu, L1_ffn_Wd, L1_ffn_f_norm, L1_ffn_fWg, L1_ffn_fWu, L1_ffn_fWd)
    return x

_drawn_inputs = setup_inputs


def setup_inputs(seed=0):
    import zlib

    import numpy as np

    out = dict(_drawn_inputs(seed))
    spreads = {'L0_xattn_b_film_in': (0.0, 0.291),
     'L0_xattn_b_film_out': (0.0, 0.1),
     'L0_xattn_g_norm_in': (1.0, 0.2),
     'L0_xattn_b_norm_in': (0.0, 0.1),
     'L0_xattn_g_norm_out': (1.0, 0.2),
     'L0_xattn_b_norm_out': (0.0, 0.1),
     'L0_xattn_g_ffn': (1.0, 0.6),
     'L0_xattn_b_ffn': (0.0, 0.8),
     'L0_xattn_b1': (0.0, 0.8),
     'L0_xattn_b2': (0.0, 0.285),
     'L0_xattn_A_re': (-0.5, 0.6),
     'L0_attn_gate_b1': (0.0, 0.8),
     'L0_attn_gate_b2': (0.0, 0.8),
     'L0_attn_out_b': (0.0, 0.1),
     'L0_ffn_gate_b': (0.0, 0.1),
     'L0_ffn_b1': (0.0, 0.354),
     'L0_ffn_b2': (0.0, 0.1),
     'L0_ffn_sb1': (0.0, 0.8),
     'L0_ffn_sb2': (0.0, 0.8),
     'L1_xattn_bq': (0.0, 0.8),
     'L1_xattn_bk': (0.0, 0.8),
     'L1_xattn_bv': (0.0, 0.1),
     'L1_xattn_bo': (0.0, 0.1),
     'L1_ffn_norm_w': (1.0, 0.6),
     'L1_ffn_f_norm': (1.0, 0.2)}
    factors = {'L0_xattn_Wq': 8.0,
     'L0_xattn_Wk': 8.0,
     'L0_xattn_Wv': 5.275,
     'L0_xattn_W_film_in': 6.992,
     'L0_xattn_W_film_out': 8.0,
     'L0_xattn_W1': 3.455,
     'L0_xattn_W2': 3.204,
     'L0_attn_gate_w1': 8.0,
     'L0_attn_gate_w2': 8.0,
     'L0_attn_U_w': 8.0,
     'L0_attn_V_w': 8.0,
     'L0_attn_out_w': 8.0,
     'L1_xattn_Wq': 2.866,
     'L1_xattn_Wk': 2.674,
     'L1_attn_q_proj_weight': 8.0,
     'L1_attn_k_proj_weight': 8.0,
     'L1_attn_v_proj_weight': 6.101,
     'L1_attn_o_proj_weight': 6.027,
     'L1_ffn_Wr': 6.947,
     'L1_ffn_Wg': 8.0,
     'L1_ffn_Wu': 8.0,
     'L1_ffn_Wd': 8.0}
    for name, (base, spread) in spreads.items():
        noise = np.random.default_rng([zlib.crc32(name.encode()), seed]).standard_normal(out[name].shape)
        drawn = base * np.exp(spread * noise) if base else spread * noise
        out[name] = jnp.asarray(drawn.astype(out[name].dtype))
    for name, factor in factors.items():
        out[name] = (out[name] * factor).astype(out[name].dtype)
    return out
```

```python
from contextlib import ExitStack

import concourse.bass as bass
import numpy as np
from concourse import mybir

F32 = mybir.dt.float32
BF16 = mybir.dt.bfloat16
U8 = mybir.dt.uint8
I32 = mybir.dt.int32
U32 = mybir.dt.uint32
ALU = mybir.AluOpType
ACT = mybir.ActivationFunctionType
AX_X = mybir.AxisListType.X

T, D, G, DC = 64, 128, 6272, 96
P = 128
NC = G // P
KA = DC + 2
H0, DH0 = 4, 32
H1, DH1 = 16, 8
TOPK = 32
NEG = -1e30
FREQ = T + 1
RA = RB = 8
SQ = 4
NQ = H1 // SQ
GROUPS = [list(range(g, min(g + 4, NC))) for g in range(0, NC, 4)]
RING = 4
SLICE = 7
NSL = NC // SLICE
BANK = 512
SB0 = [(s, min(BANK, G - s)) for s in range(0, G, BANK)]
TWO_PI = 6.2831850
ROUND = 1.5 * 2.0 ** 23
EPS_LN, EPS_RMS = 1e-5, 1e-6

BLOB_A = {"x": (T, D), "ident": (P, P), "wq0": (D, D), "wkT0": (D, KA), "mask_h0": (P, H0)}
BLOB_S = {"a_re": (P, D), "a_im": (P, D), "c_re": (P, D), "c_im": (P, D), "log_dt": (P, D),
          "turn0": (P, 1), "mask_h1": (P, H1)}
BLOB_M = {"film_w": (D, 4 * D), "wvT0": (D, DC), "g_in": (T, D), "b_in": (T, D), "g_out": (T, D), "b_out": (T, D),
          "gate": (P, 1), "sel_t": (P, T), "dft_x": (T, 2 * FREQ),
          "idft": (FREQ, 3 * T), "g_ffn": (D, 1), "b_ffn": (D, 1), "w1": (D, 4 * D), "b1T": (P, 4),
          "w2": (P, 4 * D), "eye_tri": (T, 2 * T), "gw1": (D, 32), "gb1": (32, 1), "gw2": (32, 32), "gb2": (32, 1),
          "u_w": (D, 32), "v_w": (D, 32), "conv": (D, 3), "out_w": (32, D), "iota8": (T, 8)}
BLOB_L = {"rgT": (D, 8), "moe_b1T": (P, 36),
          "wq1": (D, D), "wkT1": (D, KA), "wv1": (KA, D), "bq1": (D, 1), "scale1": (P, 1), "wo1": (P, NQ * D),
          "mask_q": (P, SQ), "sel_r": (P, P), "wqT2": (D, D), "wkT2": (D, D), "wvT2": (D, D), "woT2": (D, D),
          "causal": (T, T), "mask_p": (P, 2), "wr": (D, 8), "norm_wT": (D, 8)}
BLOBS = {"blob_a": BLOB_A, "blob_s": BLOB_S, "blob_m": BLOB_M, "blob_l": BLOB_L}
ROWS = {0: {"film_b": 4 * D, "film_1": 4 * D, "out_b": D}, 32: {"moe_b2": 9 * D},
        64: {"e_mask": KA, "b2": D, "d_skip": D, "rb": 8, "bo1": D}}
ROWS_WIDTH = max(sum(t.values()) for t in ROWS.values())


def width(table):
    return sum(c for _, c in table.values())


def offsets(table):
    at, out = 0, {}
    for name, (r, c) in table.items():
        out[name] = (r, at, c)
        at += c
    return out


SEMAPHORES = """
ld_a ld_s ld_m ld_l ld_rows ld_gmask ld_tmask ld_ctx ld_dft ld_w1 ld_w2 ld_gu ld_down out_stored
var_ready rstd_ready ctx_aug mask_row
x0_ready x0T_ps x0T_sb q0_ps q0_bd qq0_ps qq0_sb
scores_ps scores_evac scores_max cand_ready negm0 z0_ready sel0_ready
rep_ready flag_ps topk_final e_ready w_ready slice_used attnT_ps attnT_sb
dt_ready s4_theta s4_turns s4_sin s4_mag s4_pq m1_ps m1_sb kf_ps kf_sb
s4_z s4_cs s4_inv s4_gain
wcf_ps wcf_sb film_row cT_ps cT_sb film_ps xm_ready xf_ps prod_ready y_ps h0_ready hT0_ps hT0_sb up0_ps
pre0_ready gelu0_ready mlp0_ps 
u1_ready ut_ps ut_sb g1_ps g1_sb g2_ps g2_pre g2_exp glob_ready diag_ready blk1_ps 
v_ready vT_ps vT_sb route_ps route_pre route_exp moe_up_ps moe_pre moe_gelu moe_y_ps moe_acc 
n3_ready n3T_ps n3T_sb q1_ps q1_bd qq1_ps qq1_sb qq1_bf ctx_bf v1_ps v1_sb
max_ps max_used negm1 fix_ps qq_fixed s1_ps p_ready pv_done acc_used z_part zt_ps o_ready y1_ps 
n4_ready n4T_ps n4T_sb qk2_ps q2_sb k2_bd v2_ps v2_bd s2_ps d2_ready p2_ready pT_ps pT_sb o2_ps o2_ready o2T_ps o2T_sb y2_ps 
u6_ready r6_ready u6T_ps u6T_sb h6_sb rt6_ps l6_max l6_exp e6_up_ps e6_gelu e6_gu e6_y_ps out_ready
vec_chain vec_slow pool_chain act_chain 
""".split()


def perceiver_kernel(nc, dram, out):
    with ExitStack() as ctx:
        def sb(name, shape, dt=F32):
            return ctx.enter_context(nc.sbuf_tensor(name, shape, dt))

        S = {n: ctx.enter_context(nc.semaphore(n)) for n in SEMAPHORES}
        ld_ctxT = [ctx.enter_context(nc.semaphore(f"ld_ctxT{i}")) for i in range(4)]

        blob = {n: sb(n, [P, width(t)]) for n, t in BLOBS.items()}
        W = {}
        for bn, table in BLOBS.items():
            for n, (r, at, c) in offsets(table).items():
                W[n] = blob[bn][0:r, at:at + c]
        rows = sb("rows", [65, ROWS_WIDTH])
        for part, table in ROWS.items():
            at = 0
            for n, c in table.items():
                W[n] = rows[part:part + 1, at:at + c]
                at += c
        onec = sb("onec", [P, 4 * T])
        one_at = {n: onec[part:part + 1, :] for part, table in ROWS.items() for n in table}
        ctxT = sb("ctxT", [KA, G])
        ctxn = sb("ctxn", [P, NC * DC])
        scores = sb("scores", [P, 2 * G])
        late = sb("late", [P, G])
        probs = sb("probs", [P, RING * 1024])
        moe_w1 = sb("moe_w1", [P, 9 * 4 * D])
        moe_w2 = ctxn[:, 0:9 * 4 * D]
        attnT = late[:, 0:NC * T]
        ctx_bf = late[0:KA, NC * T:NC * T + G // 2].bitcast(BF16)
        v1 = scores[:, 0:NC * D]
        e_gu = scores[:, G:G + 8 * 4 * P]
        e_dn = scores[:, G + 8 * 4 * P:G + 8 * 4 * P + 8 * 2 * D]
        gmask = ctxn[DC:DC + 1, 0:G // 4].bitcast(U8)
        tmask = sb("tmask", [P, 1], U8)

        st = sb("st", [T, 6]); mv = sb("mv", [T, 2]); ve = sb("ve", [T, 1]); rstd = sb("rstd", [T, 1])
        mhalf = sb("mhalf", [P, 1])
        x0 = sb("x0", [T, D]); xin = sb("xin", [T, D]); x0T = sb("x0T", [P, T])
        qq0 = sb("qq0", [KA, H0 * T])
        top = sb("top", [P, 2, TOPK])
        cnt = sb("cnt", [P, 4]); bad = sb("bad", [P, 2]); flag = sb("flag", [1, 2], I32)
        flagf = sb("flagf", [1, 4])
        negm0 = sb("negm0", [P, 2]); ztop = sb("ztop", [P, 2, TOPK]); z0 = sb("z0", [P, 2]); rz0 = sb("rz0", [P, 2])
        tmf = sb("tmf", [P, 1]); seln = sb("seln", [P, 2, T])
        cT = sb("cT", [DC, T]); wcf = probs[0:DC, RING * 1024 - 4 * D:RING * 1024]; 
        xm = sb("xm", [T, D]); xm2 = sb("xm2", [T, D]); kf = sb("kf", [FREQ, 2, D])
        sh = sb("sh", [T, D]); xt = sb("xt", [T, D]); hn = sb("hn", [T, D]); hT = sb("hT", [P, T])
        xt2 = sb("xt2", [T, D]); nt = sb("nt", [T, D])
        nt2 = sb("nt2", [T, D]); x1 = sb("x1", [T, D]); uT = sb("uT", [P, T + 2])
        cumT = sb("cumT", [P, T]); g1 = sb("g1", [32, T]); ub = sb("ub", [32, T]); us = sb("us", [32, T])
        ge2 = sb("ge2", [32, T]); ge3 = sb("ge3", [32, T]); ge4 = sb("ge4", [32, T]); gpre = sb("gpre", [32, T]); rpre = sb("rpre", [T, 8])
        glob = sb("glob", [32, T]); diag = sb("diag", [P, 3, P]); x2 = sb("x2", [T, D])
        vT = sb("vT", [P, T]); rex = sb("rex", [T, 8]); rex1 = sb("rex1", [T, 8]); rsc = sb("rsc", [T, 8])
        r8 = sb("r8", [T, 8]); ri = sb("ri", [T, 8], U32); rif = sb("rif", [T, 2]); rs = sb("rs", [T, 4])
        rw = sb("rw", [T, 2]); oh = sb("oh", [T, 8]); oh2 = sb("oh2", [T, 8]); comb = sb("comb", [T, 8])
        acc = sb("acc", [T, 4, D])
        n3T = sb("n3T", [P, T]); q1 = sb("q1", [P, T])
        mx = sb("mx", [P, 8, len(SB0)]); nm = sb("nm", [P, 8, 2])
        x4 = sb("x4", [T, D]); n4T = sb("n4T", [P, 2, T])
        q2 = sb("q2", [P, T]); m2 = sb("m2", [T, H1]); s2 = sb("s2", [T, H1])
        i2 = sb("i2", [T, H1]); ooT = sb("ooT", [P, T])
        x5 = sb("x5", [T, D]); u6 = sb("u6", [T, D]); u6T = sb("u6T", [P, T])
        h6T = sb("h6T", [P, T]); m8 = sb("m8", [T, 8]); nm6 = sb("nm6", [T, 1])
        ex6 = sb("ex6", [T, 8]); z6 = sb("z6", [T, 1]); iz6 = sb("iz6", [T, 1]); w6 = sb("w6", [T, 2]); sw6 = sb("sw6", [T, 1])
        msq = sb("msq", [T, 2])

        def carve(region, parts, *shapes):
            at, tiles = 0, []
            for shape in shapes:
                n = int(np.prod(shape))
                t = region[0:parts, at:at + n]
                if len(shape) > 1:
                    names = "abc"[:len(shape)]
                    t = t.rearrange(f"p ({' '.join(names)}) -> p {' '.join(names)}",
                                    **{k: v for k, v in zip(names, shape)})
                tiles.append(t)
                at += n
            assert at <= region.shape[1], (at, region.shape)
            return tiles

        mid = sb("mid", [P, 2 * 2 * NC * 8])
        cand, cwork = carve(mid, P, (2, NC * 8), (2, NC * 8))
        m1, dft_k = carve(late, P, (8, D), (RB * 2 * FREQ,))
        s4p, s4q, g4, ge = carve(moe_w1, P, (D, RA), (D, RB), (16, D), (NC * 8,))
        turns, kint = carve(late, P, (24, D), (24, D))
        mags, smore = carve(probs, P, (16, D), (5, D))
        sdt, sar, sth, stt_, q0bd = carve(scores[:, 2 * G - 6 * D:2 * G], P, (D,), (D,), (D,), (D,), (H0 * T,))
        pre0, hid0, pab = carve(mid, P, (4 * T,), (4 * T,), (4 * D,))
        pa = pab[0:FREQ, 0:2 * D].rearrange("p (c d) -> p c d", c=2)
        pb = pab[0:FREQ, 2 * D:4 * D].rearrange("p (c d) -> p c d", c=2)
        y1 = xm
        pre, = carve(mid, P, (2, BANK))
        hid, = carve(attnT, P, (9 * 4 * T,))
        qbd, qq1_all, om, qq1b_all = carve(attnT, P, (H1, T), (H1 * T,), (2, SQ * T), (H1 * T // 2,))
        qq1, qq1b = qq1_all[0:KA, :], qq1b_all[0:KA, :].bitcast(BF16)
        o1, z1, zi, o2 = carve(mid, P, (NQ, T), (NQ, T), (NQ, T), (NQ, T))
        kbd, d2_all, p2_all, pT = carve(probs, P, (H1, T), (H1, T), (H1, T), (8, T))
        d2, p2 = d2_all[0:T], p2_all[0:T]
        vbd, = carve(mid[:, 4 * NQ * T:], P, (8, 2, 8))
        h6e, gl6, gu6 = carve(attnT, P, (8, T), (8, 2, T), (8, 2, T))
        u1 = v = n3 = n4 = hn
        h6, oo = nt2, nt2

        A = ctx.enter_context(nc.psum_tensor("A", [P, 4, BANK], F32))
        B = [ctx.enter_context(nc.psum_tensor(f"B{i}", [P, BANK], F32)) for i in range(4)]
        block = ctx.enter_context(nc.Block())

        def chunk_cols(t, c):
            return t[:, c * P:(c + 1) * P]

        ctx_cuts = [0, 3 * BANK, 6 * BANK, 9 * BANK, G]

        @block.sync
        def _(sp):
            sp.dma_start(blob["blob_a"][:, :], dram["blob_a"]).then_inc(S["ld_a"], 16)
            sp.dma_start(gmask, dram["gmask"]).then_inc(S["ld_gmask"], 16)
            for part, table in ROWS.items():
                n = sum(table.values())
                sp.dma_start(rows[part:part + 1, 0:n], dram["rows"][part // 32:part // 32 + 1, 0:n]).then_inc(S["ld_rows"], 16)
            for i in range(4):
                a, b = ctx_cuts[i], ctx_cuts[i + 1]
                sp.dma_start(ctxT[0:DC, a:b], dram["ctxT"][:, a:b]).then_inc(ld_ctxT[i], 16)
                if i == 0:
                    sp.dma_start(blob["blob_s"][:, :], dram["blob_s"]).then_inc(S["ld_s"], 16)
            sp.dma_start(tmask[:, :], dram["tmask"]).then_inc(S["ld_tmask"], 16)
            sp.dma_start(blob["blob_m"][:, :], dram["blob_m"]).then_inc(S["ld_m"], 16)
            sp.dma_start(blob["blob_l"][:, :], dram["blob_l"]).then_inc(S["ld_l"], 16)
            sp.wait_ge(S["mask_row"], 4)
            sp.dma_start(ctxn[:, :], dram["ctxn"]).then_inc(S["ld_ctx"], 16)
            sp.wait_ge(S["s4_pq"], 2)
            sp.dma_start(dft_k, dram["dft_k"]).then_inc(S["ld_dft"], 16)
            sp.wait_ge(S["m1_ps"], 1)
            sp.wait_ge(S["rep_ready"], 1)
            sp.dma_start(moe_w1[:, :], dram["moe_w1"]).then_inc(S["ld_w1"], 16)
            sp.wait_ge(S["cT_ps"], 1)
            sp.dma_start(moe_w2, dram["moe_w2"]).then_inc(S["ld_w2"], 16)
            sp.wait_ge(S["w_ready"], 2 * NSL)
            sp.dma_start(e_gu, dram["e_gu"]).then_inc(S["ld_gu"], 16)
            sp.dma_start(e_dn, dram["e_dn"]).then_inc(S["ld_down"], 16)
            sp.wait_ge(S["out_ready"], 1)
            sp.dma_start(out, acc[:, 3, :]).then_inc(S["out_stored"], 16)
            sp.wait_ge(S["out_stored"], 16)

        @block.gpsimd
        def _(pool):
            chain = [0]

            def link(ins):
                chain[0] += 1
                ins.then_inc(S["pool_chain"], 1)
                pool.wait_ge(S["pool_chain"], chain[0])

            def rsqrt(n):
                pool.wait_ge(S["var_ready"], n)
                nc.gpsimd.tensor_tensor(rstd[:, :], ve[:, :], mhalf[0:T, :], ALU.pow).then_inc(S["rstd_ready"], 1)
                pool.wait_ge(S["rstd_ready"], n)

            link(nc.gpsimd.memset(mhalf[:, :], -0.5))
            for i in range(4):
                a, b = ctx_cuts[i], ctx_cuts[i + 1]
                nc.gpsimd.memset(ctxT[DC:KA, a:b], 1.0).then_inc(S["ctx_aug"], 1)
            pool.wait_ge(S["ctx_aug"], 4)
            rsqrt(1)
            pool.wait_ge(S["ld_gmask"], 16)
            for i in range(4):
                a, b = ctx_cuts[i], ctx_cuts[i + 1]
                pool.wait_ge(S["ctx_aug"], i + 1)
                nc.gpsimd.tensor_scalar(ctxT[DC:DC + 1, a:b], gmask[:, a:b], -1.0, -NEG, ALU.add, ALU.mult)\
                    .then_inc(S["mask_row"], 1)
                pool.wait_ge(S["mask_row"], i + 1)
                if i == 0:
                    rsqrt(2)
            tt = nc.gpsimd.tensor_tensor
            pool.wait_ge(S["dt_ready"], 1)
            pool.wait_ge(S["ld_s"], 16)
            tt(sar[:, :], sdt[:, :], W["a_re"], ALU.mult).then_inc(S["s4_theta"], 1)
            link(tt(sth[:, :], sdt[:, :], W["a_im"], ALU.mult))
            link(nc.gpsimd.tensor_scalar(stt_[:, :], sth[:, :], 1.0 / (2.0 * np.pi), 0.0, ALU.mult, ALU.add))
            for l in range(8):
                nc.gpsimd.tensor_scalar(turns[:, l, :], stt_[:, :], float(RB * l), 0.25, ALU.mult, ALU.add)
                nc.gpsimd.tensor_scalar(turns[:, 8 + l, :], stt_[:, :], float(RB * l), 0.0, ALU.mult, ALU.add)
                last = nc.gpsimd.tensor_scalar(turns[:, 16 + l, :], stt_[:, :], float(l), W["turn0"], ALU.mult, ALU.add)
            last.then_inc(S["s4_turns"], 1)
            link(tt(g4[:, 0, :], W["a_re"], W["a_re"], ALU.mult))
            link(tt(g4[:, 1, :], W["a_im"], W["a_im"], ALU.mult))
            tt(g4[:, 2, :], g4[:, 0, :], g4[:, 1, :], ALU.add).then_inc(S["s4_inv"], 1)
            pool.wait_ge(S["s4_z"], 1)
            link(tt(g4[:, 4, :], smore[:, 0, :], smore[:, 1, :], ALU.mult))
            link(tt(g4[:, 5, :], smore[:, 0, :], smore[:, 2, :], ALU.mult))
            link(nc.gpsimd.tensor_scalar(g4[:, 6, :], g4[:, 4, :], 1.0, -1.0, ALU.mult, ALU.add))
            link(tt(g4[:, 7, :], g4[:, 6, :], W["a_re"], ALU.mult))
            link(tt(g4[:, 8, :], g4[:, 5, :], W["a_im"], ALU.mult))
            link(tt(g4[:, 9, :], g4[:, 7, :], g4[:, 8, :], ALU.add))
            link(tt(g4[:, 7, :], g4[:, 5, :], W["a_re"], ALU.mult))
            link(tt(g4[:, 8, :], g4[:, 6, :], W["a_im"], ALU.mult))
            link(tt(g4[:, 10, :], g4[:, 7, :], g4[:, 8, :], ALU.subtract))
            pool.wait_ge(S["s4_gain"], 1)
            link(tt(g4[:, 9, :], g4[:, 9, :], g4[:, 3, :], ALU.mult))
            link(tt(g4[:, 10, :], g4[:, 10, :], g4[:, 3, :], ALU.mult))
            link(tt(g4[:, 11, :], W["c_re"], g4[:, 9, :], ALU.mult))
            link(tt(g4[:, 12, :], W["c_im"], g4[:, 10, :], ALU.mult))
            link(tt(g4[:, 13, :], g4[:, 11, :], g4[:, 12, :], ALU.subtract))
            link(tt(g4[:, 11, :], W["c_re"], g4[:, 10, :], ALU.mult))
            link(tt(g4[:, 12, :], W["c_im"], g4[:, 9, :], ALU.mult))
            link(tt(g4[:, 14, :], g4[:, 11, :], g4[:, 12, :], ALU.add))
            nc.gpsimd.tensor_scalar(g4[0:64, 0, :], g4[0:64, 13, :], 2.0, 0.0, ALU.mult, ALU.add)
            nc.gpsimd.tensor_scalar(g4[64:128, 0, :], g4[64:128, 14, :], -2.0, 0.0, ALU.mult, ALU.add)
            nc.gpsimd.tensor_scalar(g4[0:64, 1, :], g4[0:64, 14, :], -2.0, 0.0, ALU.mult, ALU.add)
            link(nc.gpsimd.tensor_scalar(g4[64:128, 1, :], g4[64:128, 13, :], -2.0, 0.0, ALU.mult, ALU.add))
            pool.wait_ge(S["s4_sin"], 1)
            pool.wait_ge(S["s4_mag"], 1)
            al = g4[:, 0:1, :].to_broadcast([P, 8, D])
            be = g4[:, 1:2, :].to_broadcast([P, 8, D])
            link(tt(kint[:, 0:8, :], turns[:, 0:8, :], al, ALU.mult))
            link(tt(kint[:, 8:16, :], turns[:, 8:16, :], be, ALU.mult))
            link(tt(kint[:, 16:24, :], kint[:, 0:8, :], kint[:, 8:16, :], ALU.add))
            tt(s4p[:, :, :].rearrange("p d l -> p l d"), kint[:, 16:24, :], mags[:, 0:8, :], ALU.mult).then_inc(S["s4_pq"], 1)
            tt(s4q[:, :, :].rearrange("p d l -> p l d"), turns[:, 16:24, :], mags[:, 8:16, :], ALU.mult).then_inc(S["s4_pq"], 1)
            pool.wait_ge(S["ld_m"], 16)
            for j in range(3):
                nc.gpsimd.tensor_scalar(diag[:, j, :], W["ident"], W["conv"][:, j:j + 1], 0.0, ALU.mult, ALU.add)\
                    .then_inc(S["diag_ready"], 1)
            pool.wait_ge(S["topk_final"], 1)
            pool.wait_ge(S["mask_row"], 4)
            for i in range(4):
                a, b = ctx_cuts[i], ctx_cuts[i + 1]
                pool.wait_ge(ld_ctxT[i], 16)
                nc.gpsimd.tensor_scalar(ctx_bf[:, a:b], ctxT[:, a:b], 1.0, 0.0, ALU.mult, ALU.add).then_inc(S["ctx_bf"], 1)
            for n in range(3, 11):
                rsqrt(n)

        @block.scalar
        def _(act):
            chain = [0]

            def link(ins):
                chain[0] += 1
                ins.then_inc(S["act_chain"], 1)
                act.wait_ge(S["act_chain"], chain[0])

            A_ = nc.scalar.activation
            act.wait_ge(S["ld_s"], 16)
            A_(sdt[:, :], W["log_dt"], ACT.Exp).then_inc(S["dt_ready"], 1)
            act.wait_ge(S["s4_theta"], 1)
            for l in range(8):
                A_(mags[:, l, :], sar[:, :], ACT.Exp, scale=float(RB * l))
                last = A_(mags[:, 8 + l, :], sar[:, :], ACT.Exp, scale=float(l))
            link(A_(smore[:, 0, :], sar[:, :], ACT.Exp))
            last.then_inc(S["s4_mag"], 1)

            def evac_scores(n):
                k, (s, w) = n // len(SB0), SB0[n % len(SB0)]
                act.wait_ge(S["scores_ps"], n + 1)
                A_(scores[:, k * G + s:k * G + s + w], A[:, n % 4, 0:w], ACT.Copy).then_inc(S["scores_evac"], 1)

            for n in range(4):
                evac_scores(n)
            act.wait_ge(S["s4_cs"], 1)
            A_(turns[:, :, :], kint[:, :, :], ACT.Sin, scale=TWO_PI).then_inc(S["s4_sin"], 1)
            A_(smore[:, 1:3, :], smore[:, 3:5, :], ACT.Sin, scale=TWO_PI).then_inc(S["s4_z"], 1)
            for n in range(4, 2 * len(SB0)):
                evac_scores(n)
            for k in range(2):
                act.wait_ge(S["negm0"], k + 1)
                A_(ztop[:, k, :], top[:, k, :], ACT.Exp, bias=negm0[:, k:k + 1], accum_out=z0[:, k:k + 1])\
                    .then_inc(S["z0_ready"], 1)
            act.wait_ge(S["s4_pq"], 2)
            act.wait_ge(S["topk_final"], 1)
            banks = [list(range(b, min(b + 8, NC))) for b in range(0, NC, 8)]

            def evac_attn(b):
                act.wait_ge(S["attnT_ps"], b + 1)
                a, n = banks[b][0], len(banks[b])
                A_(attnT[:, a * T:(a + n) * T], B[2 + b % 2][:, 0:n * T], ACT.Copy).then_inc(S["attnT_sb"], 1)

            done = 0
            for s in range(NSL):
                for k in range(2):
                    if s >= 2:
                        act.wait_ge(S["slice_used"], s - 1)
                    slot = (s % 2) * 2 + k
                    A_(probs[:, slot * 896:(slot + 1) * 896],
                       scores[:, k * G + s * 896:k * G + (s + 1) * 896], ACT.Exp, bias=negm0[:, k:k + 1])\
                        .then_inc(S["e_ready"], 1)
                while s >= 1 and done < len(banks) and banks[done][-1] < SLICE * (s - 1):
                    evac_attn(done)
                    done += 1
            while done < len(banks):
                evac_attn(done)
                done += 1
            act.wait_ge(S["pre0_ready"], 1)
            A_(hid0[:, :], pre0[:, :], ACT.Gelu).then_inc(S["gelu0_ready"], 1)
            act.wait_ge(S["g2_pre"], 1)
            A_(ge2[:, :], gpre[:, :], ACT.Exp, scale=-1.0).then_inc(S["g2_exp"], 1)
            act.wait_ge(S["route_pre"], 1)
            A_(rex[:, :], rpre[:, :], ACT.Exp, scale=-1.0).then_inc(S["route_exp"], 1)
            for p in range(5):
                act.wait_ge(S["moe_pre"], p + 1)
                w = BANK if p < 4 else 256
                A_(hid[:, p * BANK:p * BANK + w], pre[:, p % 2, 0:w], ACT.Gelu).then_inc(S["moe_gelu"], 1)
            act.wait_ge(S["qq1_sb"], 1)
            A_(qq1b[:, :], qq1[:, :], ACT.Copy).then_inc(S["qq1_bf"], 1)
            for b in range(13):
                act.wait_ge(S["v1_ps"], b + 1)
                n = min(4, NC - 4 * b)
                A_(v1[:, 4 * b * D:(4 * b + n) * D], B[b % 2][:, 0:n * D], ACT.Copy).then_inc(S["v1_sb"], 1)
            n = 0
            for j in range(NQ):
                for g, cs in enumerate(GROUPS):
                    act.wait_ge(S["s1_ps"], n + 1)
                    if n >= RING:
                        act.wait_ge(S["pv_done"], n - RING + 1)
                    w = len(cs) * SQ * T
                    A_(probs[:, (n % RING) * 1024:(n % RING) * 1024 + w],
                       A[:, 2 * (n % 2):2 * (n % 2) + 2, :].rearrange("p a b -> p (a b)")[:, 0:w],
                       ACT.Exp).then_inc(S["p_ready"], 1)
                    n += 1
            act.wait_ge(S["d2_ready"], 1)
            A_(p2[:, :, :], d2[:, :, :], ACT.Exp).then_inc(S["p2_ready"], 1)
            act.wait_ge(S["l6_max"], 1)
            A_(ex6[:, :], B[3][0:T, 0:8], ACT.Exp, bias=nm6[:, :], accum_out=z6[:, :]).then_inc(S["l6_exp"], 1)
            for p in range(4):
                act.wait_ge(S["e6_up_ps"], p + 1)
                src = A[:, p, :].rearrange("p (e u f t) -> p e u f t", e=2, u=2, f=2)[:, :, 0, :, :]
                A_(gl6[:, 2 * p:2 * p + 2, :, :], src, ACT.Gelu).then_inc(S["e6_gelu"], 1)

        @block.vector
        def _(dve):
            chain = [0]
            norm = [0]
            V = nc.vector

            def link(ins):
                chain[0] += 1
                ins.then_inc(S["vec_chain"], 1)
                dve.wait_ge(S["vec_chain"], chain[0])

            def layernorm(dst, src, signal=None):
                link(V.bn_stats(st[:, :], src))
                link(V.bn_aggr(mv[:, :], st[:, :]))
                V.tensor_scalar_add(ve[:, :], mv[:, 1:2], EPS_LN).then_inc(S["var_ready"], 1)
                norm[0] += 1
                dve.wait_ge(S["rstd_ready"], norm[0])
                ins = V.tensor_scalar(dst, src, mv[:, 0:1], rstd[:, :], ALU.subtract, ALU.mult)
                if signal:
                    ins.then_inc(signal, 1)
                else:
                    link(ins)

            link(V.memset(onec[:, :], 1.0))
            link(V.memset(nm[:, :, :], 0.0))
            link(V.memset(uT[:, :], 0.0))
            dve.wait_ge(S["ld_a"], 16)
            layernorm(x0[:, :], W["x"])
            V.tensor_scalar_add(nt[:, :], x0[:, :], 0.0).then_inc(S["x0_ready"], 1)
            dve.wait_ge(S["x0T_ps"], 1)
            V.tensor_copy(x0T[:, :], B[0][:, 0:T]).then_inc(S["x0T_sb"], 1)
            dve.wait_ge(S["q0_ps"], 1)
            V.tensor_tensor(q0bd[:, :].rearrange("p (h t) -> p h t", h=H0),
                            B[0][:, T:2 * T].unsqueeze(1).to_broadcast([P, H0, T]),
                            W["mask_h0"].unsqueeze(2).to_broadcast([P, H0, T]), ALU.mult).then_inc(S["q0_bd"], 1)
            dve.wait_ge(S["qq0_ps"], 1)
            V.tensor_copy(qq0[:, :], B[1][0:KA, 0:H0 * T]).then_inc(S["qq0_sb"], 1)
            layernorm(xin[:, :], x0[:, :])

            def chunk_max(n):
                k, (s, w) = n // len(SB0), SB0[n % len(SB0)]
                dve.wait_ge(S["scores_evac"], n + 1)
                for i in range(w // P):
                    c = s // P + i
                    last = V.max(cand[:, k, 8 * c:8 * c + 8], scores[:, k * G + c * P:k * G + (c + 1) * P])
                last.then_inc(S["scores_max"], 1)

            def top32(k):
                dve.wait_ge(S["scores_max"], len(SB0) * (k + 1))
                for r in range(TOPK // 8):
                    src = cand if r == 0 else cwork
                    link(V.max(top[:, k, 8 * r:8 * r + 8], src[:, k, :]))
                    if r < TOPK // 8 - 1:
                        link(V.match_replace(cwork[:, k, :], top[:, k, 8 * r:8 * r + 8], src[:, k, :], -3e38))
                tau = top[:, k, TOPK - 1:TOPK]
                V.tensor_scalar(negm0[:, k:k + 1], top[:, k, 0:1], -1.0, None, ALU.mult).then_inc(S["cand_ready"], 1)
                link(V.tensor_scalar(ge[:, :], cand[:, k, :], tau, None, ALU.is_ge))
                link(V.tensor_reduce(cnt[:, 2 * k:2 * k + 1], ge[:, :], AX_X, ALU.add))
                link(V.tensor_reduce(cnt[:, 2 * k + 1:2 * k + 2],
                                     ge[:, :].rearrange("p (c e) -> p c e", e=8)[:, :, 7], AX_X, ALU.add))
                link(V.tensor_tensor(bad[:, k:k + 1], cnt[:, 2 * k:2 * k + 1], cnt[:, 2 * k + 1:2 * k + 2], ALU.add))

            for n in range(len(SB0)):
                chunk_max(n)
                if n == 1:
                    dve.wait_ge(S["s4_turns"], 1)
                    link(V.tensor_scalar(kint, turns, ROUND, ROUND, ALU.add, ALU.subtract))
                    link(V.tensor_tensor(kint, turns, kint, ALU.subtract))
                    link(V.tensor_scalar(g4[:, 14, :], stt_[:, :], 1.0, 0.25, ALU.mult, ALU.add))
                    link(V.tensor_scalar(g4[:, 13, :], g4[:, 14, :], ROUND, ROUND, ALU.add, ALU.subtract))
                    link(V.tensor_scalar(g4[:, 12, :], stt_[:, :], ROUND, ROUND, ALU.add, ALU.subtract))
                    link(V.tensor_tensor(smore[:, 3, :], g4[:, 14, :], g4[:, 13, :], ALU.subtract))
                    V.tensor_tensor(smore[:, 4, :], stt_[:, :], g4[:, 12, :], ALU.subtract).then_inc(S["s4_cs"], 1)
                    dve.wait_ge(S["s4_inv"], 1)
                    V.reciprocal(g4[:, 3, :], g4[:, 2, :]).then_inc(S["s4_gain"], 1)
            top32(0)
            for n in range(len(SB0), 2 * len(SB0)):
                chunk_max(n)
            top32(1)
            dve.wait_ge(S["m1_ps"], 1)
            for q in range(2):
                V.tensor_tensor(m1[:, 4 * q:4 * q + 4, :].rearrange("p g (d b) -> p (g d) b", b=RB),
                                A[:, q, :].rearrange("p (g d b) -> p (g d) b", g=4, b=RB),
                                W["mask_h1"].unsqueeze(1).unsqueeze(3).to_broadcast([P, 4, H1, RB])
                                .rearrange("p g d b -> p g d b"), ALU.mult).then_inc(S["m1_sb"], 1)
            dve.wait_ge(S["scores_evac"], 2 * len(SB0))
            V.tensor_scalar_add(rz0[:, :], bad[:, :], 0.0).then_inc(S["rep_ready"], 1)
            dve.wait_ge(S["kf_ps"], 1)
            V.tensor_copy(kf[:, :, :], A[0:FREQ, 3, 0:2 * D].rearrange("p (c d) -> p c d", c=2)).then_inc(S["kf_sb"], 1)
            dve.wait_ge(S["flag_ps"], 1)
            link(V.tensor_reduce(flagf[:, 0:1], B[1][0:1, 0:2], AX_X, ALU.add))
            link(V.tensor_scalar(flag[:, 0:1], flagf[:, 0:1], float(2 * P * TOPK), None, ALU.is_gt))
            need_exact = dve.value_load(flag[0:1, 0:1], min_val=0, max_val=1)
            with dve.If(need_exact > 0):
                step = [0]

                def slow(ins):
                    step[0] += 1
                    ins.then_inc(S["vec_slow"], 1)
                    dve.wait_ge(S["vec_slow"], step[0])

                for k in range(2):
                    tile = scores[:, k * G:(k + 1) * G]
                    for r in range(TOPK // 8):
                        src = tile if r == 0 else late[:, :]
                        slow(V.max(top[:, k, 8 * r:8 * r + 8], src))
                        slow(V.match_replace(late[:, :], top[:, k, 8 * r:8 * r + 8], src, -3e38))
                    slow(V.tensor_scalar(late[:, :], late[:, :], -2e38, -1e36, ALU.is_gt, ALU.mult))
                    slow(V.tensor_tensor(tile, tile, late[:, :], ALU.add))
            V.tensor_scalar(negm0[:, :], top[:, :, 0], -1.0, None, ALU.mult).then_inc(S["topk_final"], 1)
            dve.wait_ge(S["topk_final"], 1)
            V.tensor_scalar(rz0[:, :], top[:, :, 0], -1.0, None, ALU.mult).then_inc(S["negm0"], 2)
            dve.wait_ge(S["ld_tmask"], 16)
            link(V.tensor_copy(tmf[:, :], tmask[:, :]))
            dve.wait_ge(S["z0_ready"], 2)
            link(V.reciprocal(rz0[:, :], z0[:, :]))
            link(V.tensor_scalar(rz0[:, :], rz0[:, :], tmf[:, :], 1.0 / H0, ALU.mult, ALU.mult))
            dve.wait_ge(S["ld_m"], 16)
            for k in range(2):
                V.tensor_scalar(seln[:, k, :], W["sel_t"], rz0[:, k:k + 1], None, ALU.mult).then_inc(S["sel0_ready"], 1)
            for s in range(NSL):
                for k in range(2):
                    dve.wait_ge(S["e_ready"], 2 * s + k + 1)
                    slot = (s % 2) * 2 + k
                    e = probs[:, slot * 896:(slot + 1) * 896]
                    V.scalar_tensor_tensor(e, scores[:, k * G + s * 896:k * G + (s + 1) * 896],
                                           top[:, k, TOPK - 1:TOPK], e, ALU.is_ge, ALU.mult).then_inc(S["w_ready"], 1)
                if s == 2:
                    dve.wait_ge(S["wcf_ps"], 1)
                    V.tensor_scalar(wcf[:, :], A[0:DC, 2, :], W["gate"][0:DC, :], None, ALU.mult).then_inc(S["wcf_sb"], 1)
                    dve.wait_ge(S["ld_rows"], 16 * len(ROWS))
                    V.scalar_tensor_tensor(W["film_1"], W["film_b"], W["gate"][0:1, :], W["film_1"],
                                           ALU.mult, ALU.add).then_inc(S["film_row"], 1)
                    link(V.tensor_tensor(xin[:, :], xin[:, :], W["g_in"], ALU.mult))
                    link(V.tensor_tensor(xin[:, :], xin[:, :], W["b_in"], ALU.add))
            dve.wait_ge(S["cT_ps"], 1)
            V.tensor_copy(cT[:, :], B[0][0:DC, 0:T]).then_inc(S["cT_sb"], 1)
            dve.wait_ge(S["film_ps"], 1)
            link(V.tensor_tensor(xm[:, :], xin[:, :], B[1][0:T, 0:D], ALU.mult))
            V.tensor_tensor(xm2[:, :], xm[:, :], B[1][0:T, D:2 * D], ALU.add).then_inc(S["xm_ready"], 1)
            link(V.tensor_tensor(sh[:, :], x0[:, :], B[1][0:T, 3 * D:4 * D], ALU.add))
            dve.wait_ge(S["xf_ps"], 1)
            xf = B[2][0:FREQ, 0:2 * D].rearrange("p (c d) -> p c d", c=2)
            dve.wait_ge(S["kf_sb"], 1)
            V.tensor_tensor(pa[:, :, :], xf, kf[:, 0:1, :].to_broadcast([FREQ, 2, D]), ALU.mult)
            V.tensor_tensor(pb[:, :, :], xf, kf[:, 1:2, :].to_broadcast([FREQ, 2, D]), ALU.mult).then_inc(S["prod_ready"], 1)
            dve.wait_ge(S["y_ps"], 1)
            link(V.tensor_copy(y1[:, :], B[3][0:T, 0:D]))
            link(V.tensor_tensor(y1[:, :], y1[:, :], B[1][0:T, 2 * D:3 * D], ALU.mult))
            link(V.tensor_tensor(xt[:, :], y1[:, :], sh[:, :], ALU.add))
            layernorm(hn[:, :], xt[:, :], S["h0_ready"])
            dve.wait_ge(S["hT0_ps"], 1)
            V.tensor_scalar(hT[:, :], B[2][:, 0:T], W["g_ffn"], W["b_ffn"], ALU.mult, ALU.add).then_inc(S["hT0_sb"], 1)
            dve.wait_ge(S["up0_ps"], 1)
            V.tensor_tensor(pre0[:, :].rearrange("p (c t) -> p c t", c=4), B[3][:, 0:4 * T].rearrange("p (c t) -> p c t", c=4),
                            W["b1T"].unsqueeze(2).to_broadcast([P, 4, T]), ALU.add).then_inc(S["pre0_ready"], 1)
            dve.wait_ge(S["mlp0_ps"], 1)
            link(V.tensor_tensor(xt2[:, :], xt[:, :], B[2][0:T, 0:D], ALU.add))
            layernorm(nt[:, :], xt2[:, :])
            link(V.tensor_tensor(nt2[:, :], nt[:, :], W["g_out"], ALU.mult))
            link(V.tensor_tensor(nt[:, :], nt2[:, :], W["b_out"], ALU.add))
            link(V.tensor_tensor(x1[:, :], nt[:, :], W["x"], ALU.add))
            layernorm(u1[:, :], x1[:, :], S["u1_ready"])
            dve.wait_ge(S["ut_ps"], 1)
            V.tensor_copy(uT[:, 1:T + 1], B[2][:, 0:T]).then_inc(S["ut_sb"], 1)
            V.tensor_copy(cumT[:, :], B[2][:, T:2 * T]).then_inc(S["ut_sb"], 1)
            dve.wait_ge(S["g1_ps"], 1)
            V.tensor_scalar(g1[:, :], B[3][0:32, 0:T], W["gb1"], 0.0, ALU.add, ALU.max).then_inc(S["g1_sb"], 1)
            link(V.tensor_copy(ub[:, :], B[3][0:32, T:2 * T]))
            dve.wait_ge(S["g1_ps"], 2)
            link(V.tensor_tensor(us[:, :], ub[:, :], B[0][0:32, 0:T], ALU.mult))
            dve.wait_ge(S["g2_ps"], 1)
            V.tensor_scalar(gpre[:, :], B[1][0:32, 0:T], W["gb2"], -87.0, ALU.add, ALU.max).then_inc(S["g2_pre"], 1)
            dve.wait_ge(S["g2_exp"], 1)
            link(V.tensor_scalar_add(ge3[:, :], ge2[:, :], 1.0))
            link(V.reciprocal(ge4[:, :], ge3[:, :]))
            V.tensor_tensor(glob[:, :], us[:, :], ge4[:, :], ALU.mult).then_inc(S["glob_ready"], 1)
            dve.wait_ge(S["blk1_ps"], 1)
            link(V.tensor_tensor(x2[:, :], x1[:, :], B[2][0:T, 0:D], ALU.add))
            layernorm(v[:, :], x2[:, :], S["v_ready"])
            dve.wait_ge(S["vT_ps"], 1)
            V.tensor_copy(vT[:, :], B[3][:, 2 * D:2 * D + T]).then_inc(S["vT_sb"], 1)
            dve.wait_ge(S["route_ps"], 1)
            V.tensor_scalar(rpre[:, :], B[3][0:T, 0:8], 1.0, -87.0, ALU.mult, ALU.max).then_inc(S["route_pre"], 1)
            dve.wait_ge(S["route_exp"], 1)
            link(V.tensor_scalar_add(rex1[:, :], rex[:, :], 1.0))
            link(V.reciprocal(rsc[:, :], rex1[:, :]))

            def choose_two(p8, r):
                link(V.max(r8[:, :], p8))
                link(V.max_index(ri[:, :], r8[:, :], p8))
                link(V.tensor_copy(rif[:, :], ri[:, 0:2]))
                r()
                link(V.tensor_scalar(oh[:, :], W["iota8"], rif[:, 0:1], rw[:, 0:1], ALU.is_equal, ALU.mult))
                link(V.tensor_scalar(oh2[:, :], W["iota8"], rif[:, 1:2], rw[:, 1:2], ALU.is_equal, ALU.mult))
                link(V.tensor_tensor(comb[:, :], oh[:, :], oh2[:, :], ALU.add))

            def normalised():
                link(V.tensor_tensor(rs[:, 0:1], r8[:, 0:1], r8[:, 1:2], ALU.add))
                link(V.tensor_scalar_add(rs[:, 1:2], rs[:, 0:1], 1e-6))
                link(V.reciprocal(rs[:, 2:3], rs[:, 1:2]))
                link(V.tensor_scalar(rw[:, :], r8[:, 0:2], rs[:, 2:3], None, ALU.mult))

            def moe_pre(p):
                dve.wait_ge(S["moe_up_ps"], p + 1)
                if p >= 2:
                    dve.wait_ge(S["moe_gelu"], p - 1)
                n = 8 if p < 4 else 4
                V.tensor_tensor(pre[:, p % 2, 0:n * T].rearrange("p (c t) -> p c t", t=T),
                                A[:, p % 4, 0:n * T].rearrange("p (c t) -> p c t", t=T),
                                W["moe_b1T"][:, 8 * p:8 * p + n].unsqueeze(2).to_broadcast([P, n, T]),
                                ALU.add).then_inc(S["moe_pre"], 1)

            dve.wait_ge(S["ld_l"], 16)
            moe_pre(0)
            moe_pre(1)
            choose_two(rsc[:, :], normalised)
            for p in range(2, 5):
                moe_pre(p)
            prev = x2[:, :]
            for e in range(9):
                dve.wait_ge(S["moe_y_ps"], e + 1)
                V.scalar_tensor_tensor(acc[:, e % 2, :], B[e % 4][0:T, 0:D], comb[:, e:e + 1] if e < 8 else 0.1,
                                       prev, ALU.mult, ALU.add).then_inc(S["moe_acc"], 1)
                dve.wait_ge(S["moe_acc"], e + 1)
                prev = acc[:, e % 2, :]
            x3 = acc[:, 2, :]
            link(V.tensor_copy(x3, prev))
            layernorm(n3[:, :], x3, S["n3_ready"])
            dve.wait_ge(S["n3T_ps"], 1)
            V.tensor_copy(n3T[:, :], B[3][:, 0:T]).then_inc(S["n3T_sb"], 1)
            dve.wait_ge(S["q1_ps"], 1)
            link(V.tensor_scalar(q1[:, :], B[3][:, T:2 * T], W["bq1"], W["scale1"], ALU.add, ALU.mult))
            V.tensor_tensor(qbd[:, :, :], q1[:, :].unsqueeze(1).to_broadcast([P, H1, T]),
                            W["mask_h1"].unsqueeze(2).to_broadcast([P, H1, T]), ALU.mult).then_inc(S["q1_bd"], 1)
            dve.wait_ge(S["qq1_ps"], 2)
            V.tensor_copy(qq1[:, :], A[0:KA, 0:2, :].rearrange("p a b -> p (a b)")).then_inc(S["qq1_sb"], 1)

            def row_max(n):
                i, (s, w) = n // len(SB0), SB0[n % len(SB0)]
                dve.wait_ge(S["max_ps"], n + 1)
                V.tensor_reduce(mx[:, i, n % len(SB0):n % len(SB0) + 1], B[2 + n % 2][:, 0:w], AX_X, ALU.max)\
                    .then_inc(S["max_used"], 1)

            def shift_quad(j):
                dve.wait_ge(S["max_used"], 2 * len(SB0) * (j + 1))
                V.tensor_reduce(nm[:, 2 * j:2 * j + 2, 1:2], mx[:, 2 * j:2 * j + 2, :], AX_X, ALU.max, negate=True)\
                    .then_inc(S["negm1"], 1)
                dve.wait_ge(S["fix_ps"], j + 1)
                cols = slice(j * SQ * T, (j + 1) * SQ * T)
                V.tensor_tensor(qq1[DC:KA, cols], B[2][DC:KA, 0:SQ * T], qq1[DC:KA, cols], ALU.add).then_inc(S["qq_fixed"], 1)

            NM = 2 * len(SB0)
            for n in range(NM):
                row_max(n)
            dve.wait_ge(S["qq1_sb"], 1)
            shift_quad(0)
            for j in range(NQ):
                if j + 1 < NQ:
                    for n in range(NM * (j + 1), NM * (j + 2)):
                        row_max(n)
                    shift_quad(j + 1)
                dve.wait_ge(S["pv_done"], len(GROUPS) * (j + 1))
                for i in range(2):
                    V.tensor_tensor(om[:, i, :].rearrange("p (h t) -> p h t", h=SQ),
                                    B[i][:, 0:SQ * T].rearrange("p (h t) -> p h t", h=SQ),
                                    W["mask_q"].unsqueeze(2).to_broadcast([P, SQ, T]), ALU.mult).then_inc(S["acc_used"], 1)
                dve.wait_ge(S["acc_used"], 2 * (j + 1))
                V.tensor_reduce(o1[:, j, :], om[:, 0, :].rearrange("p (h t) -> p t h", h=SQ), AX_X, ALU.add)
                link(V.tensor_reduce(z1[:, j, :], om[:, 1, :].rearrange("p (h t) -> p t h", h=SQ), AX_X, ALU.add))
            V.tensor_scalar_add(om[:, 0, :].rearrange("p (q t) -> p q t", q=NQ), z1[:, :, :], 0.0).then_inc(S["z_part"], 1)
            dve.wait_ge(S["zt_ps"], 1)
            link(V.reciprocal(zi[:, :, :], B[2][:, 0:NQ * T].rearrange("p (q t) -> p q t", q=NQ)))
            V.tensor_tensor(o2[:, :, :], o1[:, :, :], zi[:, :, :], ALU.mult).then_inc(S["o_ready"], 1)
            dve.wait_ge(S["y1_ps"], 1)
            link(V.tensor_tensor(x4[:, :], x3, B[3][0:T, 0:D], ALU.add))
            layernorm(n4[:, :], x4[:, :], S["n4_ready"])
            dve.wait_ge(S["n4T_ps"], 1)
            V.tensor_copy(n4T[:, 0, :], B[2][:, 0:T])
            V.tensor_copy(n4T[:, 1, :], B[2][:, 0:T]).then_inc(S["n4T_sb"], 1)
            dve.wait_ge(S["qk2_ps"], 1)
            V.tensor_scalar(q2[:, :], B[3][:, 0:T], float(DH1) ** -0.5, None, ALU.mult).then_inc(S["q2_sb"], 1)
            V.tensor_tensor(kbd[:, :, :], B[3][:, T:2 * T].unsqueeze(1).to_broadcast([P, H1, T]),
                            W["mask_h1"].unsqueeze(2).to_broadcast([P, H1, T]), ALU.mult).then_inc(S["k2_bd"], 1)
            dve.wait_ge(S["v2_ps"], 1)
            V.tensor_tensor(vbd[:, :, :, :], B[0][:, 0:D].rearrange("p (q h c) -> p q h c", h=2, c=8),
                            W["mask_p"].unsqueeze(1).unsqueeze(3).to_broadcast([P, 8, 2, 8]), ALU.mult).then_inc(S["v2_bd"], 1)
            dve.wait_ge(S["s2_ps"], 1)
            sc2 = A[0:T, 0:2, :].rearrange("p a (h k) -> p (a h) k", k=T)
            link(V.tensor_reduce(m2[:, :], sc2, AX_X, ALU.max))
            V.tensor_tensor(d2[:, :, :], sc2, m2[:, :].unsqueeze(2).to_broadcast([T, H1, T]), ALU.subtract)\
                .then_inc(S["d2_ready"], 1)
            dve.wait_ge(S["p2_ready"], 1)
            link(V.tensor_reduce(s2[:, :], p2[:, :, :], AX_X, ALU.add))
            link(V.reciprocal(i2[:, :], s2[:, :]))
            dve.wait_ge(S["pT_ps"], 1)
            V.tensor_copy(pT[:, :, :], A[:, 2, :].rearrange("p (q t) -> p q t", q=8)).then_inc(S["pT_sb"], 1)
            dve.wait_ge(S["o2_ps"], 1)
            V.tensor_tensor(oo[:, :].rearrange("p (h c) -> p h c", c=8), B[1][0:T, 0:D].rearrange("p (h c) -> p h c", c=8),
                            i2[:, :].unsqueeze(2).to_broadcast([T, H1, 8]), ALU.mult).then_inc(S["o2_ready"], 1)
            dve.wait_ge(S["o2T_ps"], 1)
            V.tensor_copy(ooT[:, :], B[2][:, 0:T]).then_inc(S["o2T_sb"], 1)
            dve.wait_ge(S["y2_ps"], 1)
            link(V.tensor_tensor(x5[:, :], x4[:, :], B[3][0:T, 0:D], ALU.add))
            layernorm(u6[:, :], x5[:, :])
            link(V.bn_stats(st[:, :], u6[:, :]))
            link(V.bn_aggr(mv[:, :], st[:, :]))
            link(V.tensor_tensor(msq[:, 0:1], mv[:, 0:1], mv[:, 0:1], ALU.mult))
            V.scalar_tensor_tensor(ve[:, :], msq[:, 0:1], EPS_RMS, mv[:, 1:2], ALU.add, ALU.add).then_inc(S["var_ready"], 1)
            V.tensor_scalar_add(nt[:, :], u6[:, :], 0.0).then_inc(S["u6_ready"], 1)
            norm[0] += 1
            dve.wait_ge(S["rstd_ready"], norm[0])
            V.tensor_scalar(h6[:, :], u6[:, :], rstd[:, :], None, ALU.mult).then_inc(S["r6_ready"], 1)
            dve.wait_ge(S["u6T_ps"], 1)
            V.tensor_copy(u6T[:, :], B[2][:, 0:T]).then_inc(S["u6T_sb"], 1)
            dve.wait_ge(S["u6T_ps"], 2)
            link(V.tensor_copy(h6T[:, :], B[2][:, T:2 * T]))
            V.tensor_tensor(h6e[:, :, :], h6T[:, :].unsqueeze(1).to_broadcast([P, 8, T]),
                            W["norm_wT"].unsqueeze(2).to_broadcast([P, 8, T]), ALU.mult).then_inc(S["h6_sb"], 1)
            dve.wait_ge(S["rt6_ps"], 1)
            link(V.max(m8[:, :], B[3][0:T, 0:8]))
            V.tensor_scalar(nm6[:, :], m8[:, 0:1], -1.0, None, ALU.mult).then_inc(S["l6_max"], 1)
            dve.wait_ge(S["l6_exp"], 1)
            link(V.reciprocal(iz6[:, :], z6[:, :]))
            link(V.tensor_scalar(rsc[:, :], ex6[:, :], iz6[:, :], None, ALU.mult))

            def plain():
                link(V.tensor_copy(rw[:, :], r8[:, 0:2]))

            choose_two(rsc[:, :], plain)
            link(V.tensor_tensor(sw6[:, :], rw[:, 0:1], rw[:, 1:2], ALU.add))
            link(V.tensor_scalar_add(w6[:, 0:1], sw6[:, :], 1.0))
            link(V.scalar_tensor_tensor(xt[:, :], u6[:, :], w6[:, 0:1], x5[:, :], ALU.mult, ALU.add))
            for p in range(4):
                dve.wait_ge(S["e6_gelu"], p + 1)
                up = A[:, p, :].rearrange("p (e u x) -> p e u x", e=2, u=2)[:, :, 1, :]
                V.tensor_tensor(gu6[:, 2 * p:2 * p + 2, :, :].rearrange("p e f t -> p e (f t)"),
                                gl6[:, 2 * p:2 * p + 2, :, :].rearrange("p e f t -> p e (f t)"), up, ALU.mult)\
                    .then_inc(S["e6_gu"], 1)
            prev = xt[:, :]
            for e in range(8):
                dve.wait_ge(S["e6_y_ps"], e + 1)
                y = B[e % 4][0:T, 0:D]
                nxt = acc[:, e % 2, :] if e < 7 else acc[:, 3, :]
                ins = V.scalar_tensor_tensor(nxt, y, comb[:, e:e + 1], prev, ALU.mult, ALU.add)
                if e < 7:
                    ins.then_inc(S["moe_acc"], 1)
                    dve.wait_ge(S["moe_acc"], 10 + e)
                else:
                    ins.then_inc(S["out_ready"], 1)
                prev = nxt

        @block.tensor
        def _(pe):
            mm = nc.tensor.matmul
            idT = W["ident"][0:T, 0:T]

            def one(out_, lhsT, rhs, start=True, stop=True):
                return mm(out_, lhsT, rhs, start=start, stop=stop)

            pe.wait_ge(S["ld_a"], 16)
            pe.wait_ge(S["x0_ready"], 1)
            nc.tensor.transpose(B[0][:, 0:T], x0[:, :], idT).then_inc(S["x0T_ps"], 1)
            pe.wait_ge(S["x0T_sb"], 1)
            one(B[0][:, T:2 * T], W["wq0"], x0T[:, :]).then_inc(S["q0_ps"], 1)
            pe.wait_ge(S["q0_bd"], 1)
            pe.wait_ge(S["ld_rows"], 16 * len(ROWS))
            one(B[1][0:KA, 0:H0 * T], W["wkT0"], q0bd[:, :], stop=False)
            one(B[1][0:KA, 0:H0 * T], W["e_mask"], one_at["e_mask"], start=False).then_inc(S["qq0_ps"], 1)
            pe.wait_ge(S["qq0_sb"], 1)
            for n in range(2 * len(SB0)):
                k, (s, w) = n // len(SB0), SB0[n % len(SB0)]
                if k == 0 and s in ctx_cuts:
                    pe.wait_ge(ld_ctxT[ctx_cuts.index(s)], 16)
                    pe.wait_ge(S["ctx_aug"], ctx_cuts.index(s) + 1)
                    pe.wait_ge(S["mask_row"], ctx_cuts.index(s) + 1)
                if n >= 4:
                    pe.wait_ge(S["scores_evac"], n - 3)
                one(A[:, n % 4, 0:w], qq0[:, k * P:(k + 1) * P], ctxT[:, s:s + w]).then_inc(S["scores_ps"], 1)
            pe.wait_ge(S["ld_m"], 16)
            pe.wait_ge(S["scores_evac"], 2 * len(SB0))
            one(A[0:DC, 2, :], W["wvT0"], W["film_w"]).then_inc(S["wcf_ps"], 1)
            pe.wait_ge(S["s4_pq"], 2)
            for g in range(8):
                last = one(A[:, g // 4, (g % 4) * P:(g % 4 + 1) * P],
                           s4p[:, 16 * g:16 * g + 16, :].rearrange("p d l -> p (d l)"),
                           s4q[:, 16 * g:16 * g + 16, :].rearrange("p d l -> p (d l)"))
            last.then_inc(S["m1_ps"], 1)
            pe.wait_ge(S["ld_dft"], 16)
            pe.wait_ge(S["m1_sb"], 2)
            for ri_ in range(2):
                o = A[0:FREQ, 3, ri_ * D:(ri_ + 1) * D]
                for bb in range(RB):
                    last = one(o, dft_k[:, (bb * 2 + ri_) * FREQ:(bb * 2 + ri_ + 1) * FREQ],
                               m1[:, :, :].rearrange("p g (d b) -> p b (g d)", b=RB)[:, bb, :],
                               start=(bb == 0), stop=(bb == RB - 1 and ri_ == 1))
                if ri_ == 0:
                    last = one(o, one_at["d_skip"][:, 0:FREQ], W["d_skip"], start=False)
            last.then_inc(S["kf_ps"], 1)
            pe.wait_ge(S["rep_ready"], 1)
            one(B[1][0:1, 0:2], onec[:, 0:1], bad[:, :]).then_inc(S["flag_ps"], 1)
            pe.wait_ge(S["sel0_ready"], 2)
            pe.wait_ge(S["ld_ctx"], 16)
            banks = [list(range(b, min(b + 8, NC))) for b in range(0, NC, 8)]

            def values(b):
                pe.wait_ge(S["attnT_sb"], b + 1)
                for c in banks[b]:
                    last = one(B[0][0:DC, 0:T], ctxn[:, c * DC:(c + 1) * DC], attnT[:, c * T:(c + 1) * T],
                               start=(c == 0), stop=(c == NC - 1))
                if b == len(banks) - 1:
                    last.then_inc(S["cT_ps"], 1)

            for c in range(NC):
                s, i = divmod(c, SLICE)
                if i == 0:
                    pe.wait_ge(S["w_ready"], 2 * s + 2)
                b = c // 8
                if c % 8 == 0 and b >= 2:
                    pe.wait_ge(S["attnT_sb"], b - 1)
                for k in range(2):
                    slot = (s % 2) * 2 + k
                    last = one(B[2 + b % 2][:, (c % 8) * T:(c % 8 + 1) * T],
                               probs[:, slot * 896 + i * P:slot * 896 + (i + 1) * P], seln[:, k, :],
                               start=(k == 0), stop=(k == 1))
                if c in (banks[b][-1],) and i == SLICE - 1:
                    last.then_inc(S["attnT_ps"], 1)
                    pe.nop().then_inc(S["slice_used"], 1)
                elif c == banks[b][-1]:
                    last.then_inc(S["attnT_ps"], 1)
                elif i == SLICE - 1:
                    last.then_inc(S["slice_used"], 1)
                if c == banks[b][-1] and b >= 1:
                    values(b - 1)
            values(len(banks) - 1)
            pe.wait_ge(S["film_row"], 1)
            pe.wait_ge(S["flag_ps"], 1)
            pe.wait_ge(S["topk_final"], 1)
            one(B[1][0:T, :], one_at["film_b"][:, 0:T], W["film_1"], stop=False)
            pe.wait_ge(S["cT_sb"], 1)
            pe.wait_ge(S["wcf_sb"], 1)
            one(B[1][0:T, :], cT[:, :], wcf[:, :], start=False).then_inc(S["film_ps"], 1)
            pe.wait_ge(S["xm_ready"], 1)
            for c in range(2):
                last = one(B[2][0:FREQ, c * D:(c + 1) * D], W["dft_x"][:, c * FREQ:(c + 1) * FREQ], xm2[:, :])
            last.then_inc(S["xf_ps"], 1)
            pe.wait_ge(S["prod_ready"], 1)
            yo = B[3][0:T, 0:D]
            one(yo, W["idft"][:, 0:T], pa[:, 0, :], stop=False)
            one(yo, W["idft"][:, T:2 * T], pb[:, 1, :], start=False, stop=False)
            one(yo, W["idft"][:, 2 * T:], pb[:, 0, :], start=False, stop=False)
            one(yo, W["idft"][:, 2 * T:], pa[:, 1, :], start=False).then_inc(S["y_ps"], 1)
            pe.wait_ge(S["h0_ready"], 1)
            nc.tensor.transpose(B[2][:, 0:T], hn[:, :], idT).then_inc(S["hT0_ps"], 1)
            pe.wait_ge(S["hT0_sb"], 1)
            for c in range(4):
                last = one(B[3][:, c * T:(c + 1) * T], W["w1"][:, c * P:(c + 1) * P], hT[:, :])
            last.then_inc(S["up0_ps"], 1)
            one(B[2][0:T, 0:D], one_at["b2"][:, 0:T], W["b2"], stop=False)
            pe.wait_ge(S["gelu0_ready"], 1)
            for c in range(4):
                last = one(B[2][0:T, 0:D], hid0[:, c * T:(c + 1) * T], W["w2"][:, c * D:(c + 1) * D],
                           start=False, stop=(c == 3))
            last.then_inc(S["mlp0_ps"], 1)
            pe.wait_ge(S["u1_ready"], 1)
            one(B[2][:, 0:2 * T], u1[:, :], W["eye_tri"]).then_inc(S["ut_ps"], 1)
            pe.wait_ge(S["ut_sb"], 1)
            one(B[3][0:32, 0:T], W["gw1"], uT[:, 1:T + 1])
            one(B[3][0:32, T:2 * T], W["u_w"], uT[:, 1:T + 1]).then_inc(S["g1_ps"], 1)
            pe.wait_ge(S["ut_sb"], 2)
            one(B[0][0:32, 0:T], W["v_w"], cumT[:, :]).then_inc(S["g1_ps"], 1)
            pe.wait_ge(S["g1_sb"], 1)
            one(B[1][0:32, 0:T], W["gw2"], g1[:, :]).then_inc(S["g2_ps"], 1)
            pe.wait_ge(S["diag_ready"], 3)
            one(B[2][0:T, 0:D], one_at["out_b"][:, 0:T], W["out_b"], stop=False)
            for j in range(3):
                one(B[2][0:T, 0:D], uT[:, j:j + T], diag[:, j, :], start=False, stop=False)
            pe.wait_ge(S["glob_ready"], 1)
            one(B[2][0:T, 0:D], glob[:, :], W["out_w"], start=False).then_inc(S["blk1_ps"], 1)
            pe.wait_ge(S["v_ready"], 1)
            nc.tensor.transpose(B[3][:, 2 * D:2 * D + T], v[:, :], idT).then_inc(S["vT_ps"], 1)
            pe.wait_ge(S["vT_sb"], 1)
            pe.wait_ge(S["ld_l"], 16)
            one(B[3][0:T, 0:8], vT[:, :], W["rgT"], stop=False)
            one(B[3][0:T, 0:8], one_at["rb"][:, 0:T], W["rb"], start=False).then_inc(S["route_ps"], 1)
            pe.wait_ge(S["ld_w1"], 16)

            def moe_up(p):
                if p >= 4:
                    pe.wait_ge(S["moe_pre"], p - 3)
                for i in range(8 if p < 4 else 4):
                    last = one(A[:, p % 4, i * T:(i + 1) * T], moe_w1[:, (8 * p + i) * P:(8 * p + i + 1) * P], vT[:, :])
                last.then_inc(S["moe_up_ps"], 1)

            def moe_down(e):
                pe.wait_ge(S["moe_gelu"], e // 2 + 1)
                y = B[e % 4][0:T, 0:D]
                if e >= 4:
                    pe.wait_ge(S["moe_acc"], e - 3)
                one(y, one_at["moe_b2"][:, 0:T], W["moe_b2"][:, e * D:(e + 1) * D], stop=False)
                for c in range(4):
                    last = one(y, hid[:, (4 * e + c) * T:(4 * e + c + 1) * T], moe_w2[:, (4 * e + c) * D:(4 * e + c + 1) * D],
                               start=False, stop=(c == 3))
                last.then_inc(S["moe_y_ps"], 1)

            pe.wait_ge(S["kf_sb"], 1)
            moe_up(0)
            moe_up(1)
            pe.wait_ge(S["ld_w2"], 16)
            for p in range(5):
                if p + 2 < 5:
                    moe_up(p + 2)
                moe_down(2 * p)
                if p < 4:
                    moe_down(2 * p + 1)
            pe.wait_ge(S["n3_ready"], 1)
            nc.tensor.transpose(B[3][:, 0:T], n3[:, :], idT).then_inc(S["n3T_ps"], 1)
            pe.wait_ge(S["n3T_sb"], 1)
            one(B[3][:, T:2 * T], W["wq1"], n3T[:, :]).then_inc(S["q1_ps"], 1)
            pe.wait_ge(S["q1_bd"], 1)
            for i in range(2):
                one(A[0:KA, i, :], W["wkT1"], qbd[:, 8 * i:8 * i + 8, :].rearrange("p h t -> p (h t)")).then_inc(S["qq1_ps"], 1)
            pe.wait_ge(S["w_ready"], 2 * NSL)
            for b in range(13):
                if b >= 2:
                    pe.wait_ge(S["v1_sb"], b - 1)
                for i, c in enumerate(range(4 * b, min(4 * b + 4, NC))):
                    last = one(B[b % 2][:, i * D:(i + 1) * D], chunk_cols(ctxT, c), W["wv1"])
                last.then_inc(S["v1_ps"], 1)
            pe.wait_ge(S["ctx_bf"], 4)
            pe.wait_ge(S["qq1_bf"], 1)

            def max_tile(n):
                i, (s, w) = n // len(SB0), SB0[n % len(SB0)]
                if n >= 2:
                    pe.wait_ge(S["max_used"], n - 1)
                one(B[2 + n % 2][:, 0:w], qq1b[:, i * P:(i + 1) * P], ctx_bf[:, s:s + w]).then_inc(S["max_ps"], 1)

            def fix_rows(j):
                pe.wait_ge(S["negm1"], j + 1)
                for i in range(2):
                    last = one(B[2][DC:KA, i * P:(i + 1) * P], nm[:, 2 * j + i, :], W["ident"])
                last.then_inc(S["fix_ps"], 1)

            NM = 2 * len(SB0)
            for n in range(NM):
                max_tile(n)
            fix_rows(0)
            pe.wait_ge(S["v1_sb"], 13)
            NG = len(GROUPS)

            def score_group(j, g):
                n = j * NG + g
                if n >= 2:
                    pe.wait_ge(S["p_ready"], n - 1)
                buf = A[:, 2 * (n % 2):2 * (n % 2) + 2, :].rearrange("p a b -> p (a b)")
                for i, c in enumerate(GROUPS[g]):
                    last = one(buf[:, i * SQ * T:(i + 1) * SQ * T], chunk_cols(ctxT, c), qq1[:, j * SQ * T:(j + 1) * SQ * T])
                last.then_inc(S["s1_ps"], 1)

            def value_group(j, g):
                n = j * NG + g
                pe.wait_ge(S["p_ready"], n + 1)
                if g == 0 and j >= 1:
                    pe.wait_ge(S["acc_used"], 2 * j)
                for kind in range(2):
                    for i, c in enumerate(GROUPS[g]):
                        r = c % 4
                        lhsT = v1[:, c * D + 32 * j:c * D + 32 * j + 32] if kind == 0 else onec[:, 0:32]
                        last = one(B[kind][32 * r:32 * r + 32, 0:SQ * T], lhsT,
                                   probs[:, (n % RING) * 1024 + i * SQ * T:(n % RING) * 1024 + (i + 1) * SQ * T],
                                   start=(c < 4), stop=(c + 4 >= NC))
                last.then_inc(S["pv_done"], 1)

            for j in range(NQ):
                pe.wait_ge(S["qq_fixed"], j + 1)
                for g in range(NG):
                    score_group(j, g)
                    if g >= 1:
                        value_group(j, g - 1)
                    if j + 1 < NQ:
                        for n in range(NM * (j + 1) + 2 * g, NM * (j + 1) + 2 * g + 2):
                            max_tile(n)
                value_group(j, NG - 1)
                if j + 1 < NQ:
                    fix_rows(j + 1)
            pe.wait_ge(S["z_part"], 1)
            one(B[2][:, 0:NQ * T], W["sel_r"], om[:, 0, :]).then_inc(S["zt_ps"], 1)
            one(B[3][0:T, 0:D], one_at["bo1"][:, 0:T], W["bo1"], stop=False)
            pe.wait_ge(S["o_ready"], 1)
            for j in range(NQ):
                last = one(B[3][0:T, 0:D], o2[:, j, :], W["wo1"][:, j * D:(j + 1) * D], start=False, stop=(j == NQ - 1))
            last.then_inc(S["y1_ps"], 1)
            cz = W["causal"].unsqueeze(1).to_broadcast([T, 8, T])
            for i in range(2):
                one(A[0:T, i, :].rearrange("p (h k) -> p h k", k=T), idT, cz, stop=False)
            pe.wait_ge(S["n4_ready"], 1)
            nc.tensor.transpose(B[2][:, 0:T], n4[:, :], idT).then_inc(S["n4T_ps"], 1)
            pe.wait_ge(S["n4T_sb"], 1)
            one(B[3][:, 0:T], W["wqT2"], n4T[:, 0, :])
            one(B[3][:, T:2 * T], W["wkT2"], n4T[:, 0, :]).then_inc(S["qk2_ps"], 1)
            one(B[0][:, 0:D], n4T[:, :, :].rearrange("p a t -> p (a t)"), W["wvT2"]).then_inc(S["v2_ps"], 1)
            pe.wait_ge(S["q2_sb"], 1)
            pe.wait_ge(S["k2_bd"], 1)
            for i in range(2):
                last = one(A[0:T, i, :], q2[:, :], kbd[:, 8 * i:8 * i + 8, :].rearrange("p h k -> p (h k)"), start=False)
            last.then_inc(S["s2_ps"], 1)
            pe.wait_ge(S["p2_ready"], 1)
            for p in range(8):
                last = nc.tensor.transpose(A[:, 2, p * T:(p + 1) * T],
                                           p2[:, 2 * p:2 * p + 2, :].rearrange("p h k -> p (h k)"), idT)
            last.then_inc(S["pT_ps"], 1)
            pe.wait_ge(S["pT_sb"], 1)
            pe.wait_ge(S["v2_bd"], 1)
            for p in range(8):
                last = one(B[1][0:T, 16 * p:16 * p + 16], pT[:, p, :], vbd[:, p, :, :].rearrange("p h c -> p (h c)"))
            last.then_inc(S["o2_ps"], 1)
            pe.wait_ge(S["o2_ready"], 1)
            nc.tensor.transpose(B[2][:, 0:T], oo[:, :], idT).then_inc(S["o2T_ps"], 1)
            pe.wait_ge(S["o2T_sb"], 1)
            one(B[3][0:T, 0:D], ooT[:, :], W["woT2"]).then_inc(S["y2_ps"], 1)
            pe.wait_ge(S["u6_ready"], 1)
            nc.tensor.transpose(B[2][:, 0:T], u6[:, :], idT).then_inc(S["u6T_ps"], 1)
            pe.wait_ge(S["u6T_sb"], 1)
            one(B[3][0:T, 0:8], u6T[:, :], W["wr"]).then_inc(S["rt6_ps"], 1)
            pe.wait_ge(S["r6_ready"], 1)
            nc.tensor.transpose(B[2][:, T:2 * T], h6[:, :], idT).then_inc(S["u6T_ps"], 1)
            pe.wait_ge(S["h6_sb"], 1)
            pe.wait_ge(S["ld_gu"], 16)
            for p in range(4):
                for e in (2 * p, 2 * p + 1):
                    for i in range(4):
                        last = one(A[:, p, (e % 2) * 256 + i * T:(e % 2) * 256 + (i + 1) * T],
                                   e_gu[:, (4 * e + i) * P:(4 * e + i + 1) * P], h6e[:, e, :])
                last.then_inc(S["e6_up_ps"], 1)
            pe.wait_ge(S["ld_down"], 16)
            for e in range(8):
                pe.wait_ge(S["e6_gu"], e // 2 + 1)
                y = B[e % 4][0:T, 0:D]
                if e >= 4:
                    pe.wait_ge(S["moe_acc"], 9 + e - 3)
                for c in range(2):
                    last = one(y, gu6[:, e, c, :], e_dn[:, (2 * e + c) * D:(2 * e + c + 1) * D], start=(c == 0), stop=(c == 1))
                last.then_inc(S["e6_y_ps"], 1)


def shape_constants():
    p = np.arange(P)
    t = np.arange(T)
    f = np.arange(FREQ)
    w = {}
    w["ident"] = np.eye(P)
    w["mask_h0"] = (p[:, None] // DH0 == np.arange(H0)) * float(DH0) ** -0.5
    w["mask_h1"] = p[:, None] // DH1 == np.arange(H1)
    w["turn0"] = np.where(p < 64, 0.25, 0.0)[:, None]
    w["sel_t"] = p[:, None] % T == t
    l = (p[:, None] % RA) * RB + np.arange(RB)[None, :]
    ang = 2 * np.pi * l[:, :, None] * f / (2 * T)
    w["dft_k"] = np.stack([np.cos(ang), -np.sin(ang)], 2).reshape(P, -1)
    ang = 2 * np.pi * t[:, None] * f / (2 * T)
    w["dft_x"] = np.stack([np.cos(ang), -np.sin(ang)], 1).reshape(T, -1)
    wt = np.where((f == 0) | (f == T), 1.0, 2.0)[:, None] / (2 * T)
    w["idft"] = np.concatenate([wt * np.cos(ang.T), -wt * np.cos(ang.T), -wt * np.sin(ang.T)], 1)
    w["eye_tri"] = np.concatenate([np.eye(T), t[:, None] <= t], 1)
    w["iota8"] = np.broadcast_to(np.arange(8), (T, 8))
    w["mask_q"] = (p[:, None] % 32) // DH1 == np.arange(SQ)
    w["sel_r"] = p[:, None] % 32 == p % 32
    w["causal"] = np.where(t[:, None] >= t, 0.0, NEG)
    w["mask_p"] = p[:, None] // T == np.arange(2)
    w["e_mask"] = np.arange(KA) == DC
    w["film_1"] = (np.arange(4 * D) // D) % 2 == 0
    return {k: np.ascontiguousarray(a, dtype=np.float32) for k, a in w.items()}


def lay_out(i):
    dup = lambda a: np.concatenate([a, a], 0)
    over = lambda a, n: np.broadcast_to(np.reshape(a, (1, -1)), (n, np.size(a)))
    col = lambda a: np.reshape(a, (-1, 1))
    pad2 = lambda a: np.concatenate([a, np.zeros((a.shape[0], 2), a.dtype)], 1)
    w = shape_constants()
    x0, a0, m0, x1, a1, m1 = ({k[len(s):]: v for k, v in i.items() if k.startswith(s)} for s in
                              ("L0_xattn_", "L0_attn_", "L0_ffn_", "L1_xattn_", "L1_attn_", "L1_ffn_"))
    w["x"] = i["x"][0]
    w["wq0"], w["wkT0"] = x0["Wq"], pad2(x0["Wk"].T)
    for n, k in (("a_re", "A_re"), ("a_im", "A_im"), ("c_re", "C_re"), ("c_im", "C_im")):
        w[n] = dup(x0[k].T)
    w["log_dt"] = over(x0["log_dt"], P)
    w["film_w"] = np.concatenate([x0["W_film_in"], x0["W_film_out"]], 1)
    w["film_b"] = np.concatenate([x0["b_film_in"], x0["b_film_out"]])
    w["wvT0"] = x0["Wv"].T
    for n, k in (("g_in", "g_norm_in"), ("b_in", "b_norm_in"), ("g_out", "g_norm_out"), ("b_out", "b_norm_out")):
        w[n] = over(x0[k], T)
    w["gate"] = over(x0["mod_gate"], P).reshape(P, 1)
    w["g_ffn"], w["b_ffn"] = col(x0["g_ffn"]), col(x0["b_ffn"])
    w["w1"], w["b1T"] = x0["W1"], x0["b1"].reshape(4, P).T
    w["w2"] = x0["W2"].reshape(4, P, D).transpose(1, 0, 2).reshape(P, -1)
    w["b2"], w["d_skip"] = x0["b2"], x0["D_skip"]
    w["gw1"], w["gb1"], w["gw2"], w["gb2"] = a0["gate_w1"], col(a0["gate_b1"]), a0["gate_w2"], col(a0["gate_b2"])
    w["u_w"], w["v_w"], w["conv"], w["out_w"], w["out_b"] = a0["U_w"], a0["V_w"], a0["conv_w"], a0["out_w"], a0["out_b"]
    w["rgT"], w["rb"] = m0["gate_w"].T, m0["gate_b"]
    w["moe_b1T"] = np.concatenate([m0["b1"].reshape(32, P), m0["sb1"].reshape(4, P)], 0).T
    w["moe_b2"] = np.concatenate([m0["b2"].reshape(-1), m0["sb2"]])
    w["wq1"], w["bq1"] = x1["Wq"], col(x1["bq"])
    w["wkT1"] = np.concatenate([x1["Wk"].T, np.zeros((D, 1), np.float32), col(x1["bk"])], 1)
    w["wv1"] = np.concatenate([x1["Wv"], np.zeros((1, D), np.float32), x1["bv"][None]], 0)
    w["scale1"] = over(x1["scale"], P).reshape(P, 1)
    w["wo1"] = np.concatenate([np.tile(x1["Wo"][32 * j:32 * j + 32], (4, 1)) for j in range(NQ)], 1)
    w["bo1"] = x1["bo"]
    for n, k in (("wqT2", "q"), ("wkT2", "k"), ("wvT2", "v"), ("woT2", "o")):
        w[n] = a1[f"{k}_proj_weight"].T
    w["wr"], w["norm_wT"] = m1["Wr"], m1["norm_w"].T
    out = {}
    for bn, table in BLOBS.items():
        a = np.zeros((P, width(table)), np.float32)
        for n, (r, at, c) in offsets(table).items():
            a[0:r, at:at + c] = w[n]
        out[bn] = a
    out["rows"] = np.zeros((3, ROWS_WIDTH), np.float32)
    for part, table in ROWS.items():
        at = 0
        for n, k in table.items():
            out["rows"][part // 32, at:at + k] = w[n]
            at += k
    out["dft_k"] = w["dft_k"]
    c = i["ctx_768"][0]
    out["ctxT"] = c.T
    out["ctxn"] = c.reshape(NC, P, DC).transpose(1, 0, 2).reshape(P, -1)
    out["gmask"] = i["mask_BxS2_bf1"].view(np.uint8).reshape(1, G)
    out["tmask"] = dup(i["mask_BxS_bf1"].view(np.uint8).reshape(T, 1))
    out["moe_w1"] = np.concatenate([m0["w1"].transpose(1, 0, 2).reshape(D, -1), m0["sw1"]], 1)
    out["moe_w2"] = np.concatenate([m0["w2"].reshape(32, P, D), m0["sw2"].reshape(4, P, D)], 0).transpose(1, 0, 2).reshape(P, -1)
    out["e_gu"] = np.concatenate([m1["Wg"], m1["Wu"]], 2).transpose(1, 0, 2).reshape(D, -1)
    out["e_dn"] = m1["Wd"].reshape(16, P, D).transpose(1, 0, 2).reshape(P, -1)
    return {k: np.ascontiguousarray(a) for k, a in out.items()}


def kernel(**inputs):
    import concourse.bacc as _bacc
    from concourse.bass_utils import run_bass_kernel_spmd as _run

    nc = _bacc.Bacc("TRN2", target_bir_lowering=False, num_devices=1)
    arrays = lay_out({k: np.asarray(a) for k, a in inputs.items()})
    dram = {n: nc.dram_tensor(f"in_{n}", a.shape, mybir.dt.from_np(a.dtype), kind="ExternalInput").ap()
            for n, a in arrays.items()}
    out = nc.dram_tensor("out", (T, D), F32, kind="ExternalOutput").ap()
    perceiver_kernel(nc, dram, out)
    r = _run(nc, [{f"in_{n}": a for n, a in arrays.items()}], core_ids=[0])
    return r.results[0]["out"].reshape(1, T, D)
```

```python
from contextlib import ExitStack

import concourse.bass as bass
import numpy as np
from concourse import mybir

F32 = mybir.dt.float32
BF16 = mybir.dt.bfloat16
U8 = mybir.dt.uint8
I32 = mybir.dt.int32
U32 = mybir.dt.uint32
ALU = mybir.AluOpType
ACT = mybir.ActivationFunctionType
AX_X = mybir.AxisListType.X

T, D, G, DC = 64, 128, 6272, 96
P = 128
NC = G // P
KA = DC + 2
H0, DH0 = 4, 32
H1, DH1 = 16, 8
TOPK = 32
NEG = -1e30
FREQ = T + 1
RA = RB = 8
SQ = 4
PAIR = 2 * 8
STACK = [(0, 0, 0), (16, 1, 0), (32, 2, 0), (64, 0, 1), (80, 1, 1), (97, 0, 2)]
SHIFT_ROW = 96
KS = 97 + PAIR
NQ = H1 // SQ
GROUPS = [list(range(g, min(g + 4, NC))) for g in range(0, NC, 4)]
RING = 4
SLICE = 7
NSL = NC // SLICE
BANK = 512
SB0 = [(s, min(BANK, G - s)) for s in range(0, G, BANK)]
TWO_PI = 6.2831850
ROUND = 1.5 * 2.0 ** 23
K_AT = {"film": (0, 1), "xf": (1, 2), "y": (2, 4), "up": (4, 5), "mlp": (5, 8), "gla": (8, 10), "moe": (10, 13)}
K_LOW = [(3, 2), (4, 4), (5, 4), (6, 9), (None, 13)]
KF_AT = 4
SIN_AT, TURNS_AT = 13, 7
V_GAP = 5
EPS_LN, EPS_RMS = 1e-5, 1e-6

BLOB_A = {"x": (T, D), "ident": (P, P), "wq0": (D, D), "wkT0": (D, KA), "mask_h0": (P, H0)}
BLOB_S = {"a_re": (P, D), "a_im": (P, D), "c_re": (P, D), "c_im": (P, D), "log_dt": (P, D),
          "turn0": (P, 1), "mask_h1": (P, H1)}
BLOB_M = {"film_w": (D, 4 * D), "wvT0": (D, DC), "g_in": (T, D), "b_in": (T, D), "g_out": (T, D), "b_out": (T, D),
          "gate": (P, 1), "sel_t": (P, T), "dft_x": (T, 2 * FREQ),
          "idft": (FREQ, 3 * T), "g_ffn": (D, 1), "b_ffn": (D, 1), "w1": (D, 4 * D), "b1T": (P, 4),
          "w2": (P, 4 * D), "eye_tri": (T, 2 * T), "gw1": (D, 32), "gb1": (32, 1), "gw2": (32, 32), "gb2": (32, 1),
          "u_w": (D, 32), "v_w": (D, 32), "conv": (D, 3), "out_w": (32, D), "iota8": (T, 8)}
BLOB_L = {"rgT": (D, 8), "moe_b1T": (P, 36),
          "wq1": (D, D), "wkT1": (D, KA), "wv1": (KA, D), "bq1": (D, 1), "scale1": (P, 1), "wo1": (P, NQ * D),
          "mask_q": (P, SQ), "sel_r": (P, P), "wk1": (KA, D), "rep_q": (P, KS), "wqT2": (D, D), "wkT2": (D, D), "wvT2": (D, D), "woT2": (D, D),
          "causal": (T, T), "mask_p": (P, 2), "wr": (D, 8), "norm_wT": (D, 8)}
BLOBS = {"blob_a": BLOB_A, "blob_s": BLOB_S, "blob_m": BLOB_M, "blob_l": BLOB_L}
ROWS = {0: {"film_b": 4 * D, "film_1": 4 * D, "out_b": D}, 32: {"moe_b2": 9 * D},
        64: {"e_mask": KA, "b2": D, "d_skip": D, "rb": 8, "bo1": D}}
ROWS_WIDTH = max(sum(t.values()) for t in ROWS.values())


def width(table):
    return sum(c for _, c in table.values())


def offsets(table):
    at, out = 0, {}
    for name, (r, c) in table.items():
        out[name] = (r, at, c)
        at += c
    return out


SEMAPHORES = """
tokT_ps tokT_sb norm_ready k_ps k_hi k_rest k_mid k_low qst_ps qst_hi qst_rest qst_mid qst_sb
ld_a ld_s ld_m ld_l ld_rows ld_gmask ld_tmask ld_ctx ld_dft ld_w1 ld_w2 ld_gu ld_down out_stored
var_ready rstd_ready mask_row
q0_ps q0_bd qq0_ps qq0_sb
scores_ps scores_evac scores_max cand_ready negm0 z0_ready sel0_ready
rep_ready flag_ps topk_final e_ready w_ready slice_used attnT_ps attnT_sb
dt_ready s4_theta s4_turns s4_sin s4_mag s4_pq m1_ps m1_sb kf_ps kf_sb
s4_z s4_cs s4_inv s4_gain
wcf_ps wcf_sb film_row c2T_ps c2T_sb c2_ps c2_sb cT_ps cT_sb film_ps xm_ready xf_ps prod_ready y_ps up0_ps
pre0_ready gelu0_ready mlp0_ps 
ut_ps ut_sb g1_ps g1_sb g2_ps g2_pre g2_exp glob_ready diag_ready blk1_ps 
route_ps route_pre route_exp moe_up_ps moe_pre moe_gelu moe_y_ps moe_acc 
q1_ps q1_bd qq1_ps qq1_bf ctx_bf v1_ps v1_sb
max_ps max_used negm1 fix_ps qq_fixed s1_ps p_ready pv_done acc_used z_part zt_ps o_ready y1_ps 
qk2_ps q2_sb k2_bd v2_ps v2_bd s2_ps d2_ready p2_ready pT_ps pT_sb o2_ps o2_ready y2_ps 
r6_ready h6_sb rt6_ps l6_max l6_exp e6_up_ps e6_gelu e6_gu e6_y_ps out_ready
vec_chain vec_slow pool_chain act_chain 
""".split()


def stack_count(j):
    return 16 * 2 * (2 + len(STACK) * (j // 2 + 1))


def perceiver_kernel(nc, dram, out):
    with ExitStack() as ctx:
        def sb(name, shape, dt=F32):
            return ctx.enter_context(nc.sbuf_tensor(name, shape, dt))

        S = {n: ctx.enter_context(nc.semaphore(n)) for n in SEMAPHORES}
        stack_ld = [ctx.enter_context(nc.semaphore(f"stack_ld{i}")) for i in range(2)]
        ld_ctxT = [ctx.enter_context(nc.semaphore(f"ld_ctxT{i}")) for i in range(4)]

        blob = {n: sb(n, [P, width(t)]) for n, t in BLOBS.items()}
        W = {}
        for bn, table in BLOBS.items():
            for n, (r, at, c) in offsets(table).items():
                W[n] = blob[bn][0:r, at:at + c]
        rows = sb("rows", [65, ROWS_WIDTH])
        for part, table in ROWS.items():
            at = 0
            for n, c in table.items():
                W[n] = rows[part:part + 1, at:at + c]
                at += c
        onec = sb("onec", [P, 4 * T])
        one_at = {n: onec[part:part + 1, :] for part, table in ROWS.items() for n in table}
        ctxT = sb("ctxT", [P, G])
        ctxn = sb("ctxn", [P, NC * DC])
        scores = sb("scores", [P, 2 * G])
        late = sb("late", [P, G])
        probs = sb("probs", [P, RING * 1024])
        moe_w1 = sb("moe_w1", [P, 9 * 4 * D])
        moe_w2 = ctxn[:, 0:9 * 4 * D]
        ctx_bf = late[0:KA, NC * T:NC * T + G // 2].bitcast(BF16)
        v1 = scores[:, 0:NC * D]
        kpart = [scores[:, G:G + G // 2].bitcast(BF16), scores[:, G + G // 2:2 * G].bitcast(BF16),
                 late[:, 0:G // 2].bitcast(BF16)]
        kstack = [t[0:KS, a:a + G // 2].bitcast(BF16) for t, a in ((ctxn, 0), (moe_w1, 0), (ctxT, 0), (ctxT, G // 2))]
        e_gu = scores[:, G:G + 8 * 4 * P]
        e_dn = scores[:, G + 8 * 4 * P:G + 8 * 4 * P + 8 * 2 * D]
        gmask = ctxn[DC:DC + 1, 0:G // 4].bitcast(U8)
        tmask = sb("tmask", [P, 1], U8)

        st = sb("st", [T, 6]); mv = sb("mv", [T, 2]); ve = sb("ve", [T, 1]); rstd = sb("rstd", [T, 1])
        mhalf = sb("mhalf", [P, 1])
        x0 = sb("x0", [T, D]); xin = sb("xin", [T, D]); x0T = sb("x0T", [P, T])
        qq0 = sb("qq0", [KA, H0 * T])
        top = sb("top", [P, 2, TOPK])
        cnt = sb("cnt", [P, 4]); bad = sb("bad", [P, 2]); flag = sb("flag", [1, 2], I32)
        flagf = sb("flagf", [1, 4])
        negm0 = sb("negm0", [P, 2]); ztop = sb("ztop", [P, 2, TOPK]); z0 = sb("z0", [P, 2]); rz0 = sb("rz0", [P, 2])
        tmf = sb("tmf", [P, 1]); seln = sb("seln", [P, T]); rho = sb("rho", [P, 1])
        c2T = sb("c2T", [DC, P]); c2 = sb("c2", [P, DC])
        cT = sb("cT", [DC, T]); wcf = probs[0:DC, RING * 1024 - 4 * D:RING * 1024]; 
        xm = sb("xm", [T, D]); xm2 = sb("xm2", [T, D]); kf = sb("kf", [FREQ, 2, D])
        sh = sb("sh", [T, D]); xt = sb("xt", [T, D]); hn = sb("hn", [T, D]); hT = sb("hT", [P, T])
        xt2 = sb("xt2", [T, D]); nt = sb("nt", [T, D])
        nt2 = sb("nt2", [T, D]); x1 = sb("x1", [T, D]); uT = sb("uT", [P, T + 2])
        cumT = sb("cumT", [P, T]); g1 = sb("g1", [32, T]); ub = sb("ub", [32, T]); us = sb("us", [32, T])
        ge2 = sb("ge2", [32, T]); ge3 = sb("ge3", [32, T]); ge4 = sb("ge4", [32, T]); gpre = sb("gpre", [32, T]); rpre = sb("rpre", [T, 8])
        glob = sb("glob", [32, T]); diag = sb("diag", [P, 3, P]); x2 = sb("x2", [T, D])
        vT = sb("vT", [P, T]); rex = sb("rex", [T, 8]); rex1 = sb("rex1", [T, 8]); rsc = sb("rsc", [T, 8])
        r8 = sb("r8", [T, 8]); ri = sb("ri", [T, 8], U32); rif = sb("rif", [T, 2]); rs = sb("rs", [T, 4])
        rw = sb("rw", [T, 2]); oh = sb("oh", [T, 8]); oh2 = sb("oh2", [T, 8]); comb = sb("comb", [T, 8])
        acc = sb("acc", [T, 4, D])
        n3T = sb("n3T", [P, T]); q1 = sb("q1", [P, T])
        mx = sb("mx", [P, 8, len(SB0)]); nm = sb("nm", [P, 8, 2])
        x4 = sb("x4", [T, D]); n4T = sb("n4T", [P, 2, T])
        q2 = sb("q2", [P, T]); m2 = sb("m2", [T, H1]); s2 = sb("s2", [T, H1])
        i2 = sb("i2", [T, H1]); ooT = sb("ooT", [P, T])
        x5 = sb("x5", [T, D]); u6 = sb("u6", [T, D]); u6T = sb("u6T", [P, T])
        h6T = sb("h6T", [P, T]); m8 = sb("m8", [T, 8]); nm6 = sb("nm6", [T, 1])
        ex6 = sb("ex6", [T, 8]); z6 = sb("z6", [T, 1]); iz6 = sb("iz6", [T, 1]); w6 = sb("w6", [T, 2]); sw6 = sb("sw6", [T, 1])
        msq = sb("msq", [T, 2])

        def carve(region, parts, *shapes):
            at, tiles = 0, []
            for shape in shapes:
                n = int(np.prod(shape))
                t = region[0:parts, at:at + n]
                if len(shape) > 1:
                    names = "abc"[:len(shape)]
                    t = t.rearrange(f"p ({' '.join(names)}) -> p {' '.join(names)}",
                                    **{k: v for k, v in zip(names, shape)})
                tiles.append(t)
                at += n
            assert at <= region.shape[1], (at, region.shape)
            return tiles

        mid = sb("mid", [P, 2 * 2 * NC * 8])
        cand, cwork = carve(mid, P, (2, NC * 8), (2, NC * 8))
        s4p, s4q, g4, _, ge = carve(moe_w1, P, (D, RA), (D, RB), (16, D), (16,), (NC * 8,))
        m1, dft_k = carve(moe_w1[:, D * (RA + RB):], P, (8, D), (RB * 2 * FREQ,))
        attnT, = carve(mid, P, (3, BANK))
        turns, kint = carve(late, P, (24, D), (24, D))
        mags, smore = carve(probs, P, (16, D), (5, D))
        sdt, sar, sth, stt_, q0bd = carve(scores[:, 2 * G - 6 * D:2 * G], P, (D,), (D,), (D,), (D,), (H0 * T,))
        pre0, hid0, pab = carve(mid, P, (4 * T,), (4 * T,), (4 * D,))
        pa = pab[0:FREQ, 0:2 * D].rearrange("p (c d) -> p c d", c=2)
        pb = pab[0:FREQ, 2 * D:4 * D].rearrange("p (c d) -> p c d", c=2)
        y1 = xm
        pre, = carve(mid, P, (2, BANK))
        hid, krest = carve(probs, P, (9 * 4 * T,), (2, BANK))
        qbd, om = carve(ctxn[:, G // 2:], P, (H1, T), (2, SQ * T))
        qq1b_all, qst_all = carve(moe_w1[:, G // 2:], P, (H1 * T // 2,), (H1 * T // 2,))
        qrest, = carve(mid, P, (H1 * T,))
        qq1b, qst = qq1b_all[0:KA, :].bitcast(BF16), qst_all[0:KS, :].bitcast(BF16)
        o1, z1, zi, o2 = carve(mid, P, (NQ, T), (NQ, T), (NQ, T), (NQ, T))
        kbd, d2_all, p2_all, pT = carve(probs, P, (H1, T), (H1, T), (H1, T), (8, T))
        d2, p2 = d2_all[0:T], p2_all[0:T]
        vbd, = carve(mid[:, 4 * NQ * T:], P, (8, 2, 8))
        h6e, gl6, gu6 = carve(late, P, (8, T), (8, 2, T), (8, 2, T))
        u1 = v = n3 = n4 = hn
        h6, oo = nt2, nt2

        A = ctx.enter_context(nc.psum_tensor("A", [P, 4, BANK], F32))
        B = [ctx.enter_context(nc.psum_tensor(f"B{i}", [P, BANK], F32)) for i in range(4)]
        block = ctx.enter_context(nc.Block())

        attn_bank = [B[2], B[3], A[:, 0, :], A[:, 1, :]]

        def chunk_cols(t, c):
            return t[:, c * P:(c + 1) * P]

        ctx_cuts = [0, 3 * BANK, 6 * BANK, 9 * BANK, G]

        @block.sync
        def _(sp):
            sp.dma_start(blob["blob_a"][:, :], dram["blob_a"]).then_inc(S["ld_a"], 16)
            sp.dma_start(gmask, dram["gmask"]).then_inc(S["ld_gmask"], 16)
            sp.dma_start(blob["blob_s"][:, :], dram["blob_s"]).then_inc(S["ld_s"], 16)
            for part, table in ROWS.items():
                n = sum(table.values())
                sp.dma_start(rows[part:part + 1, 0:n], dram["rows"][part // 32:part // 32 + 1, 0:n]).then_inc(S["ld_rows"], 16)
            for i in range(4):
                a, b = ctx_cuts[i], ctx_cuts[i + 1]
                sp.dma_start(ctxT[0:KA, a:b], dram["ctxT"][:, a:b]).then_inc(ld_ctxT[i], 16)
            sp.dma_start(tmask[:, :], dram["tmask"]).then_inc(S["ld_tmask"], 16)
            sp.dma_start(blob["blob_m"][:, :], dram["blob_m"]).then_inc(S["ld_m"], 16)
            sp.dma_start(blob["blob_l"][:, :], dram["blob_l"]).then_inc(S["ld_l"], 16)
            sp.wait_ge(S["mask_row"], 4)
            sp.dma_start(ctxn[:, :], dram["ctxn"]).then_inc(S["ld_ctx"], 16)
            sp.wait_ge(S["s4_pq"], 2)
            sp.dma_start(dft_k, dram["dft_k"]).then_inc(S["ld_dft"], 16)
            sp.wait_ge(S["kf_ps"], 1)
            sp.wait_ge(S["rep_ready"], 1)
            sp.dma_start(moe_w1[:, :], dram["moe_w1"]).then_inc(S["ld_w1"], 16)
            sp.wait_ge(S["cT_ps"], 1)
            sp.dma_start(moe_w2, dram["moe_w2"]).then_inc(S["ld_w2"], 16)
            for m in range(H1 // 2):
                j = m // 2
                if m == 0:
                    sp.wait_ge(S["moe_y_ps"], 9)
                    sp.wait_ge(S["k_low"], len(SB0))
                elif m == 2:
                    sp.wait_ge(S["v1_ps"], len(SB0))
                    sp.wait_ge(S["ctx_bf"], 4)
                elif m % 2 == 0:
                    sp.wait_ge(S["s1_ps"], len(GROUPS) * (j - 1))
                slot = kstack[m % 4]
                if m < 4:
                    sp.dma_start(slot[48:64, :], dram["fill"][0:16, :].bitcast(BF16)).then_inc(stack_ld[j % 2], 16)
                    sp.dma_start(slot[SHIFT_ROW:SHIFT_ROW + 1, :], dram["fill"][16:17, :].bitcast(BF16)).then_inc(stack_ld[j % 2], 16)
                for row, kp, _ in STACK:
                    sp.dma_start(slot[row:row + PAIR, :], kpart[kp][PAIR * m:PAIR * (m + 1), :]).then_inc(stack_ld[j % 2], 16)
            sp.wait_ge(stack_ld[0], stack_count(2))
            sp.wait_ge(stack_ld[1], stack_count(3))
            sp.dma_start(e_gu, dram["e_gu"]).then_inc(S["ld_gu"], 16)
            sp.dma_start(e_dn, dram["e_dn"]).then_inc(S["ld_down"], 16)
            sp.wait_ge(S["out_ready"], 1)
            sp.dma_start(out, acc[:, 3, :]).then_inc(S["out_stored"], 16)
            sp.wait_ge(S["out_stored"], 16)

        @block.gpsimd
        def _(pool):
            chain = [0]

            def link(ins):
                chain[0] += 1
                ins.then_inc(S["pool_chain"], 1)
                pool.wait_ge(S["pool_chain"], chain[0])

            def rsqrt(n):
                pool.wait_ge(S["var_ready"], n)
                nc.gpsimd.tensor_tensor(rstd[:, :], ve[:, :], mhalf[0:T, :], ALU.pow).then_inc(S["rstd_ready"], 1)
                pool.wait_ge(S["rstd_ready"], n)

            link(nc.gpsimd.memset(mhalf[:, :], -0.5))
            rsqrt(1)
            tt = nc.gpsimd.tensor_tensor
            pool.wait_ge(S["dt_ready"], 1)
            pool.wait_ge(S["ld_s"], 16)
            tt(sar[:, :], sdt[:, :], W["a_re"], ALU.mult).then_inc(S["s4_theta"], 1)
            link(tt(sth[:, :], sdt[:, :], W["a_im"], ALU.mult))
            link(nc.gpsimd.tensor_scalar(stt_[:, :], sth[:, :], 1.0 / (2.0 * np.pi), 0.0, ALU.mult, ALU.add))
            for l in range(8):
                nc.gpsimd.tensor_scalar(turns[:, l, :], stt_[:, :], float(RB * l), 0.25, ALU.mult, ALU.add)
                nc.gpsimd.tensor_scalar(turns[:, 8 + l, :], stt_[:, :], float(RB * l), 0.0, ALU.mult, ALU.add)
                last = nc.gpsimd.tensor_scalar(turns[:, 16 + l, :], stt_[:, :], float(l), W["turn0"], ALU.mult, ALU.add)
            last.then_inc(S["s4_turns"], 1)
            rsqrt(2)
            link(tt(g4[:, 0, :], W["a_re"], W["a_re"], ALU.mult))
            link(tt(g4[:, 1, :], W["a_im"], W["a_im"], ALU.mult))
            tt(g4[:, 2, :], g4[:, 0, :], g4[:, 1, :], ALU.add).then_inc(S["s4_inv"], 1)
            pool.wait_ge(S["s4_z"], 1)
            link(tt(g4[:, 4, :], smore[:, 0, :], smore[:, 1, :], ALU.mult))
            link(tt(g4[:, 5, :], smore[:, 0, :], smore[:, 2, :], ALU.mult))
            link(nc.gpsimd.tensor_scalar(g4[:, 6, :], g4[:, 4, :], 1.0, -1.0, ALU.mult, ALU.add))
            link(tt(g4[:, 7, :], g4[:, 6, :], W["a_re"], ALU.mult))
            link(tt(g4[:, 8, :], g4[:, 5, :], W["a_im"], ALU.mult))
            link(tt(g4[:, 9, :], g4[:, 7, :], g4[:, 8, :], ALU.add))
            link(tt(g4[:, 7, :], g4[:, 5, :], W["a_re"], ALU.mult))
            link(tt(g4[:, 8, :], g4[:, 6, :], W["a_im"], ALU.mult))
            link(tt(g4[:, 10, :], g4[:, 7, :], g4[:, 8, :], ALU.subtract))
            pool.wait_ge(S["s4_gain"], 1)
            link(tt(g4[:, 9, :], g4[:, 9, :], g4[:, 3, :], ALU.mult))
            link(tt(g4[:, 10, :], g4[:, 10, :], g4[:, 3, :], ALU.mult))
            link(tt(g4[:, 11, :], W["c_re"], g4[:, 9, :], ALU.mult))
            link(tt(g4[:, 12, :], W["c_im"], g4[:, 10, :], ALU.mult))
            link(tt(g4[:, 13, :], g4[:, 11, :], g4[:, 12, :], ALU.subtract))
            link(tt(g4[:, 11, :], W["c_re"], g4[:, 10, :], ALU.mult))
            link(tt(g4[:, 12, :], W["c_im"], g4[:, 9, :], ALU.mult))
            link(tt(g4[:, 14, :], g4[:, 11, :], g4[:, 12, :], ALU.add))
            nc.gpsimd.tensor_scalar(g4[0:64, 0, :], g4[0:64, 13, :], 2.0, 0.0, ALU.mult, ALU.add)
            nc.gpsimd.tensor_scalar(g4[64:128, 0, :], g4[64:128, 14, :], -2.0, 0.0, ALU.mult, ALU.add)
            nc.gpsimd.tensor_scalar(g4[0:64, 1, :], g4[0:64, 14, :], -2.0, 0.0, ALU.mult, ALU.add)
            link(nc.gpsimd.tensor_scalar(g4[64:128, 1, :], g4[64:128, 13, :], -2.0, 0.0, ALU.mult, ALU.add))
            pool.wait_ge(S["s4_sin"], 1)
            pool.wait_ge(S["s4_mag"], 1)
            al = g4[:, 0:1, :].to_broadcast([P, 8, D])
            be = g4[:, 1:2, :].to_broadcast([P, 8, D])
            link(tt(kint[:, 0:8, :], turns[:, 0:8, :], al, ALU.mult))
            link(tt(kint[:, 8:16, :], turns[:, 8:16, :], be, ALU.mult))
            link(tt(kint[:, 16:24, :], kint[:, 0:8, :], kint[:, 8:16, :], ALU.add))
            tt(s4p[:, :, :].rearrange("p d l -> p l d"), kint[:, 16:24, :], mags[:, 0:8, :], ALU.mult).then_inc(S["s4_pq"], 1)
            tt(s4q[:, :, :].rearrange("p d l -> p l d"), turns[:, 16:24, :], mags[:, 8:16, :], ALU.mult).then_inc(S["s4_pq"], 1)
            pool.wait_ge(S["ld_m"], 16)
            for j in range(3):
                nc.gpsimd.tensor_scalar(diag[:, j, :], W["ident"], W["conv"][:, j:j + 1], 0.0, ALU.mult, ALU.add)\
                    .then_inc(S["diag_ready"], 1)
            pool.wait_ge(S["s4_pq"], 2)
            pool.wait_ge(S["topk_final"], 1)
            pool.wait_ge(S["mask_row"], 4)
            for i in range(4):
                a, b = ctx_cuts[i], ctx_cuts[i + 1]
                pool.wait_ge(ld_ctxT[i], 16)
                nc.gpsimd.tensor_scalar(ctx_bf[:, a:b], ctxT[0:KA, a:b], 1.0, 0.0, ALU.mult, ALU.add).then_inc(S["ctx_bf"], 1)

            def key_low(n):
                s, w = SB0[n]
                pool.wait_ge(S["k_mid"], n + 1)
                tt(kpart[2][:, s:s + w], krest[:, n % 2, 0:w], kpart[1][:, s:s + w], ALU.subtract).then_inc(S["k_low"], 1)

            done = 0
            for norm, keys in K_LOW:
                for n in range(done, keys):
                    key_low(n)
                if norm:
                    rsqrt(norm)
                done = keys
            for n in range(7, 11):
                rsqrt(n)

        @block.scalar
        def _(act):
            chain = [0]

            def link(ins):
                chain[0] += 1
                ins.then_inc(S["act_chain"], 1)
                act.wait_ge(S["act_chain"], chain[0])

            A_ = nc.scalar.activation
            act.wait_ge(S["ld_s"], 16)
            A_(sdt[:, :], W["log_dt"], ACT.Exp).then_inc(S["dt_ready"], 1)
            act.wait_ge(S["ld_gmask"], 16)
            for i in range(4):
                a, b = ctx_cuts[i], ctx_cuts[i + 1]
                act.wait_ge(ld_ctxT[i], 16)
                A_(ctxT[DC:DC + 1, a:b], gmask[:, a:b], ACT.Copy, scale=-NEG, bias=NEG).then_inc(S["mask_row"], 1)
            act.wait_ge(S["s4_theta"], 1)
            for l in range(8):
                A_(mags[:, l, :], sar[:, :], ACT.Exp, scale=float(RB * l))
                last = A_(mags[:, 8 + l, :], sar[:, :], ACT.Exp, scale=float(l))
            link(A_(smore[:, 0, :], sar[:, :], ACT.Exp))
            last.then_inc(S["s4_mag"], 1)

            def evac_scores(n):
                k, (s, w) = n // len(SB0), SB0[n % len(SB0)]
                act.wait_ge(S["scores_ps"], n + 1)
                A_(scores[:, k * G + s:k * G + s + w], A[:, n % 4, 0:w], ACT.Copy).then_inc(S["scores_evac"], 1)

            for n in range(SIN_AT):
                evac_scores(n)
            act.wait_ge(S["s4_cs"], 1)
            A_(turns[:, :, :], kint[:, :, :], ACT.Sin, scale=TWO_PI).then_inc(S["s4_sin"], 1)
            A_(smore[:, 1:3, :], smore[:, 3:5, :], ACT.Sin, scale=TWO_PI).then_inc(S["s4_z"], 1)
            for n in range(SIN_AT, 2 * len(SB0)):
                evac_scores(n)
            for k in range(2):
                act.wait_ge(S["negm0"], k + 1)
                A_(ztop[:, k, :], top[:, k, :], ACT.Exp, bias=negm0[:, k:k + 1], accum_out=z0[:, k:k + 1])\
                    .then_inc(S["z0_ready"], 1)
            act.wait_ge(S["s4_pq"], 2)
            act.wait_ge(S["topk_final"], 1)

            def evac_attn(b):
                act.wait_ge(S["attnT_ps"], b + 1)
                n = len(GROUPS[b]) * P
                A_(attnT[:, b % 3, 0:n], attn_bank[b % 4][:, 0:n], ACT.Copy).then_inc(S["attnT_sb"], 1)

            done = 0
            for s in range(NSL):
                for k in range(2):
                    if s >= 2:
                        act.wait_ge(S["slice_used"], s - 1)
                    slot = (s % 2) * 2 + k
                    A_(probs[:, slot * 896:(slot + 1) * 896],
                       scores[:, k * G + s * 896:k * G + (s + 1) * 896], ACT.Exp, bias=negm0[:, k:k + 1])\
                        .then_inc(S["e_ready"], 1)
                while s >= 1 and GROUPS[done][-1] < SLICE * (s - 1):
                    evac_attn(done)
                    done += 1
            while done < len(GROUPS):
                evac_attn(done)
                done += 1

            def key_hi(n):
                s, w = SB0[n]
                act.wait_ge(S["k_ps"], n + 1)
                A_(kpart[0][:, s:s + w], A[:, n % 4, 0:w], ACT.Copy).then_inc(S["k_hi"], 1)

            def key_mid(n):
                s, w = SB0[n]
                act.wait_ge(S["k_rest"], n + 1)
                A_(kpart[1][:, s:s + w], krest[:, n % 2, 0:w], ACT.Copy).then_inc(S["k_mid"], 1)

            def keys_at(place):
                for n in range(*K_AT[place]):
                    key_hi(n)
                    if n > 0:
                        key_mid(n - 1)

            for place in ("film", "xf", "y"):
                keys_at(place)
            act.wait_ge(S["pre0_ready"], 1)
            A_(hid0[:, :], pre0[:, :], ACT.Gelu).then_inc(S["gelu0_ready"], 1)
            for place in ("up", "mlp"):
                keys_at(place)
            act.wait_ge(S["g2_pre"], 1)
            A_(ge2[:, :], gpre[:, :], ACT.Exp, scale=-1.0).then_inc(S["g2_exp"], 1)
            keys_at("gla")
            act.wait_ge(S["route_pre"], 1)
            A_(rex[:, :], rpre[:, :], ACT.Exp, scale=-1.0).then_inc(S["route_exp"], 1)
            keys_at("moe")
            key_mid(len(SB0) - 1)
            for p in range(5):
                act.wait_ge(S["moe_pre"], p + 1)
                w = BANK if p < 4 else 256
                A_(hid[:, p * BANK:p * BANK + w], pre[:, p % 2, 0:w], ACT.Gelu).then_inc(S["moe_gelu"], 1)
            for b in range(V_GAP):
                act.wait_ge(S["v1_ps"], b + 1)
                A_(v1[:, 4 * b * D:(4 * b + 4) * D], B[b % 2][:, :], ACT.Copy).then_inc(S["v1_sb"], 1)
            act.wait_ge(S["qst_ps"], 1)
            A_(qst[:, :], A[0:KS, 2:4, :].rearrange("p a b -> p (a b)"), ACT.Copy).then_inc(S["qst_hi"], 1)
            act.wait_ge(S["qst_rest"], 1)
            A_(qst[64:KS, :], qrest[64:KS, :], ACT.Copy).then_inc(S["qst_mid"], 1)
            for b in range(V_GAP, 13):
                act.wait_ge(S["v1_ps"], b + 1)
                n = min(4, NC - 4 * b)
                A_(v1[:, 4 * b * D:(4 * b + n) * D], B[b % 2][:, 0:n * D], ACT.Copy).then_inc(S["v1_sb"], 1)
            n = 0
            for j in range(NQ):
                for g, cs in enumerate(GROUPS):
                    act.wait_ge(S["s1_ps"], n + 1)
                    if n >= RING:
                        act.wait_ge(S["pv_done"], n - RING + 1)
                    w = len(cs) * SQ * T
                    A_(probs[:, (n % RING) * 1024:(n % RING) * 1024 + w],
                       A[:, 2 * (n % 2):2 * (n % 2) + 2, :].rearrange("p a b -> p (a b)")[:, 0:w],
                       ACT.Exp).then_inc(S["p_ready"], 1)
                    n += 1
            act.wait_ge(S["d2_ready"], 1)
            A_(p2[:, :, :], d2[:, :, :], ACT.Exp).then_inc(S["p2_ready"], 1)
            act.wait_ge(S["l6_max"], 1)
            A_(ex6[:, :], B[3][0:T, 0:8], ACT.Exp, bias=nm6[:, :], accum_out=z6[:, :]).then_inc(S["l6_exp"], 1)
            for p in range(4):
                act.wait_ge(S["e6_up_ps"], p + 1)
                src = A[:, p, :].rearrange("p (e u f t) -> p e u f t", e=2, u=2, f=2)[:, :, 0, :, :]
                A_(gl6[:, 2 * p:2 * p + 2, :, :], src, ACT.Gelu).then_inc(S["e6_gelu"], 1)

        @block.vector
        def _(dve):
            chain = [0]
            norm = [0]
            V = nc.vector

            def link(ins):
                chain[0] += 1
                ins.then_inc(S["vec_chain"], 1)
                dve.wait_ge(S["vec_chain"], chain[0])

            def layernorm(dst, src, signal=None, meanwhile=None):
                link(V.bn_stats(st[:, :], src))
                link(V.bn_aggr(mv[:, :], st[:, :]))
                V.tensor_scalar_add(ve[:, :], mv[:, 1:2], EPS_LN).then_inc(S["var_ready"], 1)
                norm[0] += 1
                if meanwhile:
                    meanwhile()
                dve.wait_ge(S["rstd_ready"], norm[0])
                ins = V.tensor_scalar(dst, src, mv[:, 0:1], rstd[:, :], ALU.subtract, ALU.mult)
                if signal:
                    ins.then_inc(signal, 1)
                else:
                    link(ins)

            link(V.memset(onec[:, :], 1.0))
            link(V.memset(nm[:, :, :], 0.0))
            link(V.memset(uT[:, :], 0.0))
            dve.wait_ge(S["ld_a"], 16)
            layernorm(x0[:, :], W["x"])
            V.tensor_scalar_add(nt[:, :], x0[:, :], 0.0).then_inc(S["norm_ready"], 1)
            dve.wait_ge(S["tokT_ps"], 1)
            V.tensor_copy(x0T[:, :], B[0][:, 0:T]).then_inc(S["tokT_sb"], 1)
            dve.wait_ge(S["q0_ps"], 1)
            V.tensor_tensor(q0bd[:, :].rearrange("p (h t) -> p h t", h=H0),
                            B[0][:, T:2 * T].unsqueeze(1).to_broadcast([P, H0, T]),
                            W["mask_h0"].unsqueeze(2).to_broadcast([P, H0, T]), ALU.mult).then_inc(S["q0_bd"], 1)
            dve.wait_ge(S["qq0_ps"], 1)
            V.tensor_copy(qq0[:, :], B[1][0:KA, 0:H0 * T]).then_inc(S["qq0_sb"], 1)
            layernorm(xin[:, :], x0[:, :])

            def chunk_max(n):
                k, (s, w) = n // len(SB0), SB0[n % len(SB0)]
                dve.wait_ge(S["scores_evac"], n + 1)
                for i in range(w // P):
                    c = s // P + i
                    last = V.max(cand[:, k, 8 * c:8 * c + 8], scores[:, k * G + c * P:k * G + (c + 1) * P])
                last.then_inc(S["scores_max"], 1)

            def top32(k):
                dve.wait_ge(S["scores_max"], len(SB0) * (k + 1))
                for r in range(TOPK // 8):
                    src = cand if r == 0 else cwork
                    link(V.max(top[:, k, 8 * r:8 * r + 8], src[:, k, :]))
                    if r < TOPK // 8 - 1:
                        link(V.match_replace(cwork[:, k, :], top[:, k, 8 * r:8 * r + 8], src[:, k, :], -3e38))
                tau = top[:, k, TOPK - 1:TOPK]
                V.tensor_scalar(negm0[:, k:k + 1], top[:, k, 0:1], -1.0, None, ALU.mult).then_inc(S["cand_ready"], 1)
                link(V.tensor_scalar(ge[:, :], cand[:, k, :], tau, None, ALU.is_ge))
                link(V.tensor_reduce(cnt[:, 2 * k:2 * k + 1], ge[:, :], AX_X, ALU.add))
                link(V.tensor_reduce(cnt[:, 2 * k + 1:2 * k + 2],
                                     ge[:, :].rearrange("p (c e) -> p c e", e=8)[:, :, 7], AX_X, ALU.add))
                link(V.tensor_tensor(bad[:, k:k + 1], cnt[:, 2 * k:2 * k + 1], cnt[:, 2 * k + 1:2 * k + 2], ALU.add))

            for n in range(len(SB0)):
                chunk_max(n)
                if n == TURNS_AT - 1:
                    dve.wait_ge(S["s4_turns"], 1)
                    link(V.tensor_scalar(kint, turns, ROUND, ROUND, ALU.add, ALU.subtract))
                    link(V.tensor_tensor(kint, turns, kint, ALU.subtract))
                    link(V.tensor_scalar(g4[:, 14, :], stt_[:, :], 1.0, 0.25, ALU.mult, ALU.add))
                    link(V.tensor_scalar(g4[:, 13, :], g4[:, 14, :], ROUND, ROUND, ALU.add, ALU.subtract))
                    link(V.tensor_scalar(g4[:, 12, :], stt_[:, :], ROUND, ROUND, ALU.add, ALU.subtract))
                    link(V.tensor_tensor(smore[:, 3, :], g4[:, 14, :], g4[:, 13, :], ALU.subtract))
                    V.tensor_tensor(smore[:, 4, :], stt_[:, :], g4[:, 12, :], ALU.subtract).then_inc(S["s4_cs"], 1)
                    dve.wait_ge(S["s4_inv"], 1)
                    V.reciprocal(g4[:, 3, :], g4[:, 2, :]).then_inc(S["s4_gain"], 1)
            top32(0)
            for n in range(len(SB0), 2 * len(SB0)):
                chunk_max(n)
            top32(1)
            dve.wait_ge(S["scores_evac"], 2 * len(SB0))
            V.tensor_scalar_add(rz0[:, :], bad[:, :], 0.0).then_inc(S["rep_ready"], 1)
            dve.wait_ge(S["flag_ps"], 1)
            link(V.tensor_reduce(flagf[:, 0:1], B[1][0:1, 0:2], AX_X, ALU.add))
            link(V.tensor_scalar(flag[:, 0:1], flagf[:, 0:1], float(2 * P * TOPK), None, ALU.is_gt))
            need_exact = dve.value_load(flag[0:1, 0:1], min_val=0, max_val=1)
            with dve.If(need_exact > 0):
                step = [0]

                def slow(ins):
                    step[0] += 1
                    ins.then_inc(S["vec_slow"], 1)
                    dve.wait_ge(S["vec_slow"], step[0])

                dve.wait_ge(S["s4_pq"], 2)
                for k in range(2):
                    tile = scores[:, k * G:(k + 1) * G]
                    for r in range(TOPK // 8):
                        src = tile if r == 0 else late[:, :]
                        slow(V.max(top[:, k, 8 * r:8 * r + 8], src))
                        slow(V.match_replace(late[:, :], top[:, k, 8 * r:8 * r + 8], src, -3e38))
                    slow(V.tensor_scalar(late[:, :], late[:, :], -2e38, -1e36, ALU.is_gt, ALU.mult))
                    slow(V.tensor_tensor(tile, tile, late[:, :], ALU.add))
            V.tensor_scalar(negm0[:, :], top[:, :, 0], -1.0, None, ALU.mult).then_inc(S["topk_final"], 1)
            dve.wait_ge(S["topk_final"], 1)
            V.tensor_scalar(rz0[:, :], top[:, :, 0], -1.0, None, ALU.mult).then_inc(S["negm0"], 2)
            dve.wait_ge(S["ld_tmask"], 16)
            link(V.tensor_copy(tmf[:, :], tmask[:, :]))
            dve.wait_ge(S["z0_ready"], 2)
            link(V.reciprocal(rz0[:, :], z0[:, :]))
            link(V.tensor_tensor(rho[:, :], z0[:, 1:2], rz0[:, 0:1], ALU.mult))
            link(V.tensor_scalar(rz0[:, :], rz0[:, :], tmf[:, :], 1.0 / H0, ALU.mult, ALU.mult))
            dve.wait_ge(S["ld_m"], 16)
            V.tensor_scalar(seln[:, :], W["sel_t"], rz0[:, 1:2], None, ALU.mult).then_inc(S["sel0_ready"], 1)
            for s in range(NSL):
                e = [probs[:, ((s % 2) * 2 + k) * 896:((s % 2) * 2 + k + 1) * 896] for k in range(2)]
                for k in range(2):
                    dve.wait_ge(S["e_ready"], 2 * s + k + 1)
                    last = V.scalar_tensor_tensor(e[k], scores[:, k * G + s * 896:k * G + (s + 1) * 896],
                                                  top[:, k, TOPK - 1:TOPK], e[k], ALU.is_ge, ALU.mult)
                link(last)
                V.scalar_tensor_tensor(e[0], e[0], rho[:, :], e[1], ALU.mult, ALU.add).then_inc(S["w_ready"], 1)
                if s == 0:
                    dve.wait_ge(S["m1_ps"], 1)
                    for q in range(2):
                        V.tensor_tensor(m1[:, 4 * q:4 * q + 4, :].rearrange("p g (d b) -> p (g d) b", b=RB),
                                        A[:, q, :].rearrange("p (g d b) -> p (g d) b", g=4, b=RB),
                                        W["mask_h1"].unsqueeze(1).unsqueeze(3).to_broadcast([P, 4, H1, RB])
                                        .rearrange("p g d b -> p g d b"), ALU.mult).then_inc(S["m1_sb"], 1)
                if s == KF_AT:
                    dve.wait_ge(S["kf_ps"], 1)
                    V.tensor_copy(kf[:, :, :], A[0:FREQ, 3, 0:2 * D].rearrange("p (c d) -> p c d", c=2))\
                        .then_inc(S["kf_sb"], 1)
                if s == 2:
                    dve.wait_ge(S["wcf_ps"], 1)
                    V.tensor_scalar(wcf[:, :], A[0:DC, 2, :], W["gate"][0:DC, :], None, ALU.mult).then_inc(S["wcf_sb"], 1)
                    dve.wait_ge(S["ld_rows"], 16 * len(ROWS))
                    V.scalar_tensor_tensor(W["film_1"], W["film_b"], W["gate"][0:1, :], W["film_1"],
                                           ALU.mult, ALU.add).then_inc(S["film_row"], 1)
                    link(V.tensor_tensor(xin[:, :], xin[:, :], W["g_in"], ALU.mult))
                    link(V.tensor_tensor(xin[:, :], xin[:, :], W["b_in"], ALU.add))

            def key_rest(place):
                for n in range(*K_AT[place]):
                    s, w = SB0[n]
                    dve.wait_ge(S["k_hi"], n + 1)
                    if n >= 2:
                        dve.wait_ge(S["k_low"], n - 1)
                    V.tensor_tensor(krest[:, n % 2, 0:w], A[:, n % 4, 0:w], kpart[0][:, s:s + w], ALU.subtract)\
                        .then_inc(S["k_rest"], 1)

            dve.wait_ge(S["c2T_ps"], 1)
            V.tensor_copy(c2T[:, :], B[0][0:DC, 0:P]).then_inc(S["c2T_sb"], 1)
            dve.wait_ge(S["c2_ps"], 1)
            V.tensor_copy(c2[:, :], B[1][:, 0:DC]).then_inc(S["c2_sb"], 1)
            dve.wait_ge(S["cT_ps"], 1)
            V.tensor_copy(cT[:, :], B[0][0:DC, P:P + T]).then_inc(S["cT_sb"], 1)
            dve.wait_ge(S["film_ps"], 1)
            link(V.tensor_tensor(xm[:, :], xin[:, :], B[1][0:T, 0:D], ALU.mult))
            V.tensor_tensor(xm2[:, :], xm[:, :], B[1][0:T, D:2 * D], ALU.add).then_inc(S["xm_ready"], 1)
            link(V.tensor_tensor(sh[:, :], x0[:, :], B[1][0:T, 3 * D:4 * D], ALU.add))
            key_rest("film")
            dve.wait_ge(S["xf_ps"], 1)
            xf = B[2][0:FREQ, 0:2 * D].rearrange("p (c d) -> p c d", c=2)
            dve.wait_ge(S["kf_sb"], 1)
            V.tensor_tensor(pa[:, :, :], xf, kf[:, 0:1, :].to_broadcast([FREQ, 2, D]), ALU.mult)
            V.tensor_tensor(pb[:, :, :], xf, kf[:, 1:2, :].to_broadcast([FREQ, 2, D]), ALU.mult).then_inc(S["prod_ready"], 1)
            key_rest("xf")
            dve.wait_ge(S["y_ps"], 1)
            link(V.tensor_copy(y1[:, :], B[3][0:T, 0:D]))
            link(V.tensor_tensor(y1[:, :], y1[:, :], B[1][0:T, 2 * D:3 * D], ALU.mult))
            link(V.tensor_tensor(xt[:, :], y1[:, :], sh[:, :], ALU.add))
            layernorm(hn[:, :], xt[:, :], S["norm_ready"])
            key_rest("y")
            dve.wait_ge(S["tokT_ps"], 2)
            V.tensor_scalar(hT[:, :], B[2][:, 0:T], W["g_ffn"], W["b_ffn"], ALU.mult, ALU.add).then_inc(S["tokT_sb"], 1)
            dve.wait_ge(S["up0_ps"], 1)
            V.tensor_tensor(pre0[:, :].rearrange("p (c t) -> p c t", c=4), B[3][:, 0:4 * T].rearrange("p (c t) -> p c t", c=4),
                            W["b1T"].unsqueeze(2).to_broadcast([P, 4, T]), ALU.add).then_inc(S["pre0_ready"], 1)
            key_rest("up")
            dve.wait_ge(S["mlp0_ps"], 1)
            link(V.tensor_tensor(xt2[:, :], xt[:, :], B[2][0:T, 0:D], ALU.add))
            layernorm(nt[:, :], xt2[:, :])
            link(V.tensor_tensor(nt2[:, :], nt[:, :], W["g_out"], ALU.mult))
            link(V.tensor_tensor(nt[:, :], nt2[:, :], W["b_out"], ALU.add))
            link(V.tensor_tensor(x1[:, :], nt[:, :], W["x"], ALU.add))
            layernorm(u1[:, :], x1[:, :], S["norm_ready"])
            key_rest("mlp")
            dve.wait_ge(S["ut_ps"], 1)
            V.tensor_copy(uT[:, 1:T + 1], B[2][:, 0:T]).then_inc(S["ut_sb"], 1)
            V.tensor_copy(cumT[:, :], B[2][:, T:2 * T]).then_inc(S["ut_sb"], 1)
            dve.wait_ge(S["g1_ps"], 1)
            V.tensor_scalar(g1[:, :], B[3][0:32, 0:T], W["gb1"], 0.0, ALU.add, ALU.max).then_inc(S["g1_sb"], 1)
            link(V.tensor_copy(ub[:, :], B[3][0:32, T:2 * T]))
            dve.wait_ge(S["g1_ps"], 2)
            link(V.tensor_tensor(us[:, :], ub[:, :], B[0][0:32, 0:T], ALU.mult))
            dve.wait_ge(S["g2_ps"], 1)
            V.tensor_scalar(gpre[:, :], B[1][0:32, 0:T], W["gb2"], -87.0, ALU.add, ALU.max).then_inc(S["g2_pre"], 1)
            dve.wait_ge(S["g2_exp"], 1)
            link(V.tensor_scalar_add(ge3[:, :], ge2[:, :], 1.0))
            link(V.reciprocal(ge4[:, :], ge3[:, :]))
            V.tensor_tensor(glob[:, :], us[:, :], ge4[:, :], ALU.mult).then_inc(S["glob_ready"], 1)
            key_rest("gla")
            dve.wait_ge(S["blk1_ps"], 1)
            link(V.tensor_tensor(x2[:, :], x1[:, :], B[2][0:T, 0:D], ALU.add))
            layernorm(v[:, :], x2[:, :], S["norm_ready"])
            dve.wait_ge(S["tokT_ps"], 3)
            V.tensor_copy(vT[:, :], B[3][:, 2 * D:2 * D + T]).then_inc(S["tokT_sb"], 1)
            dve.wait_ge(S["route_ps"], 1)
            V.tensor_scalar(rpre[:, :], B[3][0:T, 0:8], 1.0, -87.0, ALU.mult, ALU.max).then_inc(S["route_pre"], 1)
            dve.wait_ge(S["route_exp"], 1)
            link(V.tensor_scalar_add(rex1[:, :], rex[:, :], 1.0))
            link(V.reciprocal(rsc[:, :], rex1[:, :]))

            def choose_two(p8, r):
                link(V.max(r8[:, :], p8))
                link(V.max_index(ri[:, :], r8[:, :], p8))
                link(V.tensor_copy(rif[:, :], ri[:, 0:2]))
                r()
                link(V.tensor_scalar(oh[:, :], W["iota8"], rif[:, 0:1], rw[:, 0:1], ALU.is_equal, ALU.mult))
                link(V.tensor_scalar(oh2[:, :], W["iota8"], rif[:, 1:2], rw[:, 1:2], ALU.is_equal, ALU.mult))
                link(V.tensor_tensor(comb[:, :], oh[:, :], oh2[:, :], ALU.add))

            def normalised():
                link(V.tensor_tensor(rs[:, 0:1], r8[:, 0:1], r8[:, 1:2], ALU.add))
                link(V.tensor_scalar_add(rs[:, 1:2], rs[:, 0:1], 1e-6))
                link(V.reciprocal(rs[:, 2:3], rs[:, 1:2]))
                link(V.tensor_scalar(rw[:, :], r8[:, 0:2], rs[:, 2:3], None, ALU.mult))

            def moe_pre(p):
                dve.wait_ge(S["moe_up_ps"], p + 1)
                if p >= 2:
                    dve.wait_ge(S["moe_gelu"], p - 1)
                n = 8 if p < 4 else 4
                V.tensor_tensor(pre[:, p % 2, 0:n * T].rearrange("p (c t) -> p c t", t=T),
                                A[:, p % 4, 0:n * T].rearrange("p (c t) -> p c t", t=T),
                                W["moe_b1T"][:, 8 * p:8 * p + n].unsqueeze(2).to_broadcast([P, n, T]),
                                ALU.add).then_inc(S["moe_pre"], 1)

            key_rest("moe")
            dve.wait_ge(S["ld_l"], 16)
            moe_pre(0)
            moe_pre(1)
            choose_two(rsc[:, :], normalised)
            for p in range(2, 5):
                moe_pre(p)
            prev = x2[:, :]
            for e in range(9):
                dve.wait_ge(S["moe_y_ps"], e + 1)
                V.scalar_tensor_tensor(acc[:, e % 2, :], B[e % 4][0:T, 0:D], comb[:, e:e + 1] if e < 8 else 0.1,
                                       prev, ALU.mult, ALU.add).then_inc(S["moe_acc"], 1)
                dve.wait_ge(S["moe_acc"], e + 1)
                prev = acc[:, e % 2, :]
            x3 = acc[:, 2, :]
            link(V.tensor_copy(x3, prev))
            layernorm(n3[:, :], x3, S["norm_ready"])
            dve.wait_ge(S["tokT_ps"], 4)
            V.tensor_copy(n3T[:, :], B[3][:, 0:T]).then_inc(S["tokT_sb"], 1)
            dve.wait_ge(S["q1_ps"], 1)
            link(V.tensor_scalar(q1[:, :], B[3][:, T:2 * T], W["bq1"], W["scale1"], ALU.add, ALU.mult))
            V.tensor_tensor(qbd[:, :, :], q1[:, :].unsqueeze(1).to_broadcast([P, H1, T]),
                            W["mask_h1"].unsqueeze(2).to_broadcast([P, H1, T]), ALU.mult).then_inc(S["q1_bd"], 1)
            dve.wait_ge(S["qq1_ps"], 2)
            V.tensor_copy(qq1b[:, :], A[0:KA, 0:2, :].rearrange("p a b -> p (a b)")).then_inc(S["qq1_bf"], 1)
            dve.wait_ge(S["qst_hi"], 1)
            V.tensor_tensor(qrest[64:KS, :], A[64:KS, 2:4, :].rearrange("p a b -> p (a b)"), qst[64:KS, :],
                            ALU.subtract).then_inc(S["qst_rest"], 1)

            def row_max(n):
                i, (s, w) = n // len(SB0), SB0[n % len(SB0)]
                dve.wait_ge(S["max_ps"], n + 1)
                V.tensor_reduce(mx[:, i, n % len(SB0):n % len(SB0) + 1], B[2 + n % 2][:, 0:w], AX_X, ALU.max)\
                    .then_inc(S["max_used"], 1)

            def shift_quad(j):
                dve.wait_ge(S["max_used"], 2 * len(SB0) * (j + 1))
                V.tensor_reduce(nm[:, 2 * j:2 * j + 2, 0:1], mx[:, 2 * j:2 * j + 2, :], AX_X, ALU.max, negate=True)\
                    .then_inc(S["negm1"], 1)
                dve.wait_ge(S["fix_ps"], j + 1)
                cols = slice(j * SQ * T, (j + 1) * SQ * T)
                V.tensor_copy(qst[SHIFT_ROW:SHIFT_ROW + 1, cols], B[2][SHIFT_ROW:SHIFT_ROW + 1, 0:SQ * T])\
                    .then_inc(S["qq_fixed"], 1)

            NM = 2 * len(SB0)
            for n in range(NM):
                row_max(n)
            dve.wait_ge(S["qst_mid"], 1)
            V.tensor_tensor(qst[SHIFT_ROW:KS, :], qrest[SHIFT_ROW:KS, :], qst[SHIFT_ROW:KS, :], ALU.subtract)\
                .then_inc(S["qst_sb"], 1)
            dve.wait_ge(S["qst_sb"], 1)
            shift_quad(0)
            for j in range(NQ):
                if j + 1 < NQ:
                    for n in range(NM * (j + 1), NM * (j + 2)):
                        row_max(n)
                    shift_quad(j + 1)
                dve.wait_ge(S["pv_done"], len(GROUPS) * (j + 1))
                for i in range(2):
                    V.tensor_tensor(om[:, i, :].rearrange("p (h t) -> p h t", h=SQ),
                                    B[i][:, 0:SQ * T].rearrange("p (h t) -> p h t", h=SQ),
                                    W["mask_q"].unsqueeze(2).to_broadcast([P, SQ, T]), ALU.mult).then_inc(S["acc_used"], 1)
                dve.wait_ge(S["acc_used"], 2 * (j + 1))
                V.tensor_reduce(o1[:, j, :], om[:, 0, :].rearrange("p (h t) -> p t h", h=SQ), AX_X, ALU.add)
                link(V.tensor_reduce(z1[:, j, :], om[:, 1, :].rearrange("p (h t) -> p t h", h=SQ), AX_X, ALU.add))
            V.tensor_scalar_add(om[:, 0, :].rearrange("p (q t) -> p q t", q=NQ), z1[:, :, :], 0.0).then_inc(S["z_part"], 1)
            dve.wait_ge(S["zt_ps"], 1)
            link(V.reciprocal(zi[:, :, :], B[2][:, 0:NQ * T].rearrange("p (q t) -> p q t", q=NQ)))
            V.tensor_tensor(o2[:, :, :], o1[:, :, :], zi[:, :, :], ALU.mult).then_inc(S["o_ready"], 1)
            dve.wait_ge(S["y1_ps"], 1)
            link(V.tensor_tensor(x4[:, :], x3, B[3][0:T, 0:D], ALU.add))
            layernorm(n4[:, :], x4[:, :], S["norm_ready"])
            dve.wait_ge(S["tokT_ps"], 5)
            V.tensor_copy(n4T[:, 0, :], B[2][:, 0:T])
            V.tensor_copy(n4T[:, 1, :], B[2][:, 0:T]).then_inc(S["tokT_sb"], 1)
            dve.wait_ge(S["qk2_ps"], 1)
            V.tensor_scalar(q2[:, :], B[3][:, 0:T], float(DH1) ** -0.5, None, ALU.mult).then_inc(S["q2_sb"], 1)
            V.tensor_tensor(kbd[:, :, :], B[3][:, T:2 * T].unsqueeze(1).to_broadcast([P, H1, T]),
                            W["mask_h1"].unsqueeze(2).to_broadcast([P, H1, T]), ALU.mult).then_inc(S["k2_bd"], 1)
            dve.wait_ge(S["v2_ps"], 1)
            V.tensor_tensor(vbd[:, :, :, :], B[0][:, 0:D].rearrange("p (q h c) -> p q h c", h=2, c=8),
                            W["mask_p"].unsqueeze(1).unsqueeze(3).to_broadcast([P, 8, 2, 8]), ALU.mult).then_inc(S["v2_bd"], 1)
            dve.wait_ge(S["s2_ps"], 1)
            sc2 = A[0:T, 0:2, :].rearrange("p a (h k) -> p (a h) k", k=T)
            link(V.tensor_reduce(m2[:, :], sc2, AX_X, ALU.max))
            V.tensor_tensor(d2[:, :, :], sc2, m2[:, :].unsqueeze(2).to_broadcast([T, H1, T]), ALU.subtract)\
                .then_inc(S["d2_ready"], 1)
            dve.wait_ge(S["p2_ready"], 1)
            link(V.tensor_reduce(s2[:, :], p2[:, :, :], AX_X, ALU.add))
            link(V.reciprocal(i2[:, :], s2[:, :]))
            dve.wait_ge(S["pT_ps"], 1)
            V.tensor_copy(pT[:, :, :], A[:, 2, :].rearrange("p (q t) -> p q t", q=8)).then_inc(S["pT_sb"], 1)
            dve.wait_ge(S["o2_ps"], 1)
            V.tensor_tensor(oo[:, :].rearrange("p (h c) -> p h c", c=8), B[1][0:T, 0:D].rearrange("p (h c) -> p h c", c=8),
                            i2[:, :].unsqueeze(2).to_broadcast([T, H1, 8]), ALU.mult).then_inc(S["o2_ready"], 1)
            dve.wait_ge(S["tokT_ps"], 6)
            V.tensor_copy(ooT[:, :], B[2][:, 0:T]).then_inc(S["tokT_sb"], 1)
            dve.wait_ge(S["y2_ps"], 1)
            link(V.tensor_tensor(x5[:, :], x4[:, :], B[3][0:T, 0:D], ALU.add))
            layernorm(u6[:, :], x5[:, :])
            link(V.bn_stats(st[:, :], u6[:, :]))
            link(V.bn_aggr(mv[:, :], st[:, :]))
            link(V.tensor_tensor(msq[:, 0:1], mv[:, 0:1], mv[:, 0:1], ALU.mult))
            V.scalar_tensor_tensor(ve[:, :], msq[:, 0:1], EPS_RMS, mv[:, 1:2], ALU.add, ALU.add).then_inc(S["var_ready"], 1)
            V.tensor_scalar_add(nt[:, :], u6[:, :], 0.0).then_inc(S["norm_ready"], 1)
            norm[0] += 1
            dve.wait_ge(S["rstd_ready"], norm[0])
            V.tensor_scalar(h6[:, :], u6[:, :], rstd[:, :], None, ALU.mult).then_inc(S["r6_ready"], 1)
            dve.wait_ge(S["tokT_ps"], 7)
            V.tensor_copy(u6T[:, :], B[2][:, 0:T]).then_inc(S["tokT_sb"], 1)
            dve.wait_ge(S["tokT_ps"], 8)
            link(V.tensor_copy(h6T[:, :], B[2][:, T:2 * T]))
            V.tensor_tensor(h6e[:, :, :], h6T[:, :].unsqueeze(1).to_broadcast([P, 8, T]),
                            W["norm_wT"].unsqueeze(2).to_broadcast([P, 8, T]), ALU.mult).then_inc(S["h6_sb"], 1)
            dve.wait_ge(S["rt6_ps"], 1)
            link(V.max(m8[:, :], B[3][0:T, 0:8]))
            V.tensor_scalar(nm6[:, :], m8[:, 0:1], -1.0, None, ALU.mult).then_inc(S["l6_max"], 1)
            dve.wait_ge(S["l6_exp"], 1)
            link(V.reciprocal(iz6[:, :], z6[:, :]))
            link(V.tensor_scalar(rsc[:, :], ex6[:, :], iz6[:, :], None, ALU.mult))

            def plain():
                link(V.tensor_copy(rw[:, :], r8[:, 0:2]))

            choose_two(rsc[:, :], plain)
            link(V.tensor_tensor(sw6[:, :], rw[:, 0:1], rw[:, 1:2], ALU.add))
            link(V.tensor_scalar_add(w6[:, 0:1], sw6[:, :], 1.0))
            link(V.scalar_tensor_tensor(xt[:, :], u6[:, :], w6[:, 0:1], x5[:, :], ALU.mult, ALU.add))
            for p in range(4):
                dve.wait_ge(S["e6_gelu"], p + 1)
                up = A[:, p, :].rearrange("p (e u x) -> p e u x", e=2, u=2)[:, :, 1, :]
                V.tensor_tensor(gu6[:, 2 * p:2 * p + 2, :, :].rearrange("p e f t -> p e (f t)"),
                                gl6[:, 2 * p:2 * p + 2, :, :].rearrange("p e f t -> p e (f t)"), up, ALU.mult)\
                    .then_inc(S["e6_gu"], 1)
            prev = xt[:, :]
            for e in range(8):
                dve.wait_ge(S["e6_y_ps"], e + 1)
                y = B[e % 4][0:T, 0:D]
                nxt = acc[:, e % 2, :] if e < 7 else acc[:, 3, :]
                ins = V.scalar_tensor_tensor(nxt, y, comb[:, e:e + 1], prev, ALU.mult, ALU.add)
                if e < 7:
                    ins.then_inc(S["moe_acc"], 1)
                    dve.wait_ge(S["moe_acc"], 10 + e)
                else:
                    ins.then_inc(S["out_ready"], 1)
                prev = nxt

        @block.tensor
        def _(pe):
            mm = nc.tensor.matmul
            idT = W["ident"][0:T, 0:T]

            def one(out_, lhsT, rhs, start=True, stop=True):
                return mm(out_, lhsT, rhs, start=start, stop=stop)

            pe.wait_ge(S["ld_a"], 16)
            pe.wait_ge(S["norm_ready"], 1)
            nc.tensor.transpose(B[0][:, 0:T], x0[:, :], idT).then_inc(S["tokT_ps"], 1)
            pe.wait_ge(S["tokT_sb"], 1)
            one(B[0][:, T:2 * T], W["wq0"], x0T[:, :]).then_inc(S["q0_ps"], 1)
            pe.wait_ge(S["q0_bd"], 1)
            pe.wait_ge(S["ld_rows"], 16 * len(ROWS))
            one(B[1][0:KA, 0:H0 * T], W["wkT0"], q0bd[:, :], stop=False)
            one(B[1][0:KA, 0:H0 * T], W["e_mask"], one_at["e_mask"], start=False).then_inc(S["qq0_ps"], 1)
            pe.wait_ge(S["qq0_sb"], 1)
            for n in range(2 * len(SB0)):
                k, (s, w) = n // len(SB0), SB0[n % len(SB0)]
                if k == 0 and s in ctx_cuts:
                    pe.wait_ge(ld_ctxT[ctx_cuts.index(s)], 16)
                    pe.wait_ge(S["mask_row"], ctx_cuts.index(s) + 1)
                if n >= 4:
                    pe.wait_ge(S["scores_evac"], n - 3)
                one(A[:, n % 4, 0:w], qq0[:, k * P:(k + 1) * P], ctxT[0:KA, s:s + w]).then_inc(S["scores_ps"], 1)
            pe.wait_ge(S["ld_m"], 16)
            pe.wait_ge(S["scores_evac"], 2 * len(SB0))
            one(A[0:DC, 2, :], W["wvT0"], W["film_w"]).then_inc(S["wcf_ps"], 1)
            pe.wait_ge(S["rep_ready"], 1)
            one(B[1][0:1, 0:2], onec[:, 0:1], bad[:, :]).then_inc(S["flag_ps"], 1)
            pe.wait_ge(S["s4_pq"], 2)
            for g in range(8):
                last = one(A[:, g // 4, (g % 4) * P:(g % 4 + 1) * P],
                           s4p[:, 16 * g:16 * g + 16, :].rearrange("p d l -> p (d l)"),
                           s4q[:, 16 * g:16 * g + 16, :].rearrange("p d l -> p (d l)"))
            last.then_inc(S["m1_ps"], 1)
            def spectrum():
                pe.wait_ge(S["ld_dft"], 16)
                pe.wait_ge(S["m1_sb"], 2)
                for ri_ in range(2):
                    o = A[0:FREQ, 3, ri_ * D:(ri_ + 1) * D]
                    for bb in range(RB):
                        last = one(o, dft_k[:, (bb * 2 + ri_) * FREQ:(bb * 2 + ri_ + 1) * FREQ],
                                   m1[:, :, :].rearrange("p g (d b) -> p b (g d)", b=RB)[:, bb, :],
                                   start=(bb == 0), stop=(bb == RB - 1 and ri_ == 1))
                    if ri_ == 0:
                        last = one(o, one_at["d_skip"][:, 0:FREQ], W["d_skip"], start=False)
                last.then_inc(S["kf_ps"], 1)

            pe.wait_ge(S["ld_ctx"], 16)

            def values(b):
                pe.wait_ge(S["attnT_sb"], b + 1)
                for i, c in enumerate(GROUPS[b]):
                    last = one(B[0][0:DC, 0:P], ctxn[:, c * DC:(c + 1) * DC], attnT[:, b % 3, i * P:(i + 1) * P],
                               start=(c == 0), stop=(c == NC - 1))
                return last

            for b, cs in enumerate(GROUPS):
                if b == 2:
                    pe.wait_ge(S["m1_sb"], 2)
                if b >= 4:
                    pe.wait_ge(S["attnT_sb"], b - 3)
                for i, c in enumerate(cs):
                    s = c // SLICE
                    if c % SLICE == 0:
                        pe.wait_ge(S["w_ready"], s + 1)
                    last = nc.tensor.transpose(attn_bank[b % 4][:, i * P:(i + 1) * P],
                                               probs[:, (s % 2) * 2 * 896 + (c % SLICE) * P:(s % 2) * 2 * 896 + (c % SLICE + 1) * P],
                                               W["ident"])
                    if c == cs[-1]:
                        last.then_inc(S["attnT_ps"], 1)
                    elif c % SLICE == SLICE - 1:
                        last.then_inc(S["slice_used"], 1)
                if b >= 2:
                    last = values(b - 2)
                    if cs[-1] % SLICE == SLICE - 1:
                        last.then_inc(S["slice_used"], 1)
                if b == 3:
                    spectrum()
            values(len(GROUPS) - 2)
            values(len(GROUPS) - 1).then_inc(S["c2T_ps"], 1)
            pe.wait_ge(S["flag_ps"], 1)
            pe.wait_ge(S["topk_final"], 1)
            pe.wait_ge(S["c2T_sb"], 1)
            nc.tensor.transpose(B[1][:, 0:DC], c2T[:, :], W["ident"][0:DC, 0:DC]).then_inc(S["c2_ps"], 1)
            pe.wait_ge(S["c2_sb"], 1)
            pe.wait_ge(S["sel0_ready"], 1)
            one(B[0][0:DC, P:P + T], c2[:, :], seln[:, :]).then_inc(S["cT_ps"], 1)

            def project_keys(place):
                for n in range(*K_AT[place]):
                    s, w = SB0[n]
                    if n >= 4:
                        pe.wait_ge(S["k_rest"], n - 3)
                    one(A[:, n % 4, 0:w], W["wk1"], ctxT[0:KA, s:s + w]).then_inc(S["k_ps"], 1)

            pe.wait_ge(S["kf_sb"], 1)
            pe.wait_ge(S["film_row"], 1)
            pe.wait_ge(S["flag_ps"], 1)
            pe.wait_ge(S["topk_final"], 1)
            one(B[1][0:T, :], one_at["film_b"][:, 0:T], W["film_1"], stop=False)
            pe.wait_ge(S["cT_sb"], 1)
            pe.wait_ge(S["wcf_sb"], 1)
            one(B[1][0:T, :], cT[:, :], wcf[:, :], start=False).then_inc(S["film_ps"], 1)
            pe.wait_ge(S["ld_l"], 16)
            project_keys("film")
            pe.wait_ge(S["xm_ready"], 1)
            for c in range(2):
                last = one(B[2][0:FREQ, c * D:(c + 1) * D], W["dft_x"][:, c * FREQ:(c + 1) * FREQ], xm2[:, :])
            last.then_inc(S["xf_ps"], 1)
            project_keys("xf")
            pe.wait_ge(S["prod_ready"], 1)
            yo = B[3][0:T, 0:D]
            one(yo, W["idft"][:, 0:T], pa[:, 0, :], stop=False)
            one(yo, W["idft"][:, T:2 * T], pb[:, 1, :], start=False, stop=False)
            one(yo, W["idft"][:, 2 * T:], pb[:, 0, :], start=False, stop=False)
            one(yo, W["idft"][:, 2 * T:], pa[:, 1, :], start=False).then_inc(S["y_ps"], 1)
            project_keys("y")
            pe.wait_ge(S["norm_ready"], 2)
            nc.tensor.transpose(B[2][:, 0:T], hn[:, :], idT).then_inc(S["tokT_ps"], 1)
            pe.wait_ge(S["tokT_sb"], 2)
            for c in range(4):
                last = one(B[3][:, c * T:(c + 1) * T], W["w1"][:, c * P:(c + 1) * P], hT[:, :])
            last.then_inc(S["up0_ps"], 1)
            project_keys("up")
            one(B[2][0:T, 0:D], one_at["b2"][:, 0:T], W["b2"], stop=False)
            pe.wait_ge(S["gelu0_ready"], 1)
            for c in range(4):
                last = one(B[2][0:T, 0:D], hid0[:, c * T:(c + 1) * T], W["w2"][:, c * D:(c + 1) * D],
                           start=False, stop=(c == 3))
            last.then_inc(S["mlp0_ps"], 1)
            project_keys("mlp")
            pe.wait_ge(S["norm_ready"], 3)
            one(B[2][:, 0:2 * T], u1[:, :], W["eye_tri"]).then_inc(S["ut_ps"], 1)
            pe.wait_ge(S["ut_sb"], 1)
            one(B[3][0:32, 0:T], W["gw1"], uT[:, 1:T + 1])
            one(B[3][0:32, T:2 * T], W["u_w"], uT[:, 1:T + 1]).then_inc(S["g1_ps"], 1)
            pe.wait_ge(S["ut_sb"], 2)
            one(B[0][0:32, 0:T], W["v_w"], cumT[:, :]).then_inc(S["g1_ps"], 1)
            pe.wait_ge(S["g1_sb"], 1)
            one(B[1][0:32, 0:T], W["gw2"], g1[:, :]).then_inc(S["g2_ps"], 1)
            project_keys("gla")
            pe.wait_ge(S["diag_ready"], 3)
            one(B[2][0:T, 0:D], one_at["out_b"][:, 0:T], W["out_b"], stop=False)
            for j in range(3):
                one(B[2][0:T, 0:D], uT[:, j:j + T], diag[:, j, :], start=False, stop=False)
            pe.wait_ge(S["glob_ready"], 1)
            one(B[2][0:T, 0:D], glob[:, :], W["out_w"], start=False).then_inc(S["blk1_ps"], 1)
            project_keys("moe")
            pe.wait_ge(S["norm_ready"], 4)
            nc.tensor.transpose(B[3][:, 2 * D:2 * D + T], v[:, :], idT).then_inc(S["tokT_ps"], 1)
            pe.wait_ge(S["tokT_sb"], 3)
            pe.wait_ge(S["ld_l"], 16)
            one(B[3][0:T, 0:8], vT[:, :], W["rgT"], stop=False)
            one(B[3][0:T, 0:8], one_at["rb"][:, 0:T], W["rb"], start=False).then_inc(S["route_ps"], 1)
            pe.wait_ge(S["ld_w1"], 16)

            def moe_up(p):
                if p >= 4:
                    pe.wait_ge(S["moe_pre"], p - 3)
                for i in range(8 if p < 4 else 4):
                    last = one(A[:, p % 4, i * T:(i + 1) * T], moe_w1[:, (8 * p + i) * P:(8 * p + i + 1) * P], vT[:, :])
                last.then_inc(S["moe_up_ps"], 1)

            def moe_down(e):
                pe.wait_ge(S["moe_gelu"], e // 2 + 1)
                y = B[e % 4][0:T, 0:D]
                if e >= 4:
                    pe.wait_ge(S["moe_acc"], e - 3)
                one(y, one_at["moe_b2"][:, 0:T], W["moe_b2"][:, e * D:(e + 1) * D], stop=False)
                for c in range(4):
                    last = one(y, hid[:, (4 * e + c) * T:(4 * e + c + 1) * T], moe_w2[:, (4 * e + c) * D:(4 * e + c + 1) * D],
                               start=False, stop=(c == 3))
                last.then_inc(S["moe_y_ps"], 1)

            pe.wait_ge(S["k_rest"], len(SB0))
            moe_up(0)
            moe_up(1)
            pe.wait_ge(S["ld_w2"], 16)
            for p in range(5):
                if p + 2 < 5:
                    moe_up(p + 2)
                moe_down(2 * p)
                if p < 4:
                    moe_down(2 * p + 1)

            def project_values(b):
                if b >= 2:
                    pe.wait_ge(S["v1_sb"], b - 1)
                for i, c in enumerate(range(4 * b, min(4 * b + 4, NC))):
                    last = one(B[b % 2][:, i * D:(i + 1) * D], chunk_cols(ctxT[0:KA, :], c), W["wv1"])
                last.then_inc(S["v1_ps"], 1)

            pe.wait_ge(S["moe_acc"], 9)
            for b in range(V_GAP):
                project_values(b)
            pe.wait_ge(S["norm_ready"], 5)
            nc.tensor.transpose(B[3][:, 0:T], n3[:, :], idT).then_inc(S["tokT_ps"], 1)
            pe.wait_ge(S["tokT_sb"], 4)
            one(B[3][:, T:2 * T], W["wq1"], n3T[:, :]).then_inc(S["q1_ps"], 1)
            pe.wait_ge(S["q1_bd"], 1)
            for i in range(2):
                one(A[0:KA, i, :], W["wkT1"], qbd[:, 8 * i:8 * i + 8, :].rearrange("p h t -> p (h t)")).then_inc(S["qq1_ps"], 1)
            for i in range(2):
                last = one(A[0:KS, 2 + i, :], W["rep_q"], qbd[:, 8 * i:8 * i + 8, :].rearrange("p h t -> p (h t)"))
            last.then_inc(S["qst_ps"], 1)
            pe.wait_ge(S["ctx_bf"], 4)
            pe.wait_ge(S["qq1_bf"], 1)

            def max_tile(n):
                i, (s, w) = n // len(SB0), SB0[n % len(SB0)]
                if n >= 2:
                    pe.wait_ge(S["max_used"], n - 1)
                one(B[2 + n % 2][:, 0:w], qq1b[:, i * P:(i + 1) * P], ctx_bf[:, s:s + w]).then_inc(S["max_ps"], 1)

            def fix_rows(j):
                pe.wait_ge(S["negm1"], j + 1)
                for i in range(2):
                    last = one(B[2][DC:KA, i * P:(i + 1) * P], nm[:, 2 * j + i, :], W["ident"])
                last.then_inc(S["fix_ps"], 1)

            NM = 2 * len(SB0)
            for n in range(NM):
                max_tile(n)
                if n % 3 == 2 and V_GAP + n // 3 < 13:
                    project_values(V_GAP + n // 3)
            fix_rows(0)
            pe.wait_ge(S["v1_sb"], 13)
            NG = len(GROUPS)

            def score_group(j, g):
                n = j * NG + g
                if n >= 2:
                    pe.wait_ge(S["p_ready"], n - 1)
                buf = A[:, 2 * (n % 2):2 * (n % 2) + 2, :].rearrange("p a b -> p (a b)")
                for i, c in enumerate(GROUPS[g]):
                    for m in (2 * j, 2 * j + 1):
                        last = one(buf[:, i * SQ * T + (m % 2) * P:i * SQ * T + (m % 2 + 1) * P],
                                   chunk_cols(kstack[m % 4], c), qst[:, m * P:(m + 1) * P])
                last.then_inc(S["s1_ps"], 1)

            def value_group(j, g):
                n = j * NG + g
                pe.wait_ge(S["p_ready"], n + 1)
                if g == 0 and j >= 1:
                    pe.wait_ge(S["acc_used"], 2 * j)
                for kind in range(2):
                    for i, c in enumerate(GROUPS[g]):
                        r = c % 4
                        lhsT = v1[:, c * D + 32 * j:c * D + 32 * j + 32] if kind == 0 else onec[:, 0:32]
                        last = one(B[kind][32 * r:32 * r + 32, 0:SQ * T], lhsT,
                                   probs[:, (n % RING) * 1024 + i * SQ * T:(n % RING) * 1024 + (i + 1) * SQ * T],
                                   start=(c < 4), stop=(c + 4 >= NC))
                last.then_inc(S["pv_done"], 1)

            for j in range(NQ):
                pe.wait_ge(S["qq_fixed"], j + 1)
                pe.wait_ge(stack_ld[j % 2], stack_count(j))
                for g in range(NG):
                    score_group(j, g)
                    if g >= 1:
                        value_group(j, g - 1)
                    if j + 1 < NQ:
                        for n in range(NM * (j + 1) + 2 * g, NM * (j + 1) + 2 * g + 2):
                            max_tile(n)
                value_group(j, NG - 1)
                if j + 1 < NQ:
                    fix_rows(j + 1)
            pe.wait_ge(S["z_part"], 1)
            one(B[2][:, 0:NQ * T], W["sel_r"], om[:, 0, :]).then_inc(S["zt_ps"], 1)
            one(B[3][0:T, 0:D], one_at["bo1"][:, 0:T], W["bo1"], stop=False)
            pe.wait_ge(S["o_ready"], 1)
            for j in range(NQ):
                last = one(B[3][0:T, 0:D], o2[:, j, :], W["wo1"][:, j * D:(j + 1) * D], start=False, stop=(j == NQ - 1))
            last.then_inc(S["y1_ps"], 1)
            cz = W["causal"].unsqueeze(1).to_broadcast([T, 8, T])
            for i in range(2):
                one(A[0:T, i, :].rearrange("p (h k) -> p h k", k=T), idT, cz, stop=False)
            pe.wait_ge(S["norm_ready"], 6)
            nc.tensor.transpose(B[2][:, 0:T], n4[:, :], idT).then_inc(S["tokT_ps"], 1)
            pe.wait_ge(S["tokT_sb"], 5)
            one(B[3][:, 0:T], W["wqT2"], n4T[:, 0, :])
            one(B[3][:, T:2 * T], W["wkT2"], n4T[:, 0, :]).then_inc(S["qk2_ps"], 1)
            one(B[0][:, 0:D], n4T[:, :, :].rearrange("p a t -> p (a t)"), W["wvT2"]).then_inc(S["v2_ps"], 1)
            pe.wait_ge(S["q2_sb"], 1)
            pe.wait_ge(S["k2_bd"], 1)
            for i in range(2):
                last = one(A[0:T, i, :], q2[:, :], kbd[:, 8 * i:8 * i + 8, :].rearrange("p h k -> p (h k)"), start=False)
            last.then_inc(S["s2_ps"], 1)
            pe.wait_ge(S["p2_ready"], 1)
            for p in range(8):
                last = nc.tensor.transpose(A[:, 2, p * T:(p + 1) * T],
                                           p2[:, 2 * p:2 * p + 2, :].rearrange("p h k -> p (h k)"), idT)
            last.then_inc(S["pT_ps"], 1)
            pe.wait_ge(S["pT_sb"], 1)
            pe.wait_ge(S["v2_bd"], 1)
            for p in range(8):
                last = one(B[1][0:T, 16 * p:16 * p + 16], pT[:, p, :], vbd[:, p, :, :].rearrange("p h c -> p (h c)"))
            last.then_inc(S["o2_ps"], 1)
            pe.wait_ge(S["o2_ready"], 1)
            nc.tensor.transpose(B[2][:, 0:T], oo[:, :], idT).then_inc(S["tokT_ps"], 1)
            pe.wait_ge(S["tokT_sb"], 6)
            one(B[3][0:T, 0:D], ooT[:, :], W["woT2"]).then_inc(S["y2_ps"], 1)
            pe.wait_ge(S["norm_ready"], 7)
            nc.tensor.transpose(B[2][:, 0:T], u6[:, :], idT).then_inc(S["tokT_ps"], 1)
            pe.wait_ge(S["tokT_sb"], 7)
            one(B[3][0:T, 0:8], u6T[:, :], W["wr"]).then_inc(S["rt6_ps"], 1)
            pe.wait_ge(S["r6_ready"], 1)
            nc.tensor.transpose(B[2][:, T:2 * T], h6[:, :], idT).then_inc(S["tokT_ps"], 1)
            pe.wait_ge(S["h6_sb"], 1)
            pe.wait_ge(S["ld_gu"], 16)
            for p in range(4):
                for e in (2 * p, 2 * p + 1):
                    for i in range(4):
                        last = one(A[:, p, (e % 2) * 256 + i * T:(e % 2) * 256 + (i + 1) * T],
                                   e_gu[:, (4 * e + i) * P:(4 * e + i + 1) * P], h6e[:, e, :])
                last.then_inc(S["e6_up_ps"], 1)
            pe.wait_ge(S["ld_down"], 16)
            for e in range(8):
                pe.wait_ge(S["e6_gu"], e // 2 + 1)
                y = B[e % 4][0:T, 0:D]
                if e >= 4:
                    pe.wait_ge(S["moe_acc"], 9 + e - 3)
                for c in range(2):
                    last = one(y, gu6[:, e, c, :], e_dn[:, (2 * e + c) * D:(2 * e + c + 1) * D], start=(c == 0), stop=(c == 1))
                last.then_inc(S["e6_y_ps"], 1)


def shape_constants():
    p = np.arange(P)
    t = np.arange(T)
    f = np.arange(FREQ)
    w = {}
    w["ident"] = np.eye(P)
    w["mask_h0"] = (p[:, None] // DH0 == np.arange(H0)) * float(DH0) ** -0.5
    w["mask_h1"] = p[:, None] // DH1 == np.arange(H1)
    w["turn0"] = np.where(p < 64, 0.25, 0.0)[:, None]
    w["sel_t"] = p[:, None] % T == t
    l = (p[:, None] % RA) * RB + np.arange(RB)[None, :]
    ang = 2 * np.pi * l[:, :, None] * f / (2 * T)
    w["dft_k"] = np.stack([np.cos(ang), -np.sin(ang)], 2).reshape(P, -1)
    ang = 2 * np.pi * t[:, None] * f / (2 * T)
    w["dft_x"] = np.stack([np.cos(ang), -np.sin(ang)], 1).reshape(T, -1)
    wt = np.where((f == 0) | (f == T), 1.0, 2.0)[:, None] / (2 * T)
    w["idft"] = np.concatenate([wt * np.cos(ang.T), -wt * np.cos(ang.T), -wt * np.sin(ang.T)], 1)
    w["eye_tri"] = np.concatenate([np.eye(T), t[:, None] <= t], 1)
    w["iota8"] = np.broadcast_to(np.arange(8), (T, 8))
    w["rep_q"] = np.zeros((P, KS))
    for row, _, _ in STACK:
        w["rep_q"][p, row + p % PAIR] = 1.0
    w["mask_q"] = (p[:, None] % 32) // DH1 == np.arange(SQ)
    w["sel_r"] = p[:, None] % 32 == p % 32
    w["causal"] = np.where(t[:, None] >= t, 0.0, NEG)
    w["mask_p"] = p[:, None] // T == np.arange(2)
    w["e_mask"] = np.arange(KA) == DC
    w["film_1"] = (np.arange(4 * D) // D) % 2 == 0
    return {k: np.ascontiguousarray(a, dtype=np.float32) for k, a in w.items()}


def lay_out(i):
    dup = lambda a: np.concatenate([a, a], 0)
    over = lambda a, n: np.broadcast_to(np.reshape(a, (1, -1)), (n, np.size(a)))
    col = lambda a: np.reshape(a, (-1, 1))
    pad2 = lambda a: np.concatenate([a, np.zeros((a.shape[0], 2), a.dtype)], 1)
    w = shape_constants()
    x0, a0, m0, x1, a1, m1 = ({k[len(s):]: v for k, v in i.items() if k.startswith(s)} for s in
                              ("L0_xattn_", "L0_attn_", "L0_ffn_", "L1_xattn_", "L1_attn_", "L1_ffn_"))
    w["x"] = i["x"][0]
    w["wq0"], w["wkT0"] = x0["Wq"], pad2(x0["Wk"].T)
    for n, k in (("a_re", "A_re"), ("a_im", "A_im"), ("c_re", "C_re"), ("c_im", "C_im")):
        w[n] = dup(x0[k].T)
    w["log_dt"] = over(x0["log_dt"], P)
    w["film_w"] = np.concatenate([x0["W_film_in"], x0["W_film_out"]], 1)
    w["film_b"] = np.concatenate([x0["b_film_in"], x0["b_film_out"]])
    w["wvT0"] = x0["Wv"].T
    for n, k in (("g_in", "g_norm_in"), ("b_in", "b_norm_in"), ("g_out", "g_norm_out"), ("b_out", "b_norm_out")):
        w[n] = over(x0[k], T)
    w["gate"] = over(x0["mod_gate"], P).reshape(P, 1)
    w["g_ffn"], w["b_ffn"] = col(x0["g_ffn"]), col(x0["b_ffn"])
    w["w1"], w["b1T"] = x0["W1"], x0["b1"].reshape(4, P).T
    w["w2"] = x0["W2"].reshape(4, P, D).transpose(1, 0, 2).reshape(P, -1)
    w["b2"], w["d_skip"] = x0["b2"], x0["D_skip"]
    w["gw1"], w["gb1"], w["gw2"], w["gb2"] = a0["gate_w1"], col(a0["gate_b1"]), a0["gate_w2"], col(a0["gate_b2"])
    w["u_w"], w["v_w"], w["conv"], w["out_w"], w["out_b"] = a0["U_w"], a0["V_w"], a0["conv_w"], a0["out_w"], a0["out_b"]
    w["rgT"], w["rb"] = m0["gate_w"].T, m0["gate_b"]
    w["moe_b1T"] = np.concatenate([m0["b1"].reshape(32, P), m0["sb1"].reshape(4, P)], 0).T
    w["moe_b2"] = np.concatenate([m0["b2"].reshape(-1), m0["sb2"]])
    w["wq1"], w["bq1"] = x1["Wq"], col(x1["bq"])
    w["wkT1"] = np.concatenate([x1["Wk"].T, np.zeros((D, 1), np.float32), col(x1["bk"])], 1)
    w["wk1"] = np.concatenate([x1["Wk"], np.zeros((1, D), np.float32), x1["bk"][None]], 0)
    w["wv1"] = np.concatenate([x1["Wv"], np.zeros((1, D), np.float32), x1["bv"][None]], 0)
    w["scale1"] = over(x1["scale"], P).reshape(P, 1)
    w["wo1"] = np.concatenate([np.tile(x1["Wo"][32 * j:32 * j + 32], (4, 1)) for j in range(NQ)], 1)
    w["bo1"] = x1["bo"]
    for n, k in (("wqT2", "q"), ("wkT2", "k"), ("wvT2", "v"), ("woT2", "o")):
        w[n] = a1[f"{k}_proj_weight"].T
    w["wr"], w["norm_wT"] = m1["Wr"], m1["norm_w"].T
    out = {}
    for bn, table in BLOBS.items():
        a = np.zeros((P, width(table)), np.float32)
        for n, (r, at, c) in offsets(table).items():
            a[0:r, at:at + c] = w[n]
        out[bn] = a
    out["rows"] = np.zeros((3, ROWS_WIDTH), np.float32)
    for part, table in ROWS.items():
        at = 0
        for n, k in table.items():
            out["rows"][part // 32, at:at + k] = w[n]
            at += k
    out["dft_k"] = w["dft_k"]
    out["fill"] = np.concatenate([np.zeros((16, G // 2), np.uint32), np.full((1, G // 2), 0x3F803F80, np.uint32)], 0).view(np.float32)
    c = i["ctx_768"][0]
    out["ctxT"] = np.concatenate([c.T, np.zeros((1, G), np.float32), np.ones((1, G), np.float32)], 0)
    out["ctxn"] = c.reshape(NC, P, DC).transpose(1, 0, 2).reshape(P, -1)
    out["gmask"] = i["mask_BxS2_bf1"].view(np.uint8).reshape(1, G)
    out["tmask"] = dup(i["mask_BxS_bf1"].view(np.uint8).reshape(T, 1))
    out["moe_w1"] = np.concatenate([m0["w1"].transpose(1, 0, 2).reshape(D, -1), m0["sw1"]], 1)
    out["moe_w2"] = np.concatenate([m0["w2"].reshape(32, P, D), m0["sw2"].reshape(4, P, D)], 0).transpose(1, 0, 2).reshape(P, -1)
    out["e_gu"] = np.concatenate([m1["Wg"], m1["Wu"]], 2).transpose(1, 0, 2).reshape(D, -1)
    out["e_dn"] = m1["Wd"].reshape(16, P, D).transpose(1, 0, 2).reshape(P, -1)
    return {k: np.ascontiguousarray(a) for k, a in out.items()}


def kernel(**inputs):
    import concourse.bacc as _bacc
    from concourse.bass_utils import run_bass_kernel_spmd as _run

    nc = _bacc.Bacc("TRN2", target_bir_lowering=False, num_devices=1)
    arrays = lay_out({k: np.asarray(a) for k, a in inputs.items()})
    dram = {n: nc.dram_tensor(f"in_{n}", a.shape, mybir.dt.from_np(a.dtype), kind="ExternalInput").ap()
            for n, a in arrays.items()}
    out = nc.dram_tensor("out", (T, D), F32, kind="ExternalOutput").ap()
    perceiver_kernel(nc, dram, out)
    r = _run(nc, [{f"in_{n}": a for n, a in arrays.items()}], core_ids=[0])
    return r.results[0]["out"].reshape(1, T, D)
```

```python
from contextlib import ExitStack

import concourse.bass as bass
import numpy as np
from concourse import mybir

F32 = mybir.dt.float32
BF16 = mybir.dt.bfloat16
U8 = mybir.dt.uint8
I32 = mybir.dt.int32
U32 = mybir.dt.uint32
ALU = mybir.AluOpType
ACT = mybir.ActivationFunctionType
AX_X = mybir.AxisListType.X

T, D, G, DC = 64, 128, 6272, 96
P = 128
NC = G // P
KA = DC + 2
H0, DH0 = 4, 32
H1, DH1 = 16, 8
TOPK = 32
NEG = -1e30
FREQ = T + 1
RA = RB = 8
SQ = 4
PAIR = 2 * 8
STACK = [(0, 0, 0), (16, 1, 0), (32, 2, 0), (64, 0, 1), (80, 1, 1), (97, 0, 2)]
SHIFT_ROW = 96
KS = 97 + PAIR
NQ = H1 // SQ
VQ = SQ * 8 + 1
V_BANKS = [list(range(c, min(c + 3, NC - 4))) for c in range(0, NC - 4, 3)] + [[NC - 4, NC - 3], [NC - 2, NC - 1]]
V_AT = {"route": (0, 0)}
V_EARLY = 0
FILL = {"n3": 2, "q1": 3, "y1": 4, "n4T": 3, "o2": 2, "y2": 8, "u6T": 2, "h6T": 2}
GROUPS = [list(range(g, min(g + 4, NC))) for g in range(0, NC, 4)]
RING = 4
EVAC_LAG = 3
BANK = 512
SB0 = [(s, min(BANK, G - s)) for s in range(0, G, BANK)]
TWO_PI = 6.2831850
ROUND = 1.5 * 2.0 ** 23
K_AT = {"film": (0, 1), "xf": (1, 2), "y": (2, 4), "up": (4, 5), "mlp": (5, 8), "gla": (8, 11), "moe": (11, 13)}
K_LOW = [(3, 2), (4, 4), (5, 4), (6, 9), (None, 13)]
SIN_AT, TURNS_AT = 14, 3
V_GAP = 4
EPS_LN, EPS_RMS = 1e-5, 1e-6

BLOB_A = {"x": (T, D), "ident": (P, P), "wq0": (D, D), "wkT0": (D, KA), "mask_h0": (P, H0)}
BLOB_S = {"a_re": (P, D), "a_im": (P, D), "c_re": (P, D), "c_im": (P, D), "log_dt": (P, D),
          "turn0": (P, 1), "mask_h1": (P, H1)}
BLOB_M = {"film_w": (D, 4 * D), "wvT0": (D, DC), "g_in": (T, D), "b_in": (T, D), "g_out": (T, D), "b_out": (T, D),
          "gate": (P, 1), "sel_t": (P, T), "dft_x": (T, 2 * FREQ),
          "idft": (FREQ, 3 * T), "g_ffn": (D, 1), "b_ffn": (D, 1), "w1": (D, 4 * D), "b1T": (P, 4),
          "w2": (P, 4 * D), "eye_tri": (T, 2 * T), "gw1": (D, 32), "gb1": (32, 1), "gw2": (32, 32), "gb2": (32, 1),
          "u_w": (D, 32), "v_w": (D, 32), "conv": (D, 3), "out_w": (32, D), "iota8": (P, 8)}
BLOB_L = {"rgT": (D, 8), "moe_b1T": (P, 36),
          "wq1": (D, D), "wkT1": (D, KA), "wv1": (KA, NQ * VQ), "bq1": (D, 1), "scale1": (P, 1), "wo1": (P, NQ * D),
          "mask_q": (P, SQ), "mask_z": (P, SQ), "wk1": (KA, D), "rep_q": (P, KS), "wqT2": (D, D), "wkT2": (D, D), "wvT2": (D, D), "woT2": (D, D),
          "causal": (T, T), "mask_p": (P, 2), "wr": (D, 8), "norm_wT": (D, 8)}
BLOBS = {"blob_a": BLOB_A, "blob_s": BLOB_S, "blob_m": BLOB_M, "blob_l": BLOB_L}
ROWS = {0: {"film_b": 4 * D, "film_1": 4 * D, "out_b": D}, 32: {"moe_b2": 9 * D},
        64: {"e_mask": KA, "b2": D, "d_skip": D, "rb": 8, "bo1": D}}
ROWS_WIDTH = max(sum(t.values()) for t in ROWS.values())


def width(table):
    return sum(c for _, c in table.values())


def offsets(table):
    at, out = 0, {}
    for name, (r, c) in table.items():
        out[name] = (r, at, c)
        at += c
    return out


SEMAPHORES = """
tokT_ps tokT_sb norm_ready k_ps k_hi k_rest k_mid k_low qst_ps qst_hi qst_rest qst_mid qst_sb
ld_a ld_s ld_m ld_l ld_rows ld_gmask ld_tmask ld_ctx ld_dft ld_w1 ld_w2 ld_gu ld_down out_stored
ones_ready var_ready rstd_ready mask_row
q0_ps q0_bd qq0_ps qq0_sb
scores_ps scores_evac scores_max cand_ready negm0 z0_ready sel0_ready
rep_ready flag_ps topk_final e_ready w_ready attnT_ps attnT_sb
dt_ready s4_theta s4_turns s4_sin s4_mag s4_pq m1_ps m1_sb kf_ps kf_sb
s4_z s4_cs s4_inv s4_gain
wcf_ps wcf_sb film_row c2T_ps c2T_sb c2_ps c2_sb cT_ps cT_sb film_ps xm_ready xf_ps prod_ready y_ps up0_ps
pre0_ready gelu0_ready mlp0_ps 
ut_ps ut_sb g1_ps g1_sb g2_ps g2_pre g2_exp glob_ready diag_ready blk1_ps 
route_ps route_pre route_exp moe_up_ps moe_raw moe_hT_ps moe_pre moe_gelu moe_y_ps moe_acc x3_ps 
q1_ps q1_bd qq1_ps qq1_bf ctx_bf v1_ps v1_sb
max_ps max_used negm1 fix_ps qq_fixed s1_ps p_ready pv_done acc_used zt_ps o_ready y1_ps 
qk2_ps q2_sb k2_bd v2_ps v2_bd s2_ps d2_ready p2_ready pT_ps pT_sb o2_ps o2_ready y2_ps 
r6_ready h6_sb rt6_ps l6_max l6_exp e6_up_ps e6_gelu e6_gu e6_guT_ps e6_guT_sb e6_y_ps out_ps out_ready
vec_chain vec_slow pool_chain act_chain 
""".split()


def stack_count(j):
    return 16 * 2 * (2 + len(STACK) * (j // 2 + 1))


def perceiver_kernel(nc, dram, out):
    with ExitStack() as ctx:
        def sb(name, shape, dt=F32):
            return ctx.enter_context(nc.sbuf_tensor(name, shape, dt))

        S = {n: ctx.enter_context(nc.semaphore(n)) for n in SEMAPHORES}
        stack_ld = [ctx.enter_context(nc.semaphore(f"stack_ld{i}")) for i in range(2)]
        ld_ctxT = [ctx.enter_context(nc.semaphore(f"ld_ctxT{i}")) for i in range(4)]

        blob = {n: sb(n, [P, width(t)]) for n, t in BLOBS.items()}
        W = {}
        for bn, table in BLOBS.items():
            for n, (r, at, c) in offsets(table).items():
                W[n] = blob[bn][0:r, at:at + c]
        rows = sb("rows", [65, ROWS_WIDTH])
        for part, table in ROWS.items():
            at = 0
            for n, c in table.items():
                W[n] = rows[part:part + 1, at:at + c]
                at += c
        onec = sb("onec", [P, 4 * T])
        ones_bf = onec[:, :].bitcast(BF16)
        one_at = {n: onec[part:part + 1, :] for part, table in ROWS.items() for n in table}
        ctxT = sb("ctxT", [P, G])
        ctxn = sb("ctxn", [P, NC * DC])
        scores = sb("scores", [P, 2 * G])
        late = sb("late", [P, G])
        probs = sb("probs", [P, RING * 1024])
        moe_w1 = sb("moe_w1", [P, 9 * 4 * D])
        moe_w2 = ctxn[:, 0:9 * 4 * D]
        ctx_bf = late[0:KA, NC * T:NC * T + G // 2].bitcast(BF16)
        v1_most = scores[:, 0:G]
        kpart = [scores[:, G:G + G // 2].bitcast(BF16), scores[:, G + G // 2:2 * G].bitcast(BF16),
                 late[:, 0:G // 2].bitcast(BF16)]
        kstack = [t[0:KS, a:a + G // 2].bitcast(BF16) for t, a in ((ctxn, 0), (moe_w1, 0), (ctxT, 0), (ctxT, G // 2))]
        e_gu = scores[:, G:G + 8 * 4 * P]
        e_dn = scores[:, G + 8 * 4 * P:G + 8 * 4 * P + 8 * 2 * D]
        gmask = ctxn[DC:DC + 1, 0:G // 4].bitcast(U8)
        tmask = sb("tmask", [P, 1], U8)

        st = sb("st", [T, 6]); mv = sb("mv", [T, 2]); ve = sb("ve", [T, 1]); rstd = sb("rstd", [T, 1])
        mhalf = sb("mhalf", [P, 1])
        x0 = sb("x0", [T, D]); xin = sb("xin", [T, D]); x0T = sb("x0T", [P, T])
        qq0 = sb("qq0", [KA, H0 * T])
        top = sb("top", [P, 2, TOPK])
        cnt = sb("cnt", [P, 4]); bad = sb("bad", [P, 2]); flag = sb("flag", [1, 2], I32)
        flagf = sb("flagf", [1, 4])
        negm0 = sb("negm0", [P, 2]); ztop = sb("ztop", [P, 2, TOPK]); z0 = sb("z0", [P, 2]); rz0 = sb("rz0", [P, 2])
        tmf = sb("tmf", [P, 1]); seln = sb("seln", [P, T]); rho = sb("rho", [P, 1])
        c2T = sb("c2T", [DC, P]); c2 = sb("c2", [P, DC])
        cT = sb("cT", [DC, T]); 
        xm = sb("xm", [T, D]); xm2 = sb("xm2", [T, D]); kf = sb("kf", [FREQ, 2, D])
        sh = sb("sh", [T, D]); xt = sb("xt", [T, D]); hn = sb("hn", [T, D]); hT = sb("hT", [P, T])
        xt2 = sb("xt2", [T, D]); nt = sb("nt", [T, D])
        nt2 = sb("nt2", [T, D]); x1 = sb("x1", [T, D]); uT = sb("uT", [P, T + 2])
        cumT = sb("cumT", [P, T]); g1 = sb("g1", [32, T]); ub = sb("ub", [32, T]); us = sb("us", [32, T])
        ge2 = sb("ge2", [32, T]); ge3 = sb("ge3", [32, T]); ge4 = sb("ge4", [32, T]); gpre = sb("gpre", [32, T]); rpre = sb("rpre", [P, 8])
        glob = sb("glob", [32, T]); diag = sb("diag", [P, 3, P]); x2w = sb("x2", [P, D])
        x2 = x2w[0:T, :]
        vT = sb("vT", [P, 2, T]); cpair = sb("cpair", [P, 4, 2]); csel = sb("csel", [P, 4]); rex = sb("rex", [P, 8]); rex1 = sb("rex1", [P, 8]); rsc = sb("rsc", [P, 8])
        r8 = sb("r8", [P, 8]); ri = sb("ri", [P, 8], U32); rif = sb("rif", [P, 2]); rs = sb("rs", [P, 4])
        rw = sb("rw", [P, 2]); oh = sb("oh", [P, 8]); oh2 = sb("oh2", [P, 8]); comb = sb("comb", [P, 8])
        acc = sb("acc", [P, 4, D])
        n3T = sb("n3T", [P, T]); q1 = sb("q1", [P, T])
        mx = sb("mx", [P, 8, len(SB0)]); nm = sb("nm", [P, 8, 2])
        x4 = sb("x4", [T, D]); n4T = sb("n4T", [P, 2, T])
        q2 = sb("q2", [P, T]); m2 = sb("m2", [T, H1]); s2 = sb("s2", [T, H1])
        i2 = sb("i2", [T, H1]); ooT = sb("ooT", [P, T])
        x5 = sb("x5", [T, D]); u6 = sb("u6", [T, D]); u6T = sb("u6T", [P, 2, T])
        h6T = sb("h6T", [P, T]); m8 = sb("m8", [P, 8]); nm6 = sb("nm6", [P, 1])
        ex6 = sb("ex6", [P, 8]); z6 = sb("z6", [P, 1]); iz6 = sb("iz6", [P, 1]); w6 = sb("w6", [T, 2]); sw6 = sb("sw6", [T, 1])
        msq = sb("msq", [T, 2])

        def carve(region, parts, *shapes):
            at, tiles = 0, []
            for shape in shapes:
                n = int(np.prod(shape))
                t = region[0:parts, at:at + n]
                if len(shape) > 1:
                    names = "abc"[:len(shape)]
                    t = t.rearrange(f"p ({' '.join(names)}) -> p {' '.join(names)}",
                                    **{k: v for k, v in zip(names, shape)})
                tiles.append(t)
                at += n
            assert at <= region.shape[1], (at, region.shape)
            return tiles

        mid = sb("mid", [P, 2 * 2 * NC * 8])
        cand, cwork = carve(mid, P, (2, NC * 8), (2, NC * 8))
        s4p, s4q, g4, _, ge = carve(moe_w1, P, (D, RA), (D, RB), (16, D), (16,), (NC * 8,))
        m1, dft_k = carve(moe_w1[:, D * (RA + RB):], P, (8, D), (RB * 2 * FREQ,))
        wcf, = carve(late, DC, (4 * D,))
        attnT, = carve(mid, P, (3, BANK))
        turns, kint = carve(late, P, (24, D), (24, D))
        mags, smore = carve(probs, P, (16, D), (5, D))
        sdt, sar, sth, stt_, q0bd = carve(scores[:, 2 * G - 6 * D:2 * G], P, (D,), (D,), (D,), (D,), (H0 * T,))
        pre0, hid0, pab = carve(mid, P, (4 * T,), (4 * T,), (4 * D,))
        pa = pab[0:FREQ, 0:2 * D].rearrange("p (c d) -> p c d", c=2)
        pb = pab[0:FREQ, 2 * D:4 * D].rearrange("p (c d) -> p c d", c=2)
        y1 = xm
        pre, hraw1 = carve(mid, P, (2, BANK), (BANK,))
        hid, krest, hraw0 = carve(probs, P, (9 * 4 * T,), (2, BANK), (BANK,))
        hraw = [hraw0, hraw1]
        qbd, om = carve(ctxn[:, G // 2:], P, (H1, T), (2, SQ * T))
        qq1b_all, qst_all, v1_rest = carve(moe_w1[:, G // 2:], P, (H1 * T // 2,), (H1 * T // 2,), (2 * NQ * VQ,))
        qrest, = carve(mid, P, (H1 * T,))
        qq1b, qst = qq1b_all[0:KA, :].bitcast(BF16), qst_all[0:KS, :].bitcast(BF16)
        o1, z1, zi, o2 = carve(mid, P, (NQ, T), (NQ, T), (NQ, T), (NQ, T))
        kbd, d2_all, p2_all, pT = carve(probs, P, (H1, T), (H1, T), (H1, T), (8, T))
        d2, p2 = d2_all[0:T], p2_all[0:T]
        vbd, = carve(mid[:, 4 * NQ * T:], P, (8, 2, 8))
        h6e, gl6, gu6 = carve(late, P, (8, T), (4, 2 * P), (4, 2 * P))
        guT, = carve(moe_w1, P, (4, 2, P))
        u1 = v = n3 = n4 = hn
        h6, oo = nt2, nt2

        A = ctx.enter_context(nc.psum_tensor("A", [P, 4, BANK], F32))
        B = [ctx.enter_context(nc.psum_tensor(f"B{i}", [P, BANK], F32)) for i in range(4)]
        block = ctx.enter_context(nc.Block())

        attn_bank = [B[2], B[3], A[:, 0, :], A[:, 1, :]]

        def v1_cols(c, at, n):
            t, i = (v1_most, c) if c < NC - 2 else (v1_rest, c - (NC - 2))
            return t[:, i * NQ * VQ + at:i * NQ * VQ + at + n]

        v_bank = [A[:, 2 + b % 2, :] if b < V_EARLY else B[b % 2] for b in range(len(V_BANKS))]

        def chunk_cols(t, c):
            return t[:, c * P:(c + 1) * P]

        ctx_cuts = [0, 3 * BANK, 6 * BANK, 9 * BANK, G]

        @block.sync
        def _(sp):
            sp.dma_start(blob["blob_a"][:, :], dram["blob_a"]).then_inc(S["ld_a"], 16)
            sp.dma_start(gmask, dram["gmask"]).then_inc(S["ld_gmask"], 16)
            sp.dma_start(blob["blob_s"][:, :], dram["blob_s"]).then_inc(S["ld_s"], 16)
            for part, table in ROWS.items():
                n = sum(table.values())
                sp.dma_start(rows[part:part + 1, 0:n], dram["rows"][part // 32:part // 32 + 1, 0:n]).then_inc(S["ld_rows"], 16)
            for i in range(4):
                a, b = ctx_cuts[i], ctx_cuts[i + 1]
                sp.dma_start(ctxT[0:KA, a:b], dram["ctxT"][:, a:b]).then_inc(ld_ctxT[i], 16)
            sp.dma_start(tmask[:, :], dram["tmask"]).then_inc(S["ld_tmask"], 16)
            sp.dma_start(blob["blob_m"][:, :], dram["blob_m"]).then_inc(S["ld_m"], 16)
            sp.dma_start(blob["blob_l"][:, :], dram["blob_l"]).then_inc(S["ld_l"], 16)
            sp.wait_ge(S["mask_row"], 4)
            sp.dma_start(ctxn[:, :], dram["ctxn"]).then_inc(S["ld_ctx"], 16)
            sp.wait_ge(S["s4_pq"], 2)
            sp.dma_start(dft_k, dram["dft_k"]).then_inc(S["ld_dft"], 16)
            sp.wait_ge(S["kf_ps"], 1)
            sp.wait_ge(S["rep_ready"], 1)
            sp.dma_start(moe_w1[:, :], dram["moe_w1"]).then_inc(S["ld_w1"], 16)
            sp.wait_ge(S["cT_ps"], 1)
            sp.dma_start(moe_w2, dram["moe_w2"]).then_inc(S["ld_w2"], 16)
            for m in range(H1 // 2):
                j = m // 2
                if m == 0:
                    sp.wait_ge(S["moe_y_ps"], 5)
                    sp.wait_ge(S["k_low"], len(SB0))
                elif m == 2:
                    sp.wait_ge(S["v1_ps"], len(V_BANKS))
                    sp.wait_ge(S["ctx_bf"], 4)
                elif m % 2 == 0:
                    sp.wait_ge(S["s1_ps"], len(GROUPS) * (j - 1))
                slot = kstack[m % 4]
                if m < 4:
                    sp.dma_start(slot[48:64, :], dram["fill"][0:16, :].bitcast(BF16)).then_inc(stack_ld[j % 2], 16)
                    sp.dma_start(slot[SHIFT_ROW:SHIFT_ROW + 1, :], dram["fill"][16:17, :].bitcast(BF16)).then_inc(stack_ld[j % 2], 16)
                for row, kp, _ in STACK:
                    sp.dma_start(slot[row:row + PAIR, :], kpart[kp][PAIR * m:PAIR * (m + 1), :]).then_inc(stack_ld[j % 2], 16)
            sp.wait_ge(stack_ld[0], stack_count(2))
            sp.wait_ge(stack_ld[1], stack_count(3))
            sp.dma_start(e_gu, dram["e_gu"]).then_inc(S["ld_gu"], 16)
            sp.dma_start(e_dn, dram["e_dn"]).then_inc(S["ld_down"], 16)
            sp.wait_ge(S["out_ready"], 1)
            sp.dma_start(out, acc[0:T, 3, :]).then_inc(S["out_stored"], 16)
            sp.wait_ge(S["out_stored"], 16)

        @block.gpsimd
        def _(pool):
            chain = [0]

            def link(ins):
                chain[0] += 1
                ins.then_inc(S["pool_chain"], 1)
                pool.wait_ge(S["pool_chain"], chain[0])

            def rsqrt(n):
                pool.wait_ge(S["var_ready"], n)
                nc.gpsimd.tensor_tensor(rstd[:, :], ve[:, :], mhalf[0:T, :], ALU.pow).then_inc(S["rstd_ready"], 1)
                pool.wait_ge(S["rstd_ready"], n)

            link(nc.gpsimd.memset(mhalf[:, :], -0.5))
            rsqrt(1)
            tt = nc.gpsimd.tensor_tensor
            pool.wait_ge(S["dt_ready"], 1)
            pool.wait_ge(S["ld_s"], 16)
            tt(sar[:, :], sdt[:, :], W["a_re"], ALU.mult).then_inc(S["s4_theta"], 1)
            link(tt(sth[:, :], sdt[:, :], W["a_im"], ALU.mult))
            link(nc.gpsimd.tensor_scalar(stt_[:, :], sth[:, :], 1.0 / (2.0 * np.pi), 0.0, ALU.mult, ALU.add))
            link(tt(g4[:, 0, :], W["a_re"], W["a_re"], ALU.mult))
            link(tt(g4[:, 1, :], W["a_im"], W["a_im"], ALU.mult))
            tt(g4[:, 2, :], g4[:, 0, :], g4[:, 1, :], ALU.add).then_inc(S["s4_inv"], 1)
            for l in range(8):
                nc.gpsimd.tensor_scalar(turns[:, l, :], stt_[:, :], float(RB * l), 0.25, ALU.mult, ALU.add)
                nc.gpsimd.tensor_scalar(turns[:, 8 + l, :], stt_[:, :], float(RB * l), 0.0, ALU.mult, ALU.add)
                last = nc.gpsimd.tensor_scalar(turns[:, 16 + l, :], stt_[:, :], float(l), W["turn0"], ALU.mult, ALU.add)
            last.then_inc(S["s4_turns"], 1)
            ts = nc.gpsimd.tensor_scalar
            link(ts(g4[:, 14, :], stt_[:, :], 1.0, 0.25, ALU.mult, ALU.add))
            link(ts(g4[:, 13, :], g4[:, 14, :], ROUND, -ROUND, ALU.add, ALU.add))
            link(ts(g4[:, 12, :], stt_[:, :], ROUND, -ROUND, ALU.add, ALU.add))
            link(ts(kint[:, 16:24, :], turns[:, 16:24, :], ROUND, -ROUND, ALU.add, ALU.add))
            link(tt(smore[:, 3, :], g4[:, 14, :], g4[:, 13, :], ALU.subtract))
            link(tt(smore[:, 4, :], stt_[:, :], g4[:, 12, :], ALU.subtract))
            tt(kint[:, 16:24, :], turns[:, 16:24, :], kint[:, 16:24, :], ALU.subtract).then_inc(S["s4_cs"], 1)
            pool.wait_ge(S["s4_z"], 1)
            link(tt(g4[:, 4, :], smore[:, 0, :], smore[:, 1, :], ALU.mult))
            link(tt(g4[:, 5, :], smore[:, 0, :], smore[:, 2, :], ALU.mult))
            link(nc.gpsimd.tensor_scalar(g4[:, 6, :], g4[:, 4, :], 1.0, -1.0, ALU.mult, ALU.add))
            link(tt(g4[:, 7, :], g4[:, 6, :], W["a_re"], ALU.mult))
            link(tt(g4[:, 8, :], g4[:, 5, :], W["a_im"], ALU.mult))
            link(tt(g4[:, 9, :], g4[:, 7, :], g4[:, 8, :], ALU.add))
            link(tt(g4[:, 7, :], g4[:, 5, :], W["a_re"], ALU.mult))
            link(tt(g4[:, 8, :], g4[:, 6, :], W["a_im"], ALU.mult))
            link(tt(g4[:, 10, :], g4[:, 7, :], g4[:, 8, :], ALU.subtract))
            pool.wait_ge(S["s4_gain"], 1)
            link(tt(g4[:, 9, :], g4[:, 9, :], g4[:, 3, :], ALU.mult))
            link(tt(g4[:, 10, :], g4[:, 10, :], g4[:, 3, :], ALU.mult))
            link(tt(g4[:, 11, :], W["c_re"], g4[:, 9, :], ALU.mult))
            link(tt(g4[:, 12, :], W["c_im"], g4[:, 10, :], ALU.mult))
            link(tt(g4[:, 13, :], g4[:, 11, :], g4[:, 12, :], ALU.subtract))
            link(tt(g4[:, 11, :], W["c_re"], g4[:, 10, :], ALU.mult))
            link(tt(g4[:, 12, :], W["c_im"], g4[:, 9, :], ALU.mult))
            link(tt(g4[:, 14, :], g4[:, 11, :], g4[:, 12, :], ALU.add))
            nc.gpsimd.tensor_scalar(g4[0:64, 0, :], g4[0:64, 13, :], 2.0, 0.0, ALU.mult, ALU.add)
            nc.gpsimd.tensor_scalar(g4[64:128, 0, :], g4[64:128, 14, :], -2.0, 0.0, ALU.mult, ALU.add)
            nc.gpsimd.tensor_scalar(g4[0:64, 1, :], g4[0:64, 14, :], -2.0, 0.0, ALU.mult, ALU.add)
            link(nc.gpsimd.tensor_scalar(g4[64:128, 1, :], g4[64:128, 13, :], -2.0, 0.0, ALU.mult, ALU.add))
            pool.wait_ge(S["s4_sin"], 1)
            pool.wait_ge(S["s4_mag"], 8)
            al = g4[:, 0:1, :].to_broadcast([P, 8, D])
            be = g4[:, 1:2, :].to_broadcast([P, 8, D])
            link(tt(kint[:, 0:8, :], turns[:, 0:8, :], al, ALU.mult))
            link(tt(kint[:, 8:16, :], turns[:, 8:16, :], be, ALU.mult))
            link(tt(kint[:, 16:24, :], kint[:, 0:8, :], kint[:, 8:16, :], ALU.add))
            tt(s4p[:, :, :].rearrange("p d l -> p l d"), kint[:, 16:24, :], mags[:, 0:8, :], ALU.mult).then_inc(S["s4_pq"], 1)
            tt(s4q[:, :, :].rearrange("p d l -> p l d"), turns[:, 16:24, :], mags[:, 8:16, :], ALU.mult).then_inc(S["s4_pq"], 1)
            rsqrt(2)
            pool.wait_ge(S["ld_m"], 16)
            for j in range(3):
                nc.gpsimd.tensor_scalar(diag[:, j, :], W["ident"], W["conv"][:, j:j + 1], 0.0, ALU.mult, ALU.add)\
                    .then_inc(S["diag_ready"], 1)
            pool.wait_ge(S["s4_pq"], 2)
            pool.wait_ge(S["topk_final"], 1)
            pool.wait_ge(S["mask_row"], 4)
            for i in range(4):
                a, b = ctx_cuts[i], ctx_cuts[i + 1]
                pool.wait_ge(ld_ctxT[i], 16)
                nc.gpsimd.tensor_scalar(ctx_bf[:, a:b], ctxT[0:KA, a:b], 1.0, 0.0, ALU.mult, ALU.add).then_inc(S["ctx_bf"], 1)

            def key_low(n):
                s, w = SB0[n]
                pool.wait_ge(S["k_mid"], n + 1)
                tt(kpart[2][:, s:s + w], krest[:, n % 2, 0:w], kpart[1][:, s:s + w], ALU.subtract).then_inc(S["k_low"], 1)

            done = 0
            for norm, keys in K_LOW:
                for n in range(done, keys):
                    key_low(n)
                if norm:
                    rsqrt(norm)
                done = keys
            for n in range(7, 11):
                rsqrt(n)

        @block.scalar
        def _(act):
            chain = [0]

            def link(ins):
                chain[0] += 1
                ins.then_inc(S["act_chain"], 1)
                act.wait_ge(S["act_chain"], chain[0])

            A_ = nc.scalar.activation
            act.wait_ge(S["ld_s"], 16)
            A_(sdt[:, :], W["log_dt"], ACT.Exp).then_inc(S["dt_ready"], 1)
            act.wait_ge(S["ld_gmask"], 16)

            def mask_row(i):
                a, b = ctx_cuts[i], ctx_cuts[i + 1]
                act.wait_ge(ld_ctxT[i], 16)
                A_(ctxT[DC:DC + 1, a:b], gmask[:, a:b], ACT.Copy, scale=-NEG, bias=NEG).then_inc(S["mask_row"], 1)

            def evac_scores(n):
                k, (s, w) = n // len(SB0), SB0[n % len(SB0)]
                act.wait_ge(S["scores_ps"], n + 1)
                A_(scores[:, k * G + s:k * G + s + w], A[:, n % 4, 0:w], ACT.Copy).then_inc(S["scores_evac"], 1)

            mask_row(0)
            mask_row(1)
            evac_scores(0)
            mask_row(2)
            evac_scores(1)
            evac_scores(2)
            mask_row(3)
            act.wait_ge(S["s4_theta"], 1)
            link(A_(smore[:, 0, :], sar[:, :], ACT.Exp))

            def magnitudes(l):
                A_(mags[:, l, :], sar[:, :], ACT.Exp, scale=float(RB * l))
                A_(mags[:, 8 + l, :], sar[:, :], ACT.Exp, scale=float(l)).then_inc(S["s4_mag"], 1)

            for n in range(3, SIN_AT):
                evac_scores(n)
            act.wait_ge(S["s4_cs"], 2)
            A_(turns[:, :, :], kint[:, :, :], ACT.Sin, scale=TWO_PI).then_inc(S["s4_sin"], 1)
            A_(smore[:, 1:3, :], smore[:, 3:5, :], ACT.Sin, scale=TWO_PI).then_inc(S["s4_z"], 1)
            for n in range(SIN_AT, 2 * len(SB0)):
                evac_scores(n)
                if n - SIN_AT < 4:
                    magnitudes(2 * (n - SIN_AT))
                    magnitudes(2 * (n - SIN_AT) + 1)
            for k in range(2):
                act.wait_ge(S["negm0"], k + 1)
                A_(ztop[:, k, :], top[:, k, :], ACT.Exp, bias=negm0[:, k:k + 1], accum_out=z0[:, k:k + 1])\
                    .then_inc(S["z0_ready"], 1)
            act.wait_ge(S["s4_pq"], 2)
            act.wait_ge(S["topk_final"], 1)

            def evac_attn(b):
                act.wait_ge(S["attnT_ps"], b + 1)
                n = len(GROUPS[b]) * P
                A_(attnT[:, b % 3, 0:n], attn_bank[b % 4][:, 0:n], ACT.Copy).then_inc(S["attnT_sb"], 1)

            for b, cs in enumerate(GROUPS):
                for k in range(2):
                    if b >= RING:
                        act.wait_ge(S["attnT_ps"], b - RING + 1)
                    w = len(cs) * P
                    A_(probs[:, (b % RING) * 1024 + k * BANK:(b % RING) * 1024 + k * BANK + w],
                       scores[:, k * G + b * BANK:k * G + b * BANK + w], ACT.Exp, bias=negm0[:, k:k + 1])\
                        .then_inc(S["e_ready"], 1)
                if b >= EVAC_LAG:
                    evac_attn(b - EVAC_LAG)
            for b in range(len(GROUPS) - EVAC_LAG, len(GROUPS)):
                evac_attn(b)

            def key_hi(n):
                s, w = SB0[n]
                act.wait_ge(S["k_ps"], n + 1)
                A_(kpart[0][:, s:s + w], A[:, n % 2, 0:w], ACT.Copy).then_inc(S["k_hi"], 1)

            def key_mid(n):
                s, w = SB0[n]
                act.wait_ge(S["k_rest"], n + 1)
                A_(kpart[1][:, s:s + w], krest[:, n % 2, 0:w], ACT.Copy).then_inc(S["k_mid"], 1)

            def evac_values(b):
                act.wait_ge(S["v1_ps"], b + 1)
                n = len(V_BANKS[b]) * NQ * VQ
                A_(v1_cols(V_BANKS[b][0], 0, n), v_bank[b][:, 0:n], ACT.Copy).then_inc(S["v1_sb"], 1)

            def keys_at(place):
                for n in range(*K_AT[place]):
                    key_hi(n)
                    if n > 0:
                        key_mid(n - 1)
                for b in range(*V_AT.get(place, (0, 0))):
                    evac_values(b)

            for place in ("film", "xf", "y"):
                keys_at(place)
            act.wait_ge(S["pre0_ready"], 1)
            A_(hid0[:, :], pre0[:, :], ACT.Gelu).then_inc(S["gelu0_ready"], 1)
            for place in ("up", "mlp"):
                keys_at(place)
            act.wait_ge(S["g2_pre"], 1)
            A_(ge2[:, :], gpre[:, :], ACT.Exp, scale=-1.0).then_inc(S["g2_exp"], 1)
            keys_at("gla")
            act.wait_ge(S["route_pre"], 1)
            A_(rex[:, :], rpre[:, :], ACT.Exp, scale=-1.0).then_inc(S["route_exp"], 1)
            keys_at("moe")
            key_mid(len(SB0) - 1)
            for b in range(*V_AT["route"]):
                evac_values(b)

            def moe_raw(p):
                act.wait_ge(S["moe_up_ps"], p + 1)
                if p >= 2:
                    act.wait_ge(S["moe_hT_ps"], p - 1)
                m = P if p < 4 else T
                A_(hraw[p % 2][0:m, :], A[0:m, p % 4, :], ACT.Copy).then_inc(S["moe_raw"], 1)

            def moe_gelu(p):
                act.wait_ge(S["moe_pre"], p + 1)
                w = BANK if p < 4 else 256
                A_(hid[:, p * BANK:p * BANK + w], pre[:, p % 2, 0:w], ACT.Gelu).then_inc(S["moe_gelu"], 1)

            moe_raw(0)
            for p in range(1, 5):
                moe_raw(p)
                moe_gelu(p - 1)
            moe_gelu(4)
            for b in range(V_EARLY, V_GAP):
                evac_values(b)
            act.wait_ge(S["qst_ps"], 1)
            A_(qst[:, :], A[0:KS, 2:4, :].rearrange("p a b -> p (a b)"), ACT.Copy).then_inc(S["qst_hi"], 1)
            act.wait_ge(S["qst_rest"], 1)
            A_(qst[64:KS, :], qrest[64:KS, :], ACT.Copy).then_inc(S["qst_mid"], 1)
            for b in range(V_GAP, len(V_BANKS)):
                evac_values(b)
            n = 0
            for j in range(NQ):
                for g, cs in enumerate(GROUPS):
                    act.wait_ge(S["s1_ps"], n + 1)
                    if n >= RING:
                        act.wait_ge(S["pv_done"], n - RING + 1)
                    w = len(cs) * SQ * T
                    A_(probs[:, (n % RING) * 1024:(n % RING) * 1024 + w],
                       A[:, 2 * (n % 2):2 * (n % 2) + 2, :].rearrange("p a b -> p (a b)")[:, 0:w],
                       ACT.Exp).then_inc(S["p_ready"], 1)
                    n += 1
            act.wait_ge(S["d2_ready"], 1)
            A_(p2[:, :, :], d2[:, :, :], ACT.Exp).then_inc(S["p2_ready"], 1)
            act.wait_ge(S["l6_max"], 1)
            A_(ex6[:, :], B[3][:, 0:8], ACT.Exp, bias=nm6[:, :], accum_out=z6[:, :]).then_inc(S["l6_exp"], 1)
            for p in range(4):
                act.wait_ge(S["e6_up_ps"], p + 1)
                A_(gl6[:, p, :], A[:, p, 0:2 * P], ACT.Gelu).then_inc(S["e6_gelu"], 1)

        @block.vector
        def _(dve):
            chain = [0]
            norm = [0]
            V = nc.vector

            def link(ins):
                chain[0] += 1
                ins.then_inc(S["vec_chain"], 1)
                dve.wait_ge(S["vec_chain"], chain[0])

            def layernorm(dst, src, signal=None, meanwhile=None):
                link(V.bn_stats(st[:, :], src))
                link(V.bn_aggr(mv[:, :], st[:, :]))
                V.tensor_scalar_add(ve[:, :], mv[:, 1:2], EPS_LN).then_inc(S["var_ready"], 1)
                norm[0] += 1
                if meanwhile:
                    meanwhile()
                dve.wait_ge(S["rstd_ready"], norm[0])
                ins = V.tensor_scalar(dst, src, mv[:, 0:1], rstd[:, :], ALU.subtract, ALU.mult)
                if signal:
                    ins.then_inc(signal, 1)
                else:
                    link(ins)

            V.memset(onec[:, :], 1.0).then_inc(S["ones_ready"], 1)
            link(V.memset(nm[:, :, :], 0.0))
            link(V.memset(uT[:, :], 0.0))
            link(V.memset(x2w[:, :], 0.0))
            dve.wait_ge(S["ld_a"], 16)
            layernorm(x0[:, :], W["x"])
            V.tensor_scalar_add(nt[:, :], x0[:, :], 0.0).then_inc(S["norm_ready"], 1)
            dve.wait_ge(S["tokT_ps"], 1)
            V.tensor_copy(x0T[:, :], B[0][:, 0:T]).then_inc(S["tokT_sb"], 1)
            dve.wait_ge(S["q0_ps"], 1)
            V.tensor_tensor(q0bd[:, :].rearrange("p (h t) -> p h t", h=H0),
                            B[0][:, T:2 * T].unsqueeze(1).to_broadcast([P, H0, T]),
                            W["mask_h0"].unsqueeze(2).to_broadcast([P, H0, T]), ALU.mult).then_inc(S["q0_bd"], 1)
            dve.wait_ge(S["qq0_ps"], 1)
            V.tensor_copy(qq0[:, :], B[1][0:KA, 0:H0 * T]).then_inc(S["qq0_sb"], 1)

            def chunk_max(n):
                k, (s, w) = n // len(SB0), SB0[n % len(SB0)]
                dve.wait_ge(S["scores_evac"], n + 1)
                for i in range(w // P):
                    c = s // P + i
                    last = V.max(cand[:, k, 8 * c:8 * c + 8], scores[:, k * G + c * P:k * G + (c + 1) * P])
                last.then_inc(S["scores_max"], 1)

            def top32(k):
                dve.wait_ge(S["scores_max"], len(SB0) * (k + 1))
                for r in range(TOPK // 8):
                    src = cand if r == 0 else cwork
                    link(V.max(top[:, k, 8 * r:8 * r + 8], src[:, k, :]))
                    if r < TOPK // 8 - 1:
                        link(V.match_replace(cwork[:, k, :], top[:, k, 8 * r:8 * r + 8], src[:, k, :], -3e38))
                tau = top[:, k, TOPK - 1:TOPK]
                V.tensor_scalar(negm0[:, k:k + 1], top[:, k, 0:1], -1.0, None, ALU.mult).then_inc(S["cand_ready"], 1)
                link(V.tensor_scalar(ge[:, :], cand[:, k, :], tau, None, ALU.is_ge))
                link(V.tensor_reduce(cnt[:, 2 * k:2 * k + 1], ge[:, :], AX_X, ALU.add))
                link(V.tensor_reduce(cnt[:, 2 * k + 1:2 * k + 2],
                                     ge[:, :].rearrange("p (c e) -> p c e", e=8)[:, :, 7], AX_X, ALU.add))
                link(V.tensor_tensor(bad[:, k:k + 1], cnt[:, 2 * k:2 * k + 1], cnt[:, 2 * k + 1:2 * k + 2], ALU.add))

            for n in range(len(SB0)):
                chunk_max(n)
                if n == TURNS_AT - 1:
                    dve.wait_ge(S["s4_turns"], 1)
                    link(V.tensor_scalar(kint[:, 0:16], turns[:, 0:16], ROUND, ROUND, ALU.add, ALU.subtract))
                    V.tensor_tensor(kint[:, 0:16], turns[:, 0:16], kint[:, 0:16], ALU.subtract).then_inc(S["s4_cs"], 1)
                    dve.wait_ge(S["s4_inv"], 1)
                    V.reciprocal(g4[:, 3, :], g4[:, 2, :]).then_inc(S["s4_gain"], 1)
            top32(0)
            for n in range(len(SB0), 2 * len(SB0)):
                chunk_max(n)
            top32(1)
            dve.wait_ge(S["scores_evac"], 2 * len(SB0))
            V.tensor_scalar_add(rz0[:, :], bad[:, :], 0.0).then_inc(S["rep_ready"], 1)
            dve.wait_ge(S["flag_ps"], 1)
            link(V.tensor_reduce(flagf[:, 0:1], B[1][0:1, 0:2], AX_X, ALU.add))
            link(V.tensor_scalar(flag[:, 0:1], flagf[:, 0:1], float(2 * P * TOPK), None, ALU.is_gt))
            need_exact = dve.value_load(flag[0:1, 0:1], min_val=0, max_val=1)
            with dve.If(need_exact > 0):
                step = [0]

                def slow(ins):
                    step[0] += 1
                    ins.then_inc(S["vec_slow"], 1)
                    dve.wait_ge(S["vec_slow"], step[0])

                dve.wait_ge(S["s4_pq"], 2)
                for k in range(2):
                    tile = scores[:, k * G:(k + 1) * G]
                    for r in range(TOPK // 8):
                        src = tile if r == 0 else late[:, :]
                        slow(V.max(top[:, k, 8 * r:8 * r + 8], src))
                        slow(V.match_replace(late[:, :], top[:, k, 8 * r:8 * r + 8], src, -3e38))
                    slow(V.tensor_scalar(late[:, :], late[:, :], -2e38, -1e36, ALU.is_gt, ALU.mult))
                    slow(V.tensor_tensor(tile, tile, late[:, :], ALU.add))
            V.tensor_scalar(negm0[:, :], top[:, :, 0], -1.0, None, ALU.mult).then_inc(S["topk_final"], 1)
            dve.wait_ge(S["topk_final"], 1)
            V.tensor_scalar(rz0[:, :], top[:, :, 0], -1.0, None, ALU.mult).then_inc(S["negm0"], 2)
            dve.wait_ge(S["ld_tmask"], 16)
            link(V.tensor_copy(tmf[:, :], tmask[:, :]))
            dve.wait_ge(S["z0_ready"], 2)
            link(V.reciprocal(rz0[:, :], z0[:, :]))
            link(V.tensor_tensor(rho[:, :], z0[:, 1:2], rz0[:, 0:1], ALU.mult))
            link(V.tensor_scalar(rz0[:, :], rz0[:, :], tmf[:, :], 1.0 / H0, ALU.mult, ALU.mult))
            dve.wait_ge(S["ld_m"], 16)
            V.tensor_scalar(seln[:, :], W["sel_t"], rz0[:, 1:2], None, ALU.mult).then_inc(S["sel0_ready"], 1)
            dve.wait_ge(S["m1_ps"], 1)
            for q in range(2):
                V.tensor_tensor(m1[:, 4 * q:4 * q + 4, :].rearrange("p g (d b) -> p (g d) b", b=RB),
                                A[:, q, :].rearrange("p (g d b) -> p (g d) b", g=4, b=RB),
                                W["mask_h1"].unsqueeze(1).unsqueeze(3).to_broadcast([P, 4, H1, RB])
                                .rearrange("p g d b -> p g d b"), ALU.mult).then_inc(S["m1_sb"], 1)
            for b, cs in enumerate(GROUPS):
                w = len(cs) * P
                e = [probs[:, (b % RING) * 1024 + k * BANK:(b % RING) * 1024 + k * BANK + w] for k in range(2)]
                for k in range(2):
                    dve.wait_ge(S["e_ready"], 2 * b + k + 1)
                    last = V.scalar_tensor_tensor(e[k], scores[:, k * G + b * BANK:k * G + b * BANK + w],
                                                  top[:, k, TOPK - 1:TOPK], e[k], ALU.is_ge, ALU.mult)
                link(last)
                V.scalar_tensor_tensor(e[0], e[0], rho[:, :], e[1], ALU.mult, ALU.add).then_inc(S["w_ready"], 1)
                if b == 4:
                    dve.wait_ge(S["wcf_ps"], 1)
                    V.tensor_scalar(wcf[:, :], A[0:DC, 2, :], W["gate"][0:DC, :], None, ALU.mult).then_inc(S["wcf_sb"], 1)
                    dve.wait_ge(S["ld_rows"], 16 * len(ROWS))
                    V.scalar_tensor_tensor(W["film_1"], W["film_b"], W["gate"][0:1, :], W["film_1"],
                                           ALU.mult, ALU.add).then_inc(S["film_row"], 1)
                    layernorm(xin[:, :], x0[:, :])
                    link(V.tensor_tensor(xin[:, :], xin[:, :], W["g_in"], ALU.mult))
                    link(V.tensor_tensor(xin[:, :], xin[:, :], W["b_in"], ALU.add))

            def key_rest(place):
                for n in range(*K_AT[place]):
                    s, w = SB0[n]
                    dve.wait_ge(S["k_hi"], n + 1)
                    if n >= 2:
                        dve.wait_ge(S["k_low"], n - 1)
                    V.tensor_tensor(krest[:, n % 2, 0:w], A[:, n % 2, 0:w], kpart[0][:, s:s + w], ALU.subtract)\
                        .then_inc(S["k_rest"], 1)

            dve.wait_ge(S["c2T_ps"], 1)
            V.tensor_copy(c2T[:, :], B[0][0:DC, 0:P]).then_inc(S["c2T_sb"], 1)
            dve.wait_ge(S["c2_ps"], 1)
            V.tensor_copy(c2[:, :], B[1][:, 0:DC]).then_inc(S["c2_sb"], 1)
            dve.wait_ge(S["cT_ps"], 1)
            V.tensor_copy(cT[:, :], B[0][0:DC, P:P + T]).then_inc(S["cT_sb"], 1)
            dve.wait_ge(S["film_ps"], 1)
            link(V.tensor_tensor(xm[:, :], xin[:, :], B[1][0:T, 0:D], ALU.mult))
            V.tensor_tensor(xm2[:, :], xm[:, :], B[1][0:T, D:2 * D], ALU.add).then_inc(S["xm_ready"], 1)
            link(V.tensor_tensor(sh[:, :], x0[:, :], B[1][0:T, 3 * D:4 * D], ALU.add))
            key_rest("film")
            dve.wait_ge(S["kf_ps"], 1)
            V.tensor_copy(kf[:, :, :], A[0:FREQ, 3, 0:2 * D].rearrange("p (c d) -> p c d", c=2)).then_inc(S["kf_sb"], 1)
            dve.wait_ge(S["kf_sb"], 1)
            dve.wait_ge(S["xf_ps"], 1)
            xf = B[2][0:FREQ, 0:2 * D].rearrange("p (c d) -> p c d", c=2)
            V.tensor_tensor(pa[:, :, :], xf, kf[:, 0:1, :].to_broadcast([FREQ, 2, D]), ALU.mult)
            V.tensor_tensor(pb[:, :, :], xf, kf[:, 1:2, :].to_broadcast([FREQ, 2, D]), ALU.mult).then_inc(S["prod_ready"], 1)
            key_rest("xf")
            dve.wait_ge(S["y_ps"], 1)
            link(V.tensor_copy(y1[:, :], B[3][0:T, 0:D]))
            link(V.tensor_tensor(y1[:, :], y1[:, :], B[1][0:T, 2 * D:3 * D], ALU.mult))
            link(V.tensor_tensor(xt[:, :], y1[:, :], sh[:, :], ALU.add))
            layernorm(hn[:, :], xt[:, :], S["norm_ready"])
            key_rest("y")
            dve.wait_ge(S["tokT_ps"], 2)
            V.tensor_scalar(hT[:, :], B[2][:, 0:T], W["g_ffn"], W["b_ffn"], ALU.mult, ALU.add).then_inc(S["tokT_sb"], 1)
            dve.wait_ge(S["up0_ps"], 1)
            V.tensor_tensor(pre0[:, :].rearrange("p (c t) -> p c t", c=4), B[3][:, 0:4 * T].rearrange("p (c t) -> p c t", c=4),
                            W["b1T"].unsqueeze(2).to_broadcast([P, 4, T]), ALU.add).then_inc(S["pre0_ready"], 1)
            key_rest("up")
            dve.wait_ge(S["mlp0_ps"], 1)
            link(V.tensor_tensor(xt2[:, :], xt[:, :], B[2][0:T, 0:D], ALU.add))
            layernorm(nt[:, :], xt2[:, :])
            link(V.tensor_tensor(nt2[:, :], nt[:, :], W["g_out"], ALU.mult))
            link(V.tensor_tensor(nt[:, :], nt2[:, :], W["b_out"], ALU.add))
            link(V.tensor_tensor(x1[:, :], nt[:, :], W["x"], ALU.add))
            layernorm(u1[:, :], x1[:, :], S["norm_ready"])
            key_rest("mlp")
            dve.wait_ge(S["ut_ps"], 1)
            V.tensor_copy(uT[:, 1:T + 1], B[2][:, 0:T]).then_inc(S["ut_sb"], 1)
            V.tensor_copy(cumT[:, :], B[2][:, T:2 * T]).then_inc(S["ut_sb"], 1)
            dve.wait_ge(S["g1_ps"], 1)
            V.tensor_scalar(g1[:, :], B[3][0:32, 0:T], W["gb1"], 0.0, ALU.add, ALU.max).then_inc(S["g1_sb"], 1)
            link(V.tensor_copy(ub[:, :], B[3][0:32, T:2 * T]))
            dve.wait_ge(S["g1_ps"], 2)
            link(V.tensor_tensor(us[:, :], ub[:, :], B[0][0:32, 0:T], ALU.mult))
            dve.wait_ge(S["g2_ps"], 1)
            V.tensor_scalar(gpre[:, :], B[1][0:32, 0:T], W["gb2"], -87.0, ALU.add, ALU.max).then_inc(S["g2_pre"], 1)
            dve.wait_ge(S["g2_exp"], 1)
            link(V.tensor_scalar_add(ge3[:, :], ge2[:, :], 1.0))
            link(V.reciprocal(ge4[:, :], ge3[:, :]))
            V.tensor_tensor(glob[:, :], us[:, :], ge4[:, :], ALU.mult).then_inc(S["glob_ready"], 1)
            key_rest("gla")
            dve.wait_ge(S["blk1_ps"], 1)
            link(V.tensor_tensor(x2[:, :], x1[:, :], B[2][0:T, 0:D], ALU.add))
            layernorm(v[:, :], x2[:, :], S["norm_ready"])
            dve.wait_ge(S["tokT_ps"], 3)
            V.tensor_copy(vT[:, 0, :], B[3][:, 2 * D:2 * D + T])
            V.tensor_copy(vT[:, 1, :], B[3][:, 2 * D:2 * D + T]).then_inc(S["tokT_sb"], 1)
            dve.wait_ge(S["route_ps"], 1)
            V.tensor_scalar(rpre[:, :], B[3][:, 0:8], 1.0, -87.0, ALU.mult, ALU.max).then_inc(S["route_pre"], 1)
            dve.wait_ge(S["route_exp"], 1)
            link(V.tensor_scalar_add(rex1[:, :], rex[:, :], 1.0))
            link(V.reciprocal(rsc[:, :], rex1[:, :]))

            def choose_two(p8, r):
                link(V.max(r8[:, :], p8))
                link(V.max_index(ri[:, :], r8[:, :], p8))
                link(V.tensor_copy(rif[:, :], ri[:, 0:2]))
                r()
                link(V.tensor_scalar(oh[:, :], W["iota8"], rif[:, 0:1], rw[:, 0:1], ALU.is_equal, ALU.mult))
                link(V.tensor_scalar(oh2[:, :], W["iota8"], rif[:, 1:2], rw[:, 1:2], ALU.is_equal, ALU.mult))
                link(V.tensor_tensor(comb[:, :], oh[:, :], oh2[:, :], ALU.add))
                link(V.tensor_tensor(cpair[:, :, :], comb[:, :].rearrange("p (a b) -> p a b", b=2),
                                     W["mask_p"].unsqueeze(1).to_broadcast([P, 4, 2]), ALU.mult))
                link(V.tensor_reduce(csel[:, :], cpair[:, :, :], AX_X, ALU.add))

            def normalised():
                link(V.tensor_tensor(rs[:, 0:1], r8[:, 0:1], r8[:, 1:2], ALU.add))
                link(V.tensor_scalar_add(rs[:, 1:2], rs[:, 0:1], 1e-6))
                link(V.reciprocal(rs[:, 2:3], rs[:, 1:2]))
                link(V.tensor_scalar(rw[:, :], r8[:, 0:2], rs[:, 2:3], None, ALU.mult))

            def moe_pre(p):
                dve.wait_ge(S["moe_hT_ps"], p + 1)
                if p >= 2:
                    dve.wait_ge(S["moe_gelu"], p - 1)
                ne = 2 if p < 4 else 1
                V.tensor_tensor(pre[:, p % 2, 0:4 * ne * T].rearrange("p (c e t) -> p c e t", c=4, e=ne),
                                B[p % 2][:, :].rearrange("p (c e t) -> p c e t", c=4, e=2)[:, :, 0:ne, :],
                                W["moe_b1T"][:, 8 * p:8 * p + 4 * ne].rearrange("p (e c) -> p c e", e=ne).unsqueeze(3)
                                .to_broadcast([P, 4, ne, T]), ALU.add).then_inc(S["moe_pre"], 1)

            def add_pair(p, prev, y_ready):
                dve.wait_ge(S[y_ready], p + 1)
                V.scalar_tensor_tensor(acc[:, p % 2, :], B[2 + p % 2][:, 0:D], csel[:, p:p + 1], prev,
                                       ALU.mult, ALU.add).then_inc(S["moe_acc"], 1)
                dve.wait_ge(S["moe_acc"], p + 1 + (0 if y_ready == "moe_y_ps" else 5))
                return acc[:, p % 2, :]

            key_rest("moe")
            dve.wait_ge(S["ld_l"], 16)
            moe_pre(0)
            moe_pre(1)
            choose_two(rsc[:, :], normalised)
            moe_pre(2)
            moe_pre(3)
            prev = add_pair(0, x2w[:, :], "moe_y_ps")
            moe_pre(4)
            for p in range(1, 4):
                prev = add_pair(p, prev, "moe_y_ps")
            dve.wait_ge(S["moe_y_ps"], 5)
            V.scalar_tensor_tensor(acc[0:T, 1, :], B[2][0:T, 0:D], 0.1, acc[0:T, 1, :], ALU.mult, ALU.add)\
                .then_inc(S["moe_acc"], 1)
            x3 = acc[0:T, 2, :]
            dve.wait_ge(S["x3_ps"], 1)
            link(V.tensor_copy(x3, B[2][0:T, 0:D]))
            layernorm(n3[:, :], x3, S["norm_ready"])
            dve.wait_ge(S["tokT_ps"], 4)
            V.tensor_copy(n3T[:, :], B[3][:, 0:T]).then_inc(S["tokT_sb"], 1)
            dve.wait_ge(S["q1_ps"], 1)
            link(V.tensor_scalar(q1[:, :], B[3][:, T:2 * T], W["bq1"], W["scale1"], ALU.add, ALU.mult))
            V.tensor_tensor(qbd[:, :, :], q1[:, :].unsqueeze(1).to_broadcast([P, H1, T]),
                            W["mask_h1"].unsqueeze(2).to_broadcast([P, H1, T]), ALU.mult).then_inc(S["q1_bd"], 1)
            dve.wait_ge(S["qq1_ps"], 2)
            V.tensor_copy(qq1b[:, :], A[0:KA, 0:2, :].rearrange("p a b -> p (a b)")).then_inc(S["qq1_bf"], 1)
            dve.wait_ge(S["qst_hi"], 1)
            V.tensor_tensor(qrest[64:KS, :], A[64:KS, 2:4, :].rearrange("p a b -> p (a b)"), qst[64:KS, :],
                            ALU.subtract).then_inc(S["qst_rest"], 1)

            def row_max(n):
                i, (s, w) = n // len(SB0), SB0[n % len(SB0)]
                dve.wait_ge(S["max_ps"], n + 1)
                V.tensor_reduce(mx[:, i, n % len(SB0):n % len(SB0) + 1], B[2 + n % 2][:, 0:w], AX_X, ALU.max)\
                    .then_inc(S["max_used"], 1)

            def shift_quad(j):
                dve.wait_ge(S["max_used"], 2 * len(SB0) * (j + 1))
                V.tensor_reduce(nm[:, 2 * j:2 * j + 2, 0:1], mx[:, 2 * j:2 * j + 2, :], AX_X, ALU.max, negate=True)\
                    .then_inc(S["negm1"], 1)
                dve.wait_ge(S["fix_ps"], j + 1)
                cols = slice(j * SQ * T, (j + 1) * SQ * T)
                V.tensor_copy(qst[SHIFT_ROW:SHIFT_ROW + 1, cols], B[2][SHIFT_ROW:SHIFT_ROW + 1, 0:SQ * T])\
                    .then_inc(S["qq_fixed"], 1)

            NM = 2 * len(SB0)
            for n in range(NM):
                row_max(n)
            dve.wait_ge(S["qst_mid"], 1)
            V.tensor_tensor(qst[SHIFT_ROW:KS, :], qrest[SHIFT_ROW:KS, :], qst[SHIFT_ROW:KS, :], ALU.subtract)\
                .then_inc(S["qst_sb"], 1)
            dve.wait_ge(S["qst_sb"], 1)
            shift_quad(0)
            def divide(j):
                dve.wait_ge(S["zt_ps"], j + 1)
                link(V.tensor_tensor(om[:, 1, :].rearrange("p (h t) -> p h t", h=SQ),
                                     B[1][:, 0:SQ * T].rearrange("p (h t) -> p h t", h=SQ),
                                     W["mask_q"].unsqueeze(2).to_broadcast([P, SQ, T]), ALU.mult))
                link(V.tensor_reduce(z1[:, j, :], om[:, 1, :].rearrange("p (h t) -> p t h", h=SQ), AX_X, ALU.add))
                link(V.reciprocal(zi[:, j, :], z1[:, j, :]))
                V.tensor_tensor(o2[:, j, :], o1[:, j, :], zi[:, j, :], ALU.mult).then_inc(S["o_ready"], 1)

            for j in range(NQ):
                if j + 1 < NQ:
                    for n in range(NM):
                        row_max(NM * (j + 1) + n)
                        if n == 3 and j >= 1:
                            divide(j - 1)
                    shift_quad(j + 1)
                if j == NQ - 1:
                    divide(j - 1)
                dve.wait_ge(S["pv_done"], len(GROUPS) * (j + 1))
                for i, m in enumerate(("mask_q", "mask_z")):
                    V.tensor_tensor(om[:, i, :].rearrange("p (h t) -> p h t", h=SQ),
                                    B[0][:, 0:SQ * T].rearrange("p (h t) -> p h t", h=SQ),
                                    W[m].unsqueeze(2).to_broadcast([P, SQ, T]), ALU.mult).then_inc(S["acc_used"], 1)
                dve.wait_ge(S["acc_used"], 2 * (j + 1))
                V.tensor_reduce(o1[:, j, :], om[:, 0, :].rearrange("p (h t) -> p t h", h=SQ), AX_X, ALU.add)
            divide(NQ - 1)
            dve.wait_ge(S["y1_ps"], 1)
            link(V.tensor_tensor(x4[:, :], x3, B[3][0:T, 0:D], ALU.add))
            layernorm(n4[:, :], x4[:, :], S["norm_ready"])
            dve.wait_ge(S["tokT_ps"], 5)
            V.tensor_copy(n4T[:, 0, :], B[2][:, 0:T])
            V.tensor_copy(n4T[:, 1, :], B[2][:, 0:T]).then_inc(S["tokT_sb"], 1)
            dve.wait_ge(S["qk2_ps"], 1)
            V.tensor_scalar(q2[:, :], B[3][:, 0:T], float(DH1) ** -0.5, None, ALU.mult).then_inc(S["q2_sb"], 1)
            V.tensor_tensor(kbd[:, :, :], B[3][:, T:2 * T].unsqueeze(1).to_broadcast([P, H1, T]),
                            W["mask_h1"].unsqueeze(2).to_broadcast([P, H1, T]), ALU.mult).then_inc(S["k2_bd"], 1)
            dve.wait_ge(S["v2_ps"], 1)
            V.tensor_tensor(vbd[:, :, :, :], B[0][:, 0:D].rearrange("p (q h c) -> p q h c", h=2, c=8),
                            W["mask_p"].unsqueeze(1).unsqueeze(3).to_broadcast([P, 8, 2, 8]), ALU.mult).then_inc(S["v2_bd"], 1)
            dve.wait_ge(S["s2_ps"], 1)
            sc2 = A[0:T, 0:2, :].rearrange("p a (h k) -> p (a h) k", k=T)
            link(V.tensor_reduce(m2[:, :], sc2, AX_X, ALU.max))
            V.tensor_tensor(d2[:, :, :], sc2, m2[:, :].unsqueeze(2).to_broadcast([T, H1, T]), ALU.subtract)\
                .then_inc(S["d2_ready"], 1)
            dve.wait_ge(S["p2_ready"], 1)
            link(V.tensor_reduce(s2[:, :], p2[:, :, :], AX_X, ALU.add))
            link(V.reciprocal(i2[:, :], s2[:, :]))
            dve.wait_ge(S["pT_ps"], 1)
            V.tensor_copy(pT[:, :, :], A[:, 2, :].rearrange("p (q t) -> p q t", q=8)).then_inc(S["pT_sb"], 1)
            dve.wait_ge(S["o2_ps"], 1)
            V.tensor_tensor(oo[:, :].rearrange("p (h c) -> p h c", c=8), B[1][0:T, 0:D].rearrange("p (h c) -> p h c", c=8),
                            i2[:, :].unsqueeze(2).to_broadcast([T, H1, 8]), ALU.mult).then_inc(S["o2_ready"], 1)
            dve.wait_ge(S["tokT_ps"], 6)
            V.tensor_copy(ooT[:, :], B[2][:, 0:T]).then_inc(S["tokT_sb"], 1)
            dve.wait_ge(S["y2_ps"], 1)
            link(V.tensor_tensor(x5[:, :], x4[:, :], B[3][0:T, 0:D], ALU.add))
            layernorm(u6[:, :], x5[:, :])
            link(V.bn_stats(st[:, :], u6[:, :]))
            link(V.bn_aggr(mv[:, :], st[:, :]))
            link(V.tensor_tensor(msq[:, 0:1], mv[:, 0:1], mv[:, 0:1], ALU.mult))
            V.scalar_tensor_tensor(ve[:, :], msq[:, 0:1], EPS_RMS, mv[:, 1:2], ALU.add, ALU.add).then_inc(S["var_ready"], 1)
            V.tensor_scalar_add(nt[:, :], u6[:, :], 0.0).then_inc(S["norm_ready"], 1)
            norm[0] += 1
            dve.wait_ge(S["rstd_ready"], norm[0])
            V.tensor_scalar(h6[:, :], u6[:, :], rstd[:, :], None, ALU.mult).then_inc(S["r6_ready"], 1)
            dve.wait_ge(S["tokT_ps"], 7)
            V.tensor_copy(u6T[:, 0, :], B[2][:, 0:T])
            V.tensor_copy(u6T[:, 1, :], B[2][:, 0:T]).then_inc(S["tokT_sb"], 1)
            dve.wait_ge(S["tokT_ps"], 8)
            link(V.tensor_copy(h6T[:, :], B[2][:, T:2 * T]))
            V.tensor_tensor(h6e[:, :, :], h6T[:, :].unsqueeze(1).to_broadcast([P, 8, T]),
                            W["norm_wT"].unsqueeze(2).to_broadcast([P, 8, T]), ALU.mult).then_inc(S["h6_sb"], 1)
            dve.wait_ge(S["rt6_ps"], 1)
            link(V.max(m8[:, :], B[3][:, 0:8]))
            V.tensor_scalar(nm6[:, :], m8[:, 0:1], -1.0, None, ALU.mult).then_inc(S["l6_max"], 1)
            dve.wait_ge(S["l6_exp"], 1)
            link(V.reciprocal(iz6[:, :], z6[:, :]))
            link(V.tensor_scalar(rsc[:, :], ex6[:, :], iz6[:, :], None, ALU.mult))

            def plain():
                link(V.tensor_copy(rw[:, :], r8[:, 0:2]))

            choose_two(rsc[:, :], plain)
            def gate_up_T(p):
                dve.wait_ge(S["e6_guT_ps"], p + 1)
                V.tensor_copy(guT[:, p, :, :], B[p % 2][:, 0:2 * P].rearrange("p (c t) -> p c t", c=2)).then_inc(S["e6_guT_sb"], 1)

            link(V.tensor_tensor(sw6[:, :], rw[0:T, 0:1], rw[0:T, 1:2], ALU.add))
            link(V.tensor_scalar_add(w6[:, 0:1], sw6[:, :], 1.0))
            link(V.scalar_tensor_tensor(x2, u6[:, :], w6[:, 0:1], x5[:, :], ALU.mult, ALU.add))
            for p in range(4):
                dve.wait_ge(S["e6_gelu"], p + 1)
                V.tensor_tensor(gu6[:, p, :], gl6[:, p, :], A[:, p, 2 * P:4 * P], ALU.mult).then_inc(S["e6_gu"], 1)
                if p >= 1:
                    gate_up_T(p - 1)
            gate_up_T(3)
            prev = x2w[:, :]
            for p in range(4):
                prev = add_pair(p, prev, "e6_y_ps")
            dve.wait_ge(S["out_ps"], 1)
            V.tensor_copy(acc[0:T, 3, :], B[0][0:T, 0:D]).then_inc(S["out_ready"], 1)

        @block.tensor
        def _(pe):
            mm = nc.tensor.matmul
            idT = W["ident"][0:T, 0:T]

            def one(out_, lhsT, rhs, start=True, stop=True):
                return mm(out_, lhsT, rhs, start=start, stop=stop)

            def keep_clock_up(place, bank=2):
                for _ in range(FILL.get(place, 0)):
                    one(A[:, bank, :], ones_bf[:, 0:P], ones_bf[:, 0:BANK])

            pe.wait_ge(S["ones_ready"], 1)
            pe.wait_ge(S["ld_a"], 16)
            pe.wait_ge(S["norm_ready"], 1)
            nc.tensor.transpose(B[0][:, 0:T], x0[:, :], idT).then_inc(S["tokT_ps"], 1)
            pe.wait_ge(S["tokT_sb"], 1)
            one(B[0][:, T:2 * T], W["wq0"], x0T[:, :]).then_inc(S["q0_ps"], 1)
            pe.wait_ge(S["q0_bd"], 1)
            pe.wait_ge(S["ld_rows"], 16 * len(ROWS))
            one(B[1][0:KA, 0:H0 * T], W["wkT0"], q0bd[:, :], stop=False)
            one(B[1][0:KA, 0:H0 * T], W["e_mask"], one_at["e_mask"], start=False).then_inc(S["qq0_ps"], 1)
            pe.wait_ge(S["qq0_sb"], 1)
            for n in range(2 * len(SB0)):
                k, (s, w) = n // len(SB0), SB0[n % len(SB0)]
                if k == 0 and s in ctx_cuts:
                    pe.wait_ge(ld_ctxT[ctx_cuts.index(s)], 16)
                    pe.wait_ge(S["mask_row"], ctx_cuts.index(s) + 1)
                if n >= 4:
                    pe.wait_ge(S["scores_evac"], n - 3)
                one(A[:, n % 4, 0:w], qq0[:, k * P:(k + 1) * P], ctxT[0:KA, s:s + w]).then_inc(S["scores_ps"], 1)
            pe.wait_ge(S["ld_m"], 16)
            pe.wait_ge(S["scores_evac"], 2 * len(SB0))
            one(A[0:DC, 2, :], W["wvT0"], W["film_w"]).then_inc(S["wcf_ps"], 1)
            pe.wait_ge(S["rep_ready"], 1)
            one(B[1][0:1, 0:2], onec[:, 0:1], bad[:, :]).then_inc(S["flag_ps"], 1)
            pe.wait_ge(S["s4_pq"], 2)
            for g in range(8):
                last = one(A[:, g // 4, (g % 4) * P:(g % 4 + 1) * P],
                           s4p[:, 16 * g:16 * g + 16, :].rearrange("p d l -> p (d l)"),
                           s4q[:, 16 * g:16 * g + 16, :].rearrange("p d l -> p (d l)"))
            last.then_inc(S["m1_ps"], 1)
            def spectrum(lo, hi):
                if lo == 0:
                    pe.wait_ge(S["ld_dft"], 16)
                    pe.wait_ge(S["m1_sb"], 2)
                for n in range(lo, hi):
                    part, bb = divmod(n, RB)
                    o = A[0:FREQ, 3, part * D:(part + 1) * D]
                    last = one(o, dft_k[:, (bb * 2 + part) * FREQ:(bb * 2 + part + 1) * FREQ],
                               m1[:, :, :].rearrange("p g (d b) -> p b (g d)", b=RB)[:, bb, :],
                               start=(bb == 0), stop=(n == 2 * RB - 1))
                    if n == RB - 1:
                        one(o, one_at["d_skip"][:, 0:FREQ], W["d_skip"], start=False)
                if hi == 2 * RB:
                    last.then_inc(S["kf_ps"], 1)

            pe.wait_ge(S["ld_ctx"], 16)

            def values(b):
                pe.wait_ge(S["attnT_sb"], b + 1)
                for i, c in enumerate(GROUPS[b]):
                    last = one(B[0][0:DC, 0:P], ctxn[:, c * DC:(c + 1) * DC], attnT[:, b % 3, i * P:(i + 1) * P],
                               start=(c == 0), stop=(c == NC - 1))
                return last

            for b, cs in enumerate(GROUPS):
                if b == 2:
                    pe.wait_ge(S["m1_sb"], 2)
                if b >= 4:
                    pe.wait_ge(S["attnT_sb"], b - 3)
                pe.wait_ge(S["w_ready"], b + 1)
                for i, c in enumerate(cs):
                    last = nc.tensor.transpose(attn_bank[b % 4][:, i * P:(i + 1) * P],
                                               probs[:, (b % RING) * 1024 + i * P:(b % RING) * 1024 + (i + 1) * P], W["ident"])
                last.then_inc(S["attnT_ps"], 1)
                if b >= 2:
                    values(b - 2)
                if b == 0:
                    spectrum(0, 4)
            values(len(GROUPS) - 2)
            values(len(GROUPS) - 1).then_inc(S["c2T_ps"], 1)
            spectrum(4, 6)
            pe.wait_ge(S["flag_ps"], 1)
            pe.wait_ge(S["topk_final"], 1)
            pe.wait_ge(S["c2T_sb"], 1)
            nc.tensor.transpose(B[1][:, 0:DC], c2T[:, :], W["ident"][0:DC, 0:DC]).then_inc(S["c2_ps"], 1)
            spectrum(6, 8)
            pe.wait_ge(S["c2_sb"], 1)
            pe.wait_ge(S["sel0_ready"], 1)
            one(B[0][0:DC, P:P + T], c2[:, :], seln[:, :]).then_inc(S["cT_ps"], 1)
            spectrum(8, 11)

            def project_values(b):
                if b >= 2:
                    pe.wait_ge(S["v1_sb"], b - 1)
                for i, c in enumerate(V_BANKS[b]):
                    last = one(v_bank[b][:, i * NQ * VQ:(i + 1) * NQ * VQ], chunk_cols(ctxT[0:KA, :], c), W["wv1"])
                last.then_inc(S["v1_ps"], 1)

            def project_keys(place):
                for n in range(*K_AT[place]):
                    s, w = SB0[n]
                    if n >= 2:
                        pe.wait_ge(S["k_rest"], n - 1)
                    one(A[:, n % 2, 0:w], W["wk1"], ctxT[0:KA, s:s + w]).then_inc(S["k_ps"], 1)
                for b in range(*V_AT.get(place, (0, 0))):
                    project_values(b)

            pe.wait_ge(S["film_row"], 1)
            pe.wait_ge(S["flag_ps"], 1)
            pe.wait_ge(S["topk_final"], 1)
            one(B[1][0:T, :], one_at["film_b"][:, 0:T], W["film_1"], stop=False)
            pe.wait_ge(S["cT_sb"], 1)
            pe.wait_ge(S["wcf_sb"], 1)
            one(B[1][0:T, :], cT[:, :], wcf[:, :], start=False).then_inc(S["film_ps"], 1)
            spectrum(11, 16)
            pe.wait_ge(S["ld_l"], 16)
            project_keys("film")
            keep_clock_up("film")
            pe.wait_ge(S["xm_ready"], 1)
            for c in range(2):
                last = one(B[2][0:FREQ, c * D:(c + 1) * D], W["dft_x"][:, c * FREQ:(c + 1) * FREQ], xm2[:, :])
            last.then_inc(S["xf_ps"], 1)
            project_keys("xf")
            keep_clock_up("xf")
            pe.wait_ge(S["prod_ready"], 1)
            yo = B[3][0:T, 0:D]
            one(yo, W["idft"][:, 0:T], pa[:, 0, :], stop=False)
            one(yo, W["idft"][:, T:2 * T], pb[:, 1, :], start=False, stop=False)
            one(yo, W["idft"][:, 2 * T:], pb[:, 0, :], start=False, stop=False)
            one(yo, W["idft"][:, 2 * T:], pa[:, 1, :], start=False).then_inc(S["y_ps"], 1)
            project_keys("y")
            keep_clock_up("y")
            pe.wait_ge(S["norm_ready"], 2)
            nc.tensor.transpose(B[2][:, 0:T], hn[:, :], idT).then_inc(S["tokT_ps"], 1)
            keep_clock_up("hT")
            pe.wait_ge(S["tokT_sb"], 2)
            for c in range(4):
                last = one(B[3][:, c * T:(c + 1) * T], W["w1"][:, c * P:(c + 1) * P], hT[:, :])
            last.then_inc(S["up0_ps"], 1)
            project_keys("up")
            keep_clock_up("up")
            one(B[2][0:T, 0:D], one_at["b2"][:, 0:T], W["b2"], stop=False)
            pe.wait_ge(S["gelu0_ready"], 1)
            for c in range(4):
                last = one(B[2][0:T, 0:D], hid0[:, c * T:(c + 1) * T], W["w2"][:, c * D:(c + 1) * D],
                           start=False, stop=(c == 3))
            last.then_inc(S["mlp0_ps"], 1)
            project_keys("mlp")
            keep_clock_up("mlp")
            pe.wait_ge(S["norm_ready"], 3)
            one(B[2][:, 0:2 * T], u1[:, :], W["eye_tri"]).then_inc(S["ut_ps"], 1)
            keep_clock_up("ut")
            pe.wait_ge(S["ut_sb"], 1)
            one(B[3][0:32, 0:T], W["gw1"], uT[:, 1:T + 1])
            one(B[3][0:32, T:2 * T], W["u_w"], uT[:, 1:T + 1]).then_inc(S["g1_ps"], 1)
            pe.wait_ge(S["ut_sb"], 2)
            one(B[0][0:32, 0:T], W["v_w"], cumT[:, :]).then_inc(S["g1_ps"], 1)
            keep_clock_up("g1")
            pe.wait_ge(S["g1_sb"], 1)
            one(B[1][0:32, 0:T], W["gw2"], g1[:, :]).then_inc(S["g2_ps"], 1)
            project_keys("gla")
            keep_clock_up("gla")
            pe.wait_ge(S["diag_ready"], 3)
            one(B[2][0:T, 0:D], one_at["out_b"][:, 0:T], W["out_b"], stop=False)
            for j in range(3):
                one(B[2][0:T, 0:D], uT[:, j:j + T], diag[:, j, :], start=False, stop=False)
            pe.wait_ge(S["glob_ready"], 1)
            one(B[2][0:T, 0:D], glob[:, :], W["out_w"], start=False).then_inc(S["blk1_ps"], 1)
            project_keys("moe")
            keep_clock_up("moe")
            pe.wait_ge(S["norm_ready"], 4)
            nc.tensor.transpose(B[3][:, 2 * D:2 * D + T], v[:, :], idT).then_inc(S["tokT_ps"], 1)
            keep_clock_up("vT")
            pe.wait_ge(S["tokT_sb"], 3)
            pe.wait_ge(S["ld_l"], 16)
            one(B[3][:, 0:8], vT[:, :, :].rearrange("p a t -> p (a t)"), W["rgT"], stop=False)
            one(B[3][:, 0:8], one_at["rb"][:, 0:P], W["rb"], start=False).then_inc(S["route_ps"], 1)
            pe.wait_ge(S["ld_w1"], 16)

            def moe_up(p):
                if p == 4:
                    pe.wait_ge(S["moe_raw"], 1)
                for e in range(2 if p < 4 else 1):
                    last = one(A[e * T:(e + 1) * T, p % 4, :], vT[:, 0, :], moe_w1[:, (2 * p + e) * BANK:(2 * p + e + 1) * BANK])
                last.then_inc(S["moe_up_ps"], 1)

            def moe_turn(p):
                pe.wait_ge(S["moe_raw"], p + 1)
                if p >= 2:
                    pe.wait_ge(S["moe_pre"], p - 1)
                m = P if p < 4 else T
                for c in range(4):
                    last = nc.tensor.transpose(B[p % 2][:, c * P:c * P + m], hraw[p % 2][0:m, c * P:(c + 1) * P],
                                               W["ident"][0:m, 0:m])
                last.then_inc(S["moe_hT_ps"], 1)

            def moe_down(p):
                pe.wait_ge(S["moe_gelu"], p + 1)
                if p >= 2:
                    pe.wait_ge(S["moe_acc"], p - 1)
                ne = 2 if p < 4 else 1
                y = [B[2 + p % 2][e * T:(e + 1) * T, 0:D] for e in range(2)]
                for e in range(ne):
                    one(y[e], one_at["moe_b2"][:, 0:T], W["moe_b2"][:, (2 * p + e) * D:(2 * p + e + 1) * D], stop=False)
                for c in range(4):
                    for e in range(ne):
                        last = one(y[e], hid[:, p * BANK + (c * ne + e) * T:p * BANK + (c * ne + e + 1) * T],
                                   moe_w2[:, (4 * (2 * p + e) + c) * D:(4 * (2 * p + e) + c + 1) * D], start=False, stop=(c == 3))
                last.then_inc(S["moe_y_ps"], 1)

            keep_clock_up("route")
            for b in range(*V_AT["route"]):
                project_values(b)
            pe.wait_ge(S["k_rest"], len(SB0))
            moe_up(0)
            moe_up(1)
            pe.wait_ge(S["route_pre"], 1)
            for p in range(5):
                moe_turn(p)
                if p == 0:
                    pe.wait_ge(S["v1_sb"], V_EARLY)
                if p + 2 < 5:
                    moe_up(p + 2)
                if p == 1:
                    pe.wait_ge(S["ld_w2"], 16)
                if p >= 1:
                    moe_down(p - 1)
            moe_down(4)
            pe.wait_ge(S["moe_acc"], 5)
            one(B[2][0:T, 0:D], W["sel_t"], acc[:, 1, :]).then_inc(S["x3_ps"], 1)

            for b in range(V_EARLY, V_GAP):
                project_values(b)
            keep_clock_up("n3", 3)
            pe.wait_ge(S["norm_ready"], 5)
            nc.tensor.transpose(B[3][:, 0:T], n3[:, :], idT).then_inc(S["tokT_ps"], 1)
            keep_clock_up("n3T", 3)
            pe.wait_ge(S["tokT_sb"], 4)
            one(B[3][:, T:2 * T], W["wq1"], n3T[:, :]).then_inc(S["q1_ps"], 1)
            keep_clock_up("q1", 3)
            pe.wait_ge(S["q1_bd"], 1)
            for i in range(2):
                one(A[0:KA, i, :], W["wkT1"], qbd[:, 8 * i:8 * i + 8, :].rearrange("p h t -> p (h t)")).then_inc(S["qq1_ps"], 1)
            for i in range(2):
                last = one(A[0:KS, 2 + i, :], W["rep_q"], qbd[:, 8 * i:8 * i + 8, :].rearrange("p h t -> p (h t)"))
            last.then_inc(S["qst_ps"], 1)
            pe.wait_ge(S["ctx_bf"], 4)
            pe.wait_ge(S["qq1_bf"], 1)

            def max_tile(n):
                i, (s, w) = n // len(SB0), SB0[n % len(SB0)]
                if n >= 2:
                    pe.wait_ge(S["max_used"], n - 1)
                one(B[2 + n % 2][:, 0:w], qq1b[:, i * P:(i + 1) * P], ctx_bf[:, s:s + w]).then_inc(S["max_ps"], 1)

            def fix_rows(j):
                pe.wait_ge(S["negm1"], j + 1)
                for i in range(2):
                    last = one(B[2][DC:KA, i * P:(i + 1) * P], nm[:, 2 * j + i, :], W["ident"])
                last.then_inc(S["fix_ps"], 1)

            NM = 2 * len(SB0)
            for n in range(NM):
                max_tile(n)
                if n % 2 == 1 and V_GAP + n // 2 < len(V_BANKS):
                    project_values(V_GAP + n // 2)
            fix_rows(0)
            pe.wait_ge(S["v1_sb"], len(V_BANKS))
            NG = len(GROUPS)

            def score_group(j, g):
                n = j * NG + g
                if n >= 2:
                    pe.wait_ge(S["p_ready"], n - 1)
                buf = A[:, 2 * (n % 2):2 * (n % 2) + 2, :].rearrange("p a b -> p (a b)")
                for i, c in enumerate(GROUPS[g]):
                    for m in (2 * j, 2 * j + 1):
                        last = one(buf[:, i * SQ * T + (m % 2) * P:i * SQ * T + (m % 2 + 1) * P],
                                   chunk_cols(kstack[m % 4], c), qst[:, m * P:(m + 1) * P])
                last.then_inc(S["s1_ps"], 1)

            def value_group(j, g):
                n = j * NG + g
                pe.wait_ge(S["p_ready"], n + 1)
                if g == 0 and j >= 1:
                    pe.wait_ge(S["acc_used"], 2 * j)
                for kind in range(2):
                    for i, c in enumerate(GROUPS[g]):
                        r = c % 4
                        lo, hi = ((0, 3 * T), (3 * T, SQ * T))[kind]
                        last = one(B[0][32 * r:32 * r + 32, lo:hi], v1_cols(c, VQ * j + 1 - kind, 32),
                                   probs[:, (n % RING) * 1024 + i * SQ * T + lo:(n % RING) * 1024 + i * SQ * T + hi],
                                   start=(c < 4 and kind == 0), stop=(c + 4 >= NC and kind == 1))
                last.then_inc(S["pv_done"], 1)

            def denominators(j):
                pe.wait_ge(S["acc_used"], 2 * (j + 1))
                one(B[1][:, 0:SQ * T], onec[:, 0:P], om[:, 1, :]).then_inc(S["zt_ps"], 1)

            for j in range(NQ):
                pe.wait_ge(S["qq_fixed"], j + 1)
                pe.wait_ge(stack_ld[j % 2], stack_count(j))
                for g in range(NG):
                    score_group(j, g)
                    if g >= 1:
                        value_group(j, g - 1)
                    if g == 2 and j >= 1:
                        denominators(j - 1)
                    if j + 1 < NQ:
                        for n in range(NM * (j + 1) + 2 * g, NM * (j + 1) + 2 * g + 2):
                            max_tile(n)
                value_group(j, NG - 1)
                if j + 1 < NQ:
                    fix_rows(j + 1)
            denominators(NQ - 1)
            one(B[3][0:T, 0:D], one_at["bo1"][:, 0:T], W["bo1"], stop=False)
            pe.wait_ge(S["o_ready"], NQ)
            for j in range(NQ):
                last = one(B[3][0:T, 0:D], o2[:, j, :], W["wo1"][:, j * D:(j + 1) * D], start=False, stop=(j == NQ - 1))
            last.then_inc(S["y1_ps"], 1)
            keep_clock_up("y1", 3)
            cz = W["causal"].unsqueeze(1).to_broadcast([T, 8, T])
            for i in range(2):
                one(A[0:T, i, :].rearrange("p (h k) -> p h k", k=T), idT, cz, stop=False)
            pe.wait_ge(S["norm_ready"], 6)
            nc.tensor.transpose(B[2][:, 0:T], n4[:, :], idT).then_inc(S["tokT_ps"], 1)
            keep_clock_up("n4T", 3)
            pe.wait_ge(S["tokT_sb"], 5)
            one(B[3][:, 0:T], W["wqT2"], n4T[:, 0, :])
            one(B[3][:, T:2 * T], W["wkT2"], n4T[:, 0, :]).then_inc(S["qk2_ps"], 1)
            one(B[0][:, 0:D], n4T[:, :, :].rearrange("p a t -> p (a t)"), W["wvT2"]).then_inc(S["v2_ps"], 1)
            keep_clock_up("v2", 3)
            pe.wait_ge(S["q2_sb"], 1)
            pe.wait_ge(S["k2_bd"], 1)
            for i in range(2):
                last = one(A[0:T, i, :], q2[:, :], kbd[:, 8 * i:8 * i + 8, :].rearrange("p h k -> p (h k)"), start=False)
            last.then_inc(S["s2_ps"], 1)
            keep_clock_up("s2", 3)
            pe.wait_ge(S["p2_ready"], 1)
            for p in range(8):
                last = nc.tensor.transpose(A[:, 2, p * T:(p + 1) * T],
                                           p2[:, 2 * p:2 * p + 2, :].rearrange("p h k -> p (h k)"), idT)
            last.then_inc(S["pT_ps"], 1)
            keep_clock_up("pT", 3)
            pe.wait_ge(S["pT_sb"], 1)
            pe.wait_ge(S["v2_bd"], 1)
            for p in range(8):
                last = one(B[1][0:T, 16 * p:16 * p + 16], pT[:, p, :], vbd[:, p, :, :].rearrange("p h c -> p (h c)"))
            last.then_inc(S["o2_ps"], 1)
            keep_clock_up("o2", 3)
            pe.wait_ge(S["o2_ready"], 1)
            nc.tensor.transpose(B[2][:, 0:T], oo[:, :], idT).then_inc(S["tokT_ps"], 1)
            keep_clock_up("o2T", 3)
            pe.wait_ge(S["tokT_sb"], 6)
            one(B[3][0:T, 0:D], ooT[:, :], W["woT2"]).then_inc(S["y2_ps"], 1)
            keep_clock_up("y2", 3)
            pe.wait_ge(S["norm_ready"], 7)
            nc.tensor.transpose(B[2][:, 0:T], u6[:, :], idT).then_inc(S["tokT_ps"], 1)
            keep_clock_up("u6T", 3)
            pe.wait_ge(S["tokT_sb"], 7)
            one(B[3][:, 0:8], u6T[:, :, :].rearrange("p a t -> p (a t)"), W["wr"]).then_inc(S["rt6_ps"], 1)
            keep_clock_up("rt6", 3)
            pe.wait_ge(S["r6_ready"], 1)
            nc.tensor.transpose(B[2][:, T:2 * T], h6[:, :], idT).then_inc(S["tokT_ps"], 1)
            keep_clock_up("h6T", 3)
            pe.wait_ge(S["h6_sb"], 1)
            pe.wait_ge(S["ld_gu"], 16)
            for p in range(4):
                for e in range(2):
                    last = one(A[e * T:(e + 1) * T, p, :], h6e[:, 2 * p + e, :], e_gu[:, (2 * p + e) * BANK:(2 * p + e + 1) * BANK])
                last.then_inc(S["e6_up_ps"], 1)
            for p in range(4):
                pe.wait_ge(S["e6_gu"], p + 1)
                if p >= 2:
                    pe.wait_ge(S["e6_guT_sb"], p - 1)
                for c in range(2):
                    last = nc.tensor.transpose(B[p % 2][:, c * P:(c + 1) * P],
                                               gu6[:, p, c * P:(c + 1) * P], W["ident"])
                last.then_inc(S["e6_guT_ps"], 1)
            pe.wait_ge(S["ld_down"], 16)
            for p in range(4):
                pe.wait_ge(S["e6_guT_sb"], p + 1)
                if p >= 2:
                    pe.wait_ge(S["moe_acc"], 5 + p - 1)
                for c in range(2):
                    for e in range(2):
                        last = one(B[2 + p % 2][e * T:(e + 1) * T, 0:D], guT[:, p, c, e * T:(e + 1) * T],
                                   e_dn[:, (2 * (2 * p + e) + c) * D:(2 * (2 * p + e) + c + 1) * D], start=(c == 0), stop=(c == 1))
                last.then_inc(S["e6_y_ps"], 1)
            pe.wait_ge(S["moe_acc"], 9)
            one(B[0][0:T, 0:D], W["sel_t"], acc[:, 1, :]).then_inc(S["out_ps"], 1)


def shape_constants():
    p = np.arange(P)
    t = np.arange(T)
    f = np.arange(FREQ)
    w = {}
    w["ident"] = np.eye(P)
    w["mask_h0"] = (p[:, None] // DH0 == np.arange(H0)) * float(DH0) ** -0.5
    w["mask_h1"] = p[:, None] // DH1 == np.arange(H1)
    w["turn0"] = np.where(p < 64, 0.25, 0.0)[:, None]
    w["sel_t"] = p[:, None] % T == t
    l = (p[:, None] % RA) * RB + np.arange(RB)[None, :]
    ang = 2 * np.pi * l[:, :, None] * f / (2 * T)
    w["dft_k"] = np.stack([np.cos(ang), -np.sin(ang)], 2).reshape(P, -1)
    ang = 2 * np.pi * t[:, None] * f / (2 * T)
    w["dft_x"] = np.stack([np.cos(ang), -np.sin(ang)], 1).reshape(T, -1)
    wt = np.where((f == 0) | (f == T), 1.0, 2.0)[:, None] / (2 * T)
    w["idft"] = np.concatenate([wt * np.cos(ang.T), -wt * np.cos(ang.T), -wt * np.sin(ang.T)], 1)
    w["eye_tri"] = np.concatenate([np.eye(T), t[:, None] <= t], 1)
    w["iota8"] = np.broadcast_to(np.arange(8), (P, 8))
    w["rep_q"] = np.zeros((P, KS))
    for row, _, _ in STACK:
        w["rep_q"][p, row + p % PAIR] = 1.0
    own = np.where(p[:, None] % 32 // DH1 == 0, SQ - 1, p[:, None] % 32 // DH1 - 1)
    w["mask_q"] = own == np.arange(SQ)
    w["mask_z"] = p[:, None] % 32 == np.array([DH1 - 1] * (SQ - 1) + [DH1])
    w["causal"] = np.where(t[:, None] >= t, 0.0, NEG)
    w["mask_p"] = p[:, None] // T == np.arange(2)
    w["e_mask"] = np.arange(KA) == DC
    w["film_1"] = (np.arange(4 * D) // D) % 2 == 0
    return {k: np.ascontiguousarray(a, dtype=np.float32) for k, a in w.items()}


def lay_out(i):
    dup = lambda a: np.concatenate([a, a], 0)
    over = lambda a, n: np.broadcast_to(np.reshape(a, (1, -1)), (n, np.size(a)))
    col = lambda a: np.reshape(a, (-1, 1))
    pad2 = lambda a: np.concatenate([a, np.zeros((a.shape[0], 2), a.dtype)], 1)
    w = shape_constants()
    x0, a0, m0, x1, a1, m1 = ({k[len(s):]: v for k, v in i.items() if k.startswith(s)} for s in
                              ("L0_xattn_", "L0_attn_", "L0_ffn_", "L1_xattn_", "L1_attn_", "L1_ffn_"))
    w["x"] = i["x"][0]
    w["wq0"], w["wkT0"] = x0["Wq"], pad2(x0["Wk"].T)
    for n, k in (("a_re", "A_re"), ("a_im", "A_im"), ("c_re", "C_re"), ("c_im", "C_im")):
        w[n] = dup(x0[k].T)
    w["log_dt"] = over(x0["log_dt"], P)
    w["film_w"] = np.concatenate([x0["W_film_in"], x0["W_film_out"]], 1)
    w["film_b"] = np.concatenate([x0["b_film_in"], x0["b_film_out"]])
    w["wvT0"] = x0["Wv"].T
    for n, k in (("g_in", "g_norm_in"), ("b_in", "b_norm_in"), ("g_out", "g_norm_out"), ("b_out", "b_norm_out")):
        w[n] = over(x0[k], T)
    w["gate"] = over(x0["mod_gate"], P).reshape(P, 1)
    w["g_ffn"], w["b_ffn"] = col(x0["g_ffn"]), col(x0["b_ffn"])
    w["w1"], w["b1T"] = x0["W1"], x0["b1"].reshape(4, P).T
    w["w2"] = x0["W2"].reshape(4, P, D).transpose(1, 0, 2).reshape(P, -1)
    w["b2"], w["d_skip"] = x0["b2"], x0["D_skip"]
    w["gw1"], w["gb1"], w["gw2"], w["gb2"] = a0["gate_w1"], col(a0["gate_b1"]), a0["gate_w2"], col(a0["gate_b2"])
    w["u_w"], w["v_w"], w["conv"], w["out_w"], w["out_b"] = a0["U_w"], a0["V_w"], a0["conv_w"], a0["out_w"], a0["out_b"]
    w["rgT"], w["rb"] = m0["gate_w"].T, m0["gate_b"]
    w["moe_b1T"] = np.concatenate([m0["b1"].reshape(32, P), m0["sb1"].reshape(4, P)], 0).T
    w["moe_b2"] = np.concatenate([m0["b2"].reshape(-1), m0["sb2"]])
    w["wq1"], w["bq1"] = x1["Wq"], col(x1["bq"])
    w["wkT1"] = np.concatenate([x1["Wk"].T, np.zeros((D, 1), np.float32), col(x1["bk"])], 1)
    w["wk1"] = np.concatenate([x1["Wk"], np.zeros((1, D), np.float32), x1["bk"][None]], 0)
    order = np.concatenate([[3], [0, 1, 2]])[:, None] * DH1 + np.arange(DH1)
    parts = []
    for j in range(NQ):
        feats = 4 * DH1 * j + order
        block = lambda f: np.concatenate([x1["Wv"][:, f], np.zeros((1, f.size), np.float32), x1["bv"][None, f]], 0)
        ones = (np.arange(KA) == KA - 1).astype(np.float32)[:, None]
        parts += [block(feats[0]), ones, block(feats[1:].reshape(-1))]
    w["wv1"] = np.concatenate(parts, 1)
    w["scale1"] = over(x1["scale"], P).reshape(P, 1)
    w["wo1"] = np.concatenate([np.tile(x1["Wo"][4 * DH1 * j + order.reshape(-1)], (4, 1)) for j in range(NQ)], 1)
    w["bo1"] = x1["bo"]
    for n, k in (("wqT2", "q"), ("wkT2", "k"), ("wvT2", "v"), ("woT2", "o")):
        w[n] = a1[f"{k}_proj_weight"].T
    w["wr"], w["norm_wT"] = m1["Wr"], m1["norm_w"].T
    out = {}
    for bn, table in BLOBS.items():
        a = np.zeros((P, width(table)), np.float32)
        for n, (r, at, c) in offsets(table).items():
            a[0:r, at:at + c] = w[n]
        out[bn] = a
    out["rows"] = np.zeros((3, ROWS_WIDTH), np.float32)
    for part, table in ROWS.items():
        at = 0
        for n, k in table.items():
            out["rows"][part // 32, at:at + k] = w[n]
            at += k
    out["dft_k"] = w["dft_k"]
    out["fill"] = np.concatenate([np.zeros((16, G // 2), np.uint32), np.full((1, G // 2), 0x3F803F80, np.uint32)], 0).view(np.float32)
    c = i["ctx_768"][0]
    out["ctxT"] = np.concatenate([c.T, np.zeros((1, G), np.float32), np.ones((1, G), np.float32)], 0)
    out["ctxn"] = c.reshape(NC, P, DC).transpose(1, 0, 2).reshape(P, -1)
    out["gmask"] = i["mask_BxS2_bf1"].view(np.uint8).reshape(1, G)
    out["tmask"] = dup(i["mask_BxS_bf1"].view(np.uint8).reshape(T, 1))
    out["moe_w1"] = np.concatenate([m0["w1"].transpose(1, 0, 2).reshape(D, -1), m0["sw1"]], 1)
    out["moe_w2"] = np.concatenate([m0["w2"].reshape(32, P, D), m0["sw2"].reshape(4, P, D)], 0).transpose(1, 0, 2).reshape(P, -1)
    out["e_gu"] = np.concatenate([m1["Wg"], m1["Wu"]], 2).transpose(1, 0, 2).reshape(D, -1)
    out["e_dn"] = m1["Wd"].reshape(16, P, D).transpose(1, 0, 2).reshape(P, -1)
    return {k: np.ascontiguousarray(a) for k, a in out.items()}


def kernel(**inputs):
    import concourse.bacc as _bacc
    from concourse.bass_utils import run_bass_kernel_spmd as _run

    nc = _bacc.Bacc("TRN2", target_bir_lowering=False, num_devices=1)
    arrays = lay_out({k: np.asarray(a) for k, a in inputs.items()})
    dram = {n: nc.dram_tensor(f"in_{n}", a.shape, mybir.dt.from_np(a.dtype), kind="ExternalInput").ap()
            for n, a in arrays.items()}
    out = nc.dram_tensor("out", (T, D), F32, kind="ExternalOutput").ap()
    perceiver_kernel(nc, dram, out)
    r = _run(nc, [{f"in_{n}": a for n, a in arrays.items()}], core_ids=[0])
    return r.results[0]["out"].reshape(1, T, D)
```
